# Optimizing a Trainium2 kernel written in Bass

```python
import numpy as np
import jax
import jax.numpy as jnp

def _softmax(x, axis=-1):
    return jax.nn.softmax(x, axis=axis)

def _gelu(x):
    return jax.nn.gelu(x, approximate=True)

def _silu(x):
    return jax.nn.silu(x)

def _sigmoid(x):
    return jax.nn.sigmoid(x)

def _layernorm(x, axis=-1, eps=1e-05):
    m = jnp.mean(x, axis=axis, keepdims=True)
    v = jnp.var(x, axis=axis, keepdims=True)
    return (x - m) / jnp.sqrt(v + eps)

def _scatter_add(tgt, idx, src, axis=0):
    return tgt.at[idx].add(src)

def _segment_sum(src, seg, n):
    return jax.ops.segment_sum(src, seg, n)
kernel_name = 'mk_seq_postln_d1_jaxref_r4_ffdbf2'

def setup_inputs(seed: int=0):
    np.random.seed(seed)
    _w = jnp.asarray

    def _L0_attn_setup():
        import jax, jax.numpy as jnp
        import numpy as np
        D_MODEL = 512
        EXPAND = 2
        D_STATE = 128
        D_CONV = 4
        HEADDIM = D_MODEL // 32
        D_INNER = EXPAND * D_MODEL
        NHEADS = D_INNER // HEADDIM
        CONV_DIM = D_INNER + 2 * D_STATE
        D_IN_PROJ = 2 * D_INNER + 2 * D_STATE + NHEADS
        CHUNK = 64
        BATCH, SEQLEN = (1, 1024)
        EPS = 1e-05

        def silu(x):
            return x * jax.nn.sigmoid(x)

        def _causal_decay(dA):
            cs = jnp.cumsum(dA, axis=-1)
            d = cs[..., :, None] - cs[..., None, :]
            c = dA.shape[-1]
            mask = jnp.tril(jnp.ones((c, c), bool))
            return jnp.where(mask, jnp.exp(jnp.where(mask, d, 0.0)), 0.0)

        def _chunked_scan(x, dt, A, B, C):
            b, l, h, p = x.shape
            n = B.shape[-1]
            nc = l // CHUNK
            xc = x.reshape(b, nc, CHUNK, h, p)
            dtc = dt.reshape(b, nc, CHUNK, h)
            Bc = B.reshape(b, nc, CHUNK, n)
            Cc = C.reshape(b, nc, CHUNK, n)
            dA = dtc * A
            dA_cum = jnp.cumsum(dA, axis=2)
            L = _causal_decay(jnp.moveaxis(dA, 2, 3))
            Xdt = xc * dtc[..., None]
            Y_diag = jnp.einsum('bzcn,bzsn,bzhcs,bzshp->bzchp', Cc, Bc, L, Xdt)
            decay_states = jnp.exp(dA_cum[:, :, -1:, :] - dA_cum)
            states = jnp.einsum('bzcn,bzch,bzchp->bzhpn', Bc, decay_states, Xdt)
            chunk_decay = jnp.exp(dA_cum[:, :, -1, :])

            def step(hprev, inp):
                st, dec = inp
                return (hprev * dec[:, :, None, None] + st, hprev)
            init = jnp.zeros((b, h, p, n), x.dtype)
            _, prev = jax.lax.scan(step, init, (jnp.moveaxis(states, 1, 0), jnp.moveaxis(chunk_decay, 1, 0)))
            prev = jnp.moveaxis(prev, 0, 1)
            Y_off = jnp.einsum('bzcn,bzhpn,bzch->bzchp', Cc, prev, jnp.exp(dA_cum))
            return (Y_diag + Y_off).reshape(b, l, h, p)
        key = jax.random.key(seed)
        ks = jax.random.split(key, 8)
        s = 0.02
        u = jax.random.normal(ks[0], (BATCH, SEQLEN, D_MODEL), jnp.float32)
        in_proj_w = jax.random.normal(ks[1], (D_IN_PROJ, D_MODEL), jnp.float32) * s
        conv_w = jax.random.normal(ks[2], (CONV_DIM, D_CONV), jnp.float32) * 0.2
        conv_b = jax.random.normal(ks[3], (CONV_DIM,), jnp.float32) * 0.02
        dt = jnp.exp(jax.random.uniform(ks[4], (NHEADS,)) * (np.log(0.1) - np.log(0.001)) + np.log(0.001))
        dt_bias = dt + jnp.log(-jnp.expm1(-dt))
        A_log = jnp.log(jax.random.uniform(ks[5], (NHEADS,), minval=1.0, maxval=16.0))
        D = jnp.ones((NHEADS,), jnp.float32)
        norm_weight = jnp.ones((D_INNER,), jnp.float32)
        out_proj_w = jax.random.normal(ks[6], (D_MODEL, D_INNER), jnp.float32) * s
        return dict(u=u, in_proj_w=in_proj_w, conv_w=conv_w, conv_b=conv_b, dt_bias=dt_bias, A_log=A_log, D=D, norm_weight=norm_weight, out_proj_w=out_proj_w)
    _L0_attn_in = _L0_attn_setup()

    def _L0_ffn_setup():
        import jax, jax.numpy as jnp
        import numpy as np
        _FP4_LUT = jnp.array([0.0, 0.5, 1.0, 1.5, 2.0, 3.0, 4.0, 6.0, -0.0, -0.5, -1.0, -1.5, -2.0, -3.0, -4.0, -6.0], dtype=jnp.float32)
        GROUP_SIZE = 128
        EPS = 1e-06

        def _dequant_fp4(packed_i32, scales_f16, group_size):
            out_f, in_p = packed_i32.shape
            w = packed_i32.astype(jnp.uint32)
            shifts = jnp.arange(8, dtype=jnp.uint32) * 4
            nib = w[:, :, None] >> shifts & jnp.uint32(15)
            vals = _FP4_LUT[nib.astype(jnp.int32)].reshape(out_f, in_p * 8)
            s = scales_f16.astype(jnp.float32).T
            s_full = jnp.repeat(s, group_size, axis=1)
            return vals * s_full
        key = jax.random.key(seed)
        k1, k2, k3, k4, k5 = jax.random.split(key, 5)
        B, S, H, I = (4, 512, 512, 1408)
        x = jax.random.normal(k1, (B, S, H), dtype=jnp.float32)
        gate_up_packed = jax.random.randint(k2, (2 * I, H // 8), 0, 2147483647, dtype=jnp.int32)
        gate_up_scales = jax.random.uniform(k3, (H // GROUP_SIZE, 2 * I), dtype=jnp.float32).astype(jnp.float16)
        down_packed = jax.random.randint(k4, (H, I // 8), 0, 2147483647, dtype=jnp.int32)
        down_scales = jax.random.uniform(k5, (I // GROUP_SIZE, H), dtype=jnp.float32).astype(jnp.float16)
        return {'x': x, 'gate_up_packed': gate_up_packed, 'gate_up_scales': gate_up_scales, 'down_packed': down_packed, 'down_scales': down_scales}
    _L0_ffn_in = _L0_ffn_setup()
    _d = {'L0_attn_u': _L0_attn_in['u'], 'L0_attn_in_proj_w': _L0_attn_in['in_proj_w'], 'L0_attn_conv_w': _L0_attn_in['conv_w'], 'L0_attn_conv_b': _L0_attn_in['conv_b'], 'L0_attn_dt_bias': _L0_attn_in['dt_bias'], 'L0_attn_A_log': _L0_attn_in['A_log'], 'L0_attn_D': _L0_attn_in['D'], 'L0_attn_norm_weight': _L0_attn_in['norm_weight'], 'L0_attn_out_proj_w': _L0_attn_in['out_proj_w'], 'L0_ffn_gate_up_packed': _L0_ffn_in['gate_up_packed'], 'L0_ffn_gate_up_scales': _L0_ffn_in['gate_up_scales'], 'L0_ffn_down_packed': _L0_ffn_in['down_packed'], 'L0_ffn_down_scales': _L0_ffn_in['down_scales']}
    _x0 = _d['L0_attn_u']
    _d['L0_attn_u'] = jax.random.normal(jax.random.fold_in(jax.random.key(seed), 1), (8, 512, 512), dtype=_x0.dtype)
    del _x0
    return _d

def reference(L0_attn_u, L0_attn_in_proj_w, L0_attn_conv_w, L0_attn_conv_b, L0_attn_dt_bias, L0_attn_A_log, L0_attn_D, L0_attn_norm_weight, L0_attn_out_proj_w, L0_ffn_gate_up_packed, L0_ffn_gate_up_scales, L0_ffn_down_packed, L0_ffn_down_scales):

    def _L0_attn_ref(u, in_proj_w, conv_w, conv_b, dt_bias, A_log, D, norm_weight, out_proj_w):
        import jax, jax.numpy as jnp
        import numpy as np
        D_MODEL = 512
        EXPAND = 2
        D_STATE = 128
        D_CONV = 4
        HEADDIM = D_MODEL // 32
        D_INNER = EXPAND * D_MODEL
        NHEADS = D_INNER // HEADDIM
        CONV_DIM = D_INNER + 2 * D_STATE
        D_IN_PROJ = 2 * D_INNER + 2 * D_STATE + NHEADS
        CHUNK = 64
        BATCH, SEQLEN = (1, 1024)
        EPS = 1e-05

        def silu(x):
            return x * jax.nn.sigmoid(x)

        def _causal_decay(dA):
            cs = jnp.cumsum(dA, axis=-1)
            d = cs[..., :, None] - cs[..., None, :]
            c = dA.shape[-1]
            mask = jnp.tril(jnp.ones((c, c), bool))
            return jnp.where(mask, jnp.exp(jnp.where(mask, d, 0.0)), 0.0)

        def _chunked_scan(x, dt, A, B, C):
            b, l, h, p = x.shape
            n = B.shape[-1]
            nc = l // CHUNK
            xc = x.reshape(b, nc, CHUNK, h, p)
            dtc = dt.reshape(b, nc, CHUNK, h)
            Bc = B.reshape(b, nc, CHUNK, n)
            Cc = C.reshape(b, nc, CHUNK, n)
            dA = dtc * A
            dA_cum = jnp.cumsum(dA, axis=2)
            L = _causal_decay(jnp.moveaxis(dA, 2, 3))
            Xdt = xc * dtc[..., None]
            Y_diag = jnp.einsum('bzcn,bzsn,bzhcs,bzshp->bzchp', Cc, Bc, L, Xdt)
            decay_states = jnp.exp(dA_cum[:, :, -1:, :] - dA_cum)
            states = jnp.einsum('bzcn,bzch,bzchp->bzhpn', Bc, decay_states, Xdt)
            chunk_decay = jnp.exp(dA_cum[:, :, -1, :])

            def step(hprev, inp):
                st, dec = inp
                return (hprev * dec[:, :, None, None] + st, hprev)
            init = jnp.zeros((b, h, p, n), x.dtype)
            _, prev = jax.lax.scan(step, init, (jnp.moveaxis(states, 1, 0), jnp.moveaxis(chunk_decay, 1, 0)))
            prev = jnp.moveaxis(prev, 0, 1)
            Y_off = jnp.einsum('bzcn,bzhpn,bzch->bzchp', Cc, prev, jnp.exp(dA_cum))
            return (Y_diag + Y_off).reshape(b, l, h, p)
        b, l, _ = u.shape
        zxbcdt = u @ in_proj_w.T
        z, xBC, dt_raw = jnp.split(zxbcdt, [D_INNER, D_INNER + CONV_DIM], axis=-1)
        xt = jnp.transpose(xBC, (0, 2, 1))
        conv = jax.lax.conv_general_dilated(xt, conv_w[:, None, :], (1,), [(D_CONV - 1, 0)], dimension_numbers=('NCH', 'OIH', 'NCH'), feature_group_count=CONV_DIM)
        xBC = silu(jnp.transpose(conv + conv_b[None, :, None], (0, 2, 1)))
        x, B, C = jnp.split(xBC, [D_INNER, D_INNER + D_STATE], axis=-1)
        dt = jax.nn.softplus(dt_raw + dt_bias)
        A = -jnp.exp(A_log)
        xh = x.reshape(b, l, NHEADS, HEADDIM)
        y = _chunked_scan(xh, dt, A, B, C)
        y = y + xh * D[:, None]
        y = y.reshape(b, l, D_INNER)
        yg = y * silu(z)
        yn = yg * jax.lax.rsqrt(jnp.mean(yg * yg, axis=-1, keepdims=True) + EPS) * norm_weight
        return yn @ out_proj_w.T

    def _L0_ffn_ref(x, gate_up_packed, gate_up_scales, down_packed, down_scales):
        import jax, jax.numpy as jnp
        import numpy as np
        _FP4_LUT = jnp.array([0.0, 0.5, 1.0, 1.5, 2.0, 3.0, 4.0, 6.0, -0.0, -0.5, -1.0, -1.5, -2.0, -3.0, -4.0, -6.0], dtype=jnp.float32)
        GROUP_SIZE = 128
        EPS = 1e-06

        def _dequant_fp4(packed_i32, scales_f16, group_size):
            out_f, in_p = packed_i32.shape
            w = packed_i32.astype(jnp.uint32)
            shifts = jnp.arange(8, dtype=jnp.uint32) * 4
            nib = w[:, :, None] >> shifts & jnp.uint32(15)
            vals = _FP4_LUT[nib.astype(jnp.int32)].reshape(out_f, in_p * 8)
            s = scales_f16.astype(jnp.float32).T
            s_full = jnp.repeat(s, group_size, axis=1)
            return vals * s_full
        I = gate_up_packed.shape[0] // 2
        w_gu = _dequant_fp4(gate_up_packed, gate_up_scales, GROUP_SIZE)
        w_down = _dequant_fp4(down_packed, down_scales, GROUP_SIZE)
        gate_up = jnp.einsum('bsh,oh->bso', x, w_gu)
        gate, up = (gate_up[..., :I], gate_up[..., I:])
        h = jax.nn.silu(gate) * up
        y = jnp.einsum('bsi,hi->bsh', h, w_down)
        rms = jnp.sqrt(jnp.mean(y * y, axis=-1, keepdims=True) + EPS)
        return y / rms
    x = L0_attn_u
    x = _layernorm(x + _L0_attn_ref(x, L0_attn_in_proj_w, L0_attn_conv_w, L0_attn_conv_b, L0_attn_dt_bias, L0_attn_A_log, L0_attn_D, L0_attn_norm_weight, L0_attn_out_proj_w), axis=-1)
    x = _layernorm(x + _L0_ffn_ref(x, L0_ffn_gate_up_packed, L0_ffn_gate_up_scales, L0_ffn_down_packed, L0_ffn_down_scales), axis=-1)
    return x

_drawn_inputs = setup_inputs


def setup_inputs(seed=0):
    import zlib

    import numpy as np

    out = dict(_drawn_inputs(seed))
    spreads = {'L0_attn_D': (1.0, 0.2), 'L0_attn_norm_weight': (1.0, 0.2)}
    factors = {}
    for name, (base, spread) in spreads.items():
        noise = np.random.default_rng([zlib.crc32(name.encode()), seed]).standard_normal(out[name].shape)
        drawn = base * np.exp(spread * noise) if base else spread * noise
        out[name] = jnp.asarray(drawn.astype(out[name].dtype))
    for name, factor in factors.items():
        out[name] = (out[name] * factor).astype(out[name].dtype)
    return out
```

```python
from contextlib import ExitStack

import numpy as np

import concourse.bass as bass
from concourse import mybir

ALU = mybir.AluOpType
ACT = mybir.ActivationFunctionType
AX = mybir.AxisListType
F32 = mybir.dt.float32
F16 = mybir.dt.float16
BF16 = mybir.dt.bfloat16
I32 = mybir.dt.int32
U16 = mybir.dt.uint16
RMAX = bass.bass_isa.ReduceOp.max

P = 128
NB = 8
L = 512
DM = 512
KT = DM // P
DI = 1024
CT = DI // P
NH = 64
HD = DI // NH
NS = 128
NP = NH // 2
CH = 64
NC = L // CH
NG = 4
SLOTS = NC * NG
TT = L // P
TAPS = 4
IN_COLS = NH + 2 * NS + 2 * DI
FI = 1408
FT = FI // P
GU_SCALES = KT * 2 * FI // P
ALL_SCALES = GU_SCALES + FT * DM // P
MAXES_READY, W_SCALED, PRO_DVE, PRO_ACT = 2, 6, 7, 1 + KT
DT_STEPS = 25
DEC = 352
NEG = -1.0e30
LOG1P = [2.0 / (2 * k + 1) for k in range(8)]

PRO_USES = [(0, "dt"), (0, "B"), (0, "C")] + [(0, f"x{i}") for i in range(CT)] + [(0, f"z{i}") for i in range(CT)]
BODY_USES = [(5, "dt"), (7, "B"), (9, "C"), (11, "x0"), (12, "q0"), (13, "o0"), (15, "x1"), (17, "x2"),
             (19, "x3"), (20, "q1"), (21, "o1"), (23, "x4"), (25, "x5"), (27, "x6"), (28, "q2"), (29, "o2"),
             (31, "x7"), (32, "z0"), (32, "q3"), (32, "o3")] + [(32, f"z{i}") for i in range(1, CT)]
LAST_USES = [(12, "q0"), (13, "o0"), (20, "q1"), (21, "o1"), (28, "q2"), (29, "o2"), (32, "q3"), (32, "o3")]
CONV_TILES = ["B", "C"] + [f"x{i}" for i in range(CT)]
IN_COL = {"dt": 0, "B": NH, "C": NH + NS}
IN_COL |= {f"x{i}": NH + 2 * NS + i * P for i in range(CT)}
IN_COL |= {f"z{i}": NH + 2 * NS + DI + i * P for i in range(CT)}


def need(eng, sem, value):
    if isinstance(value, int) and value <= 0:
        return
    eng.wait_ge(sem, value)


def banks_of(uses):
    banks = [i % 2 for i in range(len(uses))]
    names = [u for _, u in uses]
    if "z0" in names and "o3" in names:
        at = names.index("o3")
        banks[at] = banks[at - 1]
        banks[at + 1:] = [(i + 1) % 2 for i in range(len(uses) - at - 1)]
    return banks


class Stage:

    def __init__(self, kind, b):
        self.kind = kind
        self.scan = b if kind != "pro" else None
        self.proj = {"pro": 0, "body": b + 1, "last": None}[kind]
        self.uses = {"pro": PRO_USES, "body": BODY_USES, "last": LAST_USES}[kind]
        pro = [banks_of(PRO_USES).count(i) for i in range(2)]
        body = [banks_of(BODY_USES).count(i) for i in range(2)]
        self.base = [0, 0] if kind == "pro" else [b * body[i] + pro[i] for i in range(2)]

    def bank(self, name):
        at = [u for _, u in self.uses].index(name)
        banks = banks_of(self.uses)
        count = self.base[banks[at]] + banks[:at].count(banks[at])
        return banks[at], count, count + 1

    def at(self, slot):
        return [u for s, u in self.uses if s == slot]

    def before(self):
        return Stage("pro", 0) if isinstance(self.scan, int) and self.scan == 0 else Stage("body", self.scan - 1)

    def last_z(self):
        found = [self.bank(f"z{i}") for i in (CT - 2, CT - 1)]
        assert found[0][0] != found[1][0]
        return [(bk, full) for bk, _, full in found]


class Chain:

    def __init__(self, eng, sem, per, b):
        self.eng, self.sem, self.per, self.base, self.k = eng, sem, per, b * per, 0

    def step(self, ins, then=None):
        self.k += 1
        ins.then_inc(self.sem, 1)
        self.eng.wait_ge(self.sem, self.base + self.k)
        if then:
            then(self.eng)

    def end(self):
        assert self.k == self.per, (self.k, self.per)


def build(nc, u_t, u_tok, w_in_t, conv_w, conv_b, dt_bias, a_log, d_skip, norm_w, w_out_t,
          gu_words, gu_scales, dn_words, dn_scales, all_scales, c_sel, c_rhs, c_lhs, c_dec, c_ident, c_mask,
          c_shift, out, nb=NB):
    ctx = ExitStack()
    with ctx:
        def sem(name):
            return ctx.enter_context(nc.semaphore(name))

        cs_dram = nc.dram_tensor("cs_dram", [nb, 3 * NH, L], BF16, kind="Internal")
        ld_dram = nc.dram_tensor("ld_dram", [nb, 3, NP, 2, L], BF16, kind="Internal")
        x1_dram = nc.dram_tensor("x1_dram", [nb * L, DM], F32, kind="Internal")
        gu_dram = nc.dram_tensor("gu_dram", [2, KT, P, 2 * FI], F16, kind="Internal")
        dn_dram = nc.dram_tensor("dn_dram", [2, P, FT, DM], F16, kind="Internal")

        def keep(name, shape, dt=F32):
            return ctx.enter_context(nc.sbuf_tensor(name, shape, dt))

        maxes = keep("maxes", [P, 3])
        maxes_all = keep("maxes_all", [P, 3])
        pow2 = keep("pow2", [P, 3])
        inv2 = keep("inv2", [P, 3])
        scal = keep("scal", [P, 8])
        ident = keep("ident", [P, P])
        half = keep("half", [P, 1])
        w_in_scale, w_in_undo = scal[:, 0:1], scal[:, 1:2]
        gu_in_scale, dn_in_scale = scal[:, 2:3], scal[:, 3:4]
        gate_undo, up_undo, down_undo = scal[:, 4:5], scal[:, 5:6], scal[:, 6:7]
        scratch1 = scal[:, 7:8]

        p1 = ExitStack()

        def sb(name, shape, dt=F32):
            return p1.enter_context(nc.sbuf_tensor(name, shape, dt))

        w_hi = sb("w_hi", [P, KT, IN_COLS], F16)
        w_lo = sb("w_lo", [P, KT, IN_COLS], F16)
        w_out = sb("w_out", [P, CT, DM])
        pre = sb("pre", [P, 2 + CT, L])
        bc = sb("bc", [P, 2, L])
        xs = sb("xs", [P, CT, L])
        zg = sb("zg", [P, CT, L])
        u32 = sb("u32", [P, KT, L])
        u_hi = sb("u_hi", [P, KT, L], F16)
        u_lo = sb("u_lo", [P, KT, L], F16)
        res = sb("res", [P, 2, DM])
        rhs_d = sb("rhs_d", [P, 2, NP, CH], BF16)
        lhs_d = sb("lhs_d", [P, 2, NG, 2 * CH], BF16)
        decay = sb("decay", [P, NG, CT, CH])
        mix = sb("mix", [P, 2, CT, CH])
        xpad = sb("xpad", [P, 2, NP, 2 * HD])
        xend = sb("xend", [P, NP, 2 * HD])
        state = sb("state", [P, DI])
        state_d = sb("state_d", [P, DI])
        gb = sb("gb", [P, 2, CH + NS])
        dec = sb("dec", [P, 2, NP, 2])
        ebc = sb("ebc", [P, 2, CT, CH])
        yoff = sb("yoff", [P, CT, CH])
        y = sb("y", [P, 2, CT, CH])
        sq = sb("sq", [P, CT, CH])
        ssum = sb("ssum", [P, L])
        cs12 = sb("cs12", [P, L], BF16)
        cs3 = sb("cs3", [NH, L], BF16)
        cs_parts = sb("cs_parts", [NH, 3, L], BF16)
        ld_parts = sb("ld_parts", [NH, 3, L], BF16)
        dta = sb("dta", [NH, L])
        dtb = sb("dtb", [NH, L])
        dtc = sb("dtc", [NH, L])
        dtd = sb("dtd", [NH, L])
        dte = sb("dte", [NH, L])
        dtf = sb("dtf", [NH, L])
        sel = sb("sel", [P, CT, P], BF16)
        sel_dec = sb("sel_dec", [6, 2, P], BF16)
        mask = sb("mask", [NH, L], BF16)
        cw = sb("cw", [P, 2 + CT, TAPS])
        cws = sb("cws", [P, 2 + CT, TAPS])
        cb = sb("cb", [P, 2 + CT])
        dskip = sb("dskip", [P, CT])
        normw = sb("normw", [P, CT])
        dtbias = sb("dtbias", [NH, 1])
        aneg = sb("aneg", [NH, 1])
        ones = sb("ones", [P, 1])
        umax = sb("umax", [P, 1])
        umax_all = sb("umax_all", [P, 1])
        uscale = sb("uscale", [P, 1])
        uundo = sb("uundo", [P, 1])
        utmp = sb("utmp", [P, 2])
        msv = sb("msv", [P, TT])
        rinv = sb("rinv", [P, TT])
        bn = sb("bn", [P, 2, 6])
        mv = sb("mv", [P, 2, 2])
        rstd = sb("rstd", [P, 2])
        wmax = sb("wmax", [P, KT])
        scales_once = sb("scales_once", [P, ALL_SCALES], F16)
        shift = sb("shift", [P, 2], I32)
        fw_words = sb("fw_words", [P, DEC], I32)
        fw_scale = sb("fw_scale", [P, DEC], F16)
        fw_mag = sb("fw_mag", [P, DEC], I32)
        fw_sign = sb("fw_sign", [P, DEC], I32)
        fw_w = sb("fw_w", [P, DEC])
        fw_hi = sb("fw_hi", [P, DEC], F16)
        fw_lo = sb("fw_lo", [P, DEC], F16)
        p1.close()
        rooms = [(pre, 0), (pre, IN_COLS), (zg, 0), (xs, 0)]
        w_src = [t[:, :, :].rearrange("p a b -> p (a b)")[:, at:at + IN_COLS] for t, at in rooms]

        p2 = ExitStack()

        def sb2(name, shape, dt=F32):
            return p2.enter_context(nc.sbuf_tensor(name, shape, dt))

        gu_hi = sb2("gu_hi", [P, KT, 2 * FI], F16)
        gu_lo = sb2("gu_lo", [P, KT, 2 * FI], F16)
        dn_hi = sb2("dn_hi", [P, FT, DM], F16)
        dn_lo = sb2("dn_lo", [P, FT, DM], F16)
        xa = sb2("xa", [P, TT, DM])
        xt_hi = sb2("xt_hi", [P, KT, L], F16)
        xt_lo = sb2("xt_lo", [P, KT, L], F16)
        h_hi = sb2("h_hi", [P, FT, L], F16)
        h_lo = sb2("h_lo", [P, FT, L], F16)
        sg = sb2("sg", [P, 2, L])
        hf = sb2("hf", [P, 2, L])
        xr = sb2("xr", [P, 2, DM])
        junk = sb2("junk", [P, DM])
        ss2 = sb2("ss2", [P, 2])
        ms2 = sb2("ms2", [P, 2])
        ri2 = sb2("ri2", [P, 2])
        rk2 = sb2("rk2", [P, 2])
        bn2 = sb2("bn2", [P, 2, 6])
        mv2 = sb2("mv2", [P, 2, 2])
        rs2 = sb2("rs2", [P, 2])
        p2.close()

        def bank(name):
            return ctx.enter_context(nc.psum_tensor(name, [P, 512], F32))

        ps_in = [bank("ps_in0"), bank("ps_in1")]
        ps_d = [bank("ps_d0"), bank("ps_d1")]
        ps_t, ps_s, ps_yd, ps_yo = bank("ps_t"), bank("ps_s"), bank("ps_yd"), bank("ps_yo")

        const_in = sem("const_in")
        passed = sem("passed")
        w_in_in = sem("w_in_in")
        u_in = sem("u_in")
        res_in = [sem("res_in0"), sem("res_in1")]
        rq_in = [sem("rq_in0"), sem("rq_in1")]
        csp_in = sem("csp_in")
        parts_out = sem("parts_out")
        x1_out = [sem("x1_out0"), sem("x1_out1")]
        fw_in = sem("fw_in")
        fw_out = sem("fw_out")
        fw_chain = sem("fw_chain")
        fw_done = sem("fw_done")
        pro_dve = sem("pro_dve")
        pro_act = sem("pro_act")
        pro_pool = sem("pro_pool")
        u_max = sem("u_max")
        u_all = sem("u_all")
        u_scale = sem("u_scale")
        u_hi_done = sem("u_hi_done")
        u_lo_done = sem("u_lo_done")
        in_full = [sem("in_full0"), sem("in_full1")]
        in_free = [sem("in_free0"), sem("in_free1")]
        tap3 = sem("tap3")
        conv_chain = sem("conv_chain")
        silu_done = sem("silu_done")
        dt_act = sem("dt_act")
        dt_dve = sem("dt_dve")
        t_full = sem("t_full")
        t_free = sem("t_free")
        d_full = sem("d_full")
        e_done = sem("e_done")
        m_done = sem("m_done")
        xe_done = sem("xe_done")
        yd_done = sem("yd_done")
        yo_full = sem("yo_full")
        s_full = sem("s_full")
        s_add = sem("s_add")
        sd_done = sem("sd_done")
        xd_done = sem("xd_done")
        y1_done = sem("y1_done")
        y2_done = sem("y2_done")
        y_done = sem("y_done")
        gate_done = sem("gate_done")
        sum_chain = sem("sum_chain")
        rinv_done = sem("rinv_done")
        ln_chain = sem("ln_chain")
        rstd_done = sem("rstd_done")
        x1_done = sem("x1_done")

        gw_in = sem("gw_in")
        xa_in = sem("xa_in")
        xr_in = [sem("xr_in0"), sem("xr_in1")]
        tr_full = sem("tr_full")
        xh_done = sem("xh_done")
        xl_done = sem("xl_done")
        g_full = sem("g_full")
        up_full = sem("up_full")
        sg_done = sem("sg_done")
        hf_done = sem("hf_done")
        hh_done = sem("hh_done")
        hl_done = sem("hl_done")
        dn_full = sem("dn_full")
        ss_done = sem("ss_done")
        ms_done = sem("ms_done")
        ri_done = sem("ri_done")
        o_chain = sem("o_chain")
        rs_done = sem("rs_done")
        o_done = sem("o_done")
        out_out = [sem("out_out0"), sem("out_out1")]

        N_CONST = 16 * 17
        SLICE_G, SLICE_D = 2 * FI // NB, DM // NB
        assert SLICE_G == DEC and FT * SLICE_D == 2 * DEC
        fw_units = [("g", i) for i in range(KT)] + [("d", i) for i in range(2)]
        FW_SLOT = {14: 0, 16: 1, 18: 2, 22: 3, 24: 4, 26: 5}

        ps_g, ps_u, ps_t2, ps_n = ps_in, ps_d, [ps_t, ps_s], [ps_yd, ps_yo]

        block = ctx.enter_context(nc.Block())

        def settled(eng):
            eng.sem_inc(passed, 1)

        @block.sync
        def _(sp):
            def load_u(b, wait):
                if wait:
                    need(sp, u_hi_done, b * KT)
                    settled(sp)
                    need(sp, u_lo_done, b * KT)
                    settled(sp)
                    need(sp, u_max, b)
                    settled(sp)
                sp.dma_start(u32[:, :, :], u_t.rearrange("(k p) t -> p k t", p=P)[:, :, bass.ds(b * L, L)])\
                  .then_inc(u_in, 16)

            def store_parts(b):
                sp.wait_ge(dt_dve, (b + 1) * DT_STEPS)
                settled(sp)
                sp.dma_start(cs_dram[b].rearrange("(r q) t -> q r t", r=3), cs_parts[:, :, :]).then_inc(parts_out, 16)
                for h2 in range(2):
                    sp.dma_start(ld_dram[b, :, :, h2, :].rearrange("r q t -> q r t"),
                                 ld_parts[h2 * NP:(h2 + 1) * NP, :, :]).then_inc(parts_out, 16)

            def load_cs(b):
                sp.wait_ge(parts_out, (b + 1) * 48)
                settled(sp)
                need(sp, t_full, b * 32)
                settled(sp)
                sp.dma_start(cs12[:, :], cs_dram[b, 0:2 * NH, :]).then_inc(csp_in, 16)
                sp.dma_start(cs3[:, :], cs_dram[b, 2 * NH:3 * NH, :]).then_inc(csp_in, 16)

            def load_rows(b, c):
                need(sp, d_full, b * SLOTS + NG * (c - 1))
                settled(sp)
                t = slice(c * CH, (c + 1) * CH)
                sp.dma_start(rhs_d[0:6, c % 2, :, :], cs_dram[b].rearrange("(r q) t -> r q t", q=NP)[:, :, t])\
                  .then_inc(rq_in[c % 2], 16)
                sp.dma_start(lhs_d[6:30, c % 2, :, :].rearrange("r g (h s) -> r (g h) s", h=2),
                             ld_dram[b].rearrange("r (q g) h t -> (r q) (g h) t", g=NG)[:, :, t])\
                  .then_inc(rq_in[c % 2], 16)

            def load_res(b, tt):
                need(sp, x1_out[tt % 2], b * 32 + 16 * (tt // 2))
                settled(sp)
                sp.dma_start(res[:, tt % 2, :], u_tok[bass.ds(b * L + tt * P, P), :]).then_inc(res_in[tt % 2], 16)

            def store_x1(b, tt):
                sp.wait_ge(x1_done, b * TT + tt + 1)
                settled(sp)
                sp.dma_start(x1_dram[bass.ds(b * L + tt * P, P), :], res[:, tt % 2, :]).then_inc(x1_out[tt % 2], 16)

            def load_fw(b, k):
                kind, i = fw_units[k]
                need(sp, fw_done, b * 6 + k)
                settled(sp)
                if kind == "g":
                    sp.dma_start(fw_words[:, :], gu_words[:, bass.ds(b * SLICE_G, DEC)]).then_inc(fw_in, 16)
                    sp.dma_start(fw_scale[:, :], gu_scales[:, bass.ds(b * SLICE_G, DEC)]).then_inc(fw_in, 16)
                else:
                    cols = bass.ds(b * SLICE_D + i * (SLICE_D // 2), SLICE_D // 2)
                    sp.dma_start(fw_words[:, :].rearrange("p (g n) -> p g n", g=FT), dn_words[:, :, cols]).then_inc(fw_in, 16)
                    sp.dma_start(fw_scale[:, :].rearrange("p (g n) -> p g n", g=FT), dn_scales[:, :, cols]).then_inc(fw_in, 16)

            def store_fw(b, k):
                kind, i = fw_units[k]
                sp.wait_ge(fw_done, b * 6 + k + 1)
                settled(sp)
                for part, w in enumerate((fw_hi, fw_lo)):
                    if kind == "g":
                        sp.dma_start(gu_dram[part, i][:, bass.ds(b * SLICE_G, DEC)], w[:, :]).then_inc(fw_out, 16)
                    else:
                        cols = bass.ds(b * SLICE_D + i * (SLICE_D // 2), SLICE_D // 2)
                        sp.dma_start(dn_dram[part][:, :, cols], w[:, :].rearrange("p (g n) -> p g n", g=FT)).then_inc(fw_out, 16)

            def body(st):
                b = st.scan
                load_cs(b)
                load_rows(b, 0)
                load_rows(b, 1)
                if st.proj is not None:
                    load_u(b + 2, True)
                load_res(b, 0)
                load_res(b, 1)
                load_fw(b, 0)
                for n in range(SLOTS):
                    c = n // NG + 2
                    if n % NG == 1 and c < NC:
                        load_rows(b, c)
                    if n == 15 and st.proj is not None:
                        store_parts(b + 1)
                    if n in FW_SLOT:
                        store_fw(b, FW_SLOT[n])
                        if FW_SLOT[n] + 1 < 6:
                            load_fw(b, FW_SLOT[n] + 1)
                    for tt in range(2):
                        if f"o{tt}" in st.at(n):
                            store_x1(b, tt)
                            load_res(b, tt + 2)
                    if "o2" in st.at(n):
                        store_x1(b, 2)
                store_x1(b, 3)

            load_u(0, False)
            for k in range(KT):
                sp.dma_start(w_src[k], w_in_t[k * P:(k + 1) * P, :]).then_inc(w_in_in, 16)
            consts = [(cw[:, :, :], conv_w), (cb[:, :], conv_b), (dtbias[:, :], dt_bias), (aneg[:, :], a_log),
                      (dskip[:, :], d_skip), (normw[:, :], norm_w), (sel[:, :, :], c_sel),
                      (sel_dec[:, :, :], c_dec), (ident[:, :], c_ident), (mask[:, :], c_mask), (shift[:, :], c_shift),
                      (w_out[:, :, :], w_out_t.rearrange("(k p) n -> p k n", p=P))]
            consts += [(rhs_d[6:94, i, :, :], c_rhs) for i in range(2)]
            consts += [(lhs_d[:94, i, :, :], c_lhs) for i in range(2)]
            for dst, src in consts:
                if src.dtype == U16:
                    src = src.bitcast(BF16)
                sp.dma_start(dst, src).then_inc(const_in, 16)
            sp.dma_start(scales_once[:, :], all_scales).then_inc(const_in, 16)
            load_u(1, True)
            sp.wait_ge(const_in, N_CONST)
            store_parts(0)
            body(Stage("body", 0))
            with sp.Fori(1, nb - 1) as i:
                body(Stage("body", i))
            body(Stage("last", nb - 1))

            sp.wait_ge(fw_out, nb * 6 * 32)
            for k in range(2):
                sp.wait_ge(x1_out[k], nb * 32)
            for part, w in enumerate((gu_hi, gu_lo)):
                sp.dma_start(w[:, :, :], gu_dram[part].rearrange("k p n -> p k n")).then_inc(gw_in, 16)

            def load_xa(f):
                need(sp, tr_full, f * KT)
                settled(sp)
                sp.dma_start(xa[:, :, :], x1_dram[bass.ds(f * L, L), :].rearrange("(t p) n -> p t n", p=P)).then_inc(xa_in, 16)

            load_xa(0)
            for part, w in enumerate((dn_hi, dn_lo)):
                sp.dma_start(w[:, :, :], dn_dram[part]).then_inc(gw_in, 16)

            def load_xr(f, tt):
                need(sp, out_out[tt % 2], f * 32 + 16 * (tt // 2))
                settled(sp)
                sp.dma_start(xr[:, tt % 2, :], x1_dram[bass.ds(f * L + tt * P, P), :]).then_inc(xr_in[tt % 2], 16)

            def ffn(f, last):
                load_xr(f, 0)
                load_xr(f, 1)
                if not last:
                    load_xa(f + 1)
                for tt in range(TT):
                    sp.wait_ge(o_done, f * TT + tt + 1)
                    settled(sp)
                    sp.dma_start(out[bass.ds(f * L + tt * P, P), :], xr[:, tt % 2, :]).then_inc(out_out[tt % 2], 16)
                    if tt < 2:
                        load_xr(f, tt + 2)

            ffn(0, False)
            with sp.Fori(1, nb - 1) as f:
                ffn(f, False)
            ffn(nb - 1, True)
            for k in range(2):
                sp.wait_ge(out_out[k], nb * 32)

        @block.tensor
        def _(pe):
            mm, tr = nc.tensor.matmul, nc.tensor.transpose

            def project(st, name):
                bk, free, _ = st.bank(name)
                if name == "dt":
                    pe.wait_ge(u_hi_done, (st.proj + 1) * KT)
                    pe.wait_ge(u_lo_done, (st.proj + 1) * KT)
                need(pe, in_free[bk], free)
                col, m = IN_COL[name], (NH if name == "dt" else P)
                passes = [(w_hi, u_hi), (w_hi, u_lo), (w_lo, u_hi)]
                for k in range(KT):
                    for j, (w, u) in enumerate(passes):
                        last = mm(ps_in[bk][0:m, :], w[:, k, col:col + m], u[:, k, :],
                                  start=(k == 0 and j == 0), stop=(k == KT - 1 and j == 2))
                last.then_inc(in_full[bk], 1)

            def square_sum(st, tt):
                bk, free, _ = st.bank(f"q{tt}")
                pe.wait_ge(sum_chain, (st.scan * NC + 2 * tt + 2) * 4)
                need(pe, in_free[bk], free)
                mm(ps_in[bk][:, 0:1], ssum[:, tt * P:(tt + 1) * P], ones[:, :], start=True, stop=True)\
                    .then_inc(in_full[bk], 1)

            def out_proj(st, tt):
                bk, free, _ = st.bank(f"o{tt}")
                pe.wait_ge(gate_done, st.scan * NC + 2 * tt + 2)
                need(pe, in_free[bk], free)
                for k in range(CT):
                    last = mm(ps_in[bk][:, :], zg[:, k, tt * P:(tt + 1) * P], w_out[:, k, :],
                              start=(k == 0), stop=(k == CT - 1))
                last.then_inc(in_full[bk], 1)

            def use_in(st, slot):
                for name in st.at(slot):
                    if name[0] == "q":
                        square_sum(st, int(name[1]))
                    elif name[0] == "o":
                        out_proj(st, int(name[1]))
                    else:
                        project(st, name)

            def aux(b, c, use):
                need(pe, t_free, b * 32 + c * 4 + use)
                t = slice(c * CH, (c + 1) * CH)
                if use < 2:
                    pe.wait_ge(silu_done, (b + 1) * 3)
                    settled(pe)
                    for k in range(4):
                        last = tr(ps_t[0:CH, k * P:(k + 1) * P], xs[:, 4 * use + k, t], ident[:, :])
                elif use == 2:
                    mm(ps_t[0:CH, 0:CH], bc[:, 0, t], bc[:, 1, t], start=True, stop=True)
                    tr(ps_t[0:CH, CH:CH + NS], bc[:, 0, t], ident[:, :])
                    pe.wait_ge(rq_in[c % 2], b * 128 + 32 * (c // 2 + 1))
                    for h2 in range(2):
                        last = mm(ps_t[:, CH + NS + h2 * NP:CH + NS + (h2 + 1) * NP], sel_dec[:, h2, :],
                                  rhs_d[0:6, c % 2, :, CH - 1], start=True, stop=True)
                else:
                    pe.wait_ge(csp_in, (b + 1) * 32)
                    for k in range(CT):
                        o = ps_t[:, k * CH:(k + 1) * CH]
                        mm(o, sel[:, k, :], cs12[:, t], start=True, stop=False)
                        last = mm(o, sel[0:NH, k, :], cs3[:, t], start=False, stop=True)
                last.then_inc(t_full, 1)

            def exponents(b, n):
                c, g = n // NG, n % NG
                if g == 0:
                    pe.wait_ge(rq_in[c % 2], b * 128 + 32 * (c // 2 + 1))
                need(pe, e_done, b * SLOTS + n - 1)
                mm(ps_d[n % 2][:, :].rearrange("p (k t) -> p k t", k=CT), lhs_d[0:94, c % 2, g, :],
                   rhs_d[0:94, c % 2, g:NP:NG, :], start=True, stop=True).then_inc(d_full, 1)

            def within(b, n):
                c, g = n // NG, n % NG
                pe.wait_ge(m_done, b * SLOTS + n + 1)
                if g == 0:
                    pe.wait_ge(t_free, b * 32 + c * 4 + 2)
                    need(pe, y_done, b * NC + c)
                for k in range(CT):
                    last = mm(ps_yd[g * 32:(g + 1) * 32, k * CH:(k + 1) * CH], xpad[:, c % 2, k * NG + g, :],
                              mix[:, n % 2, k, :], start=True, stop=True, tile_position=(0, g * 32))
                last.then_inc(yd_done, 1)

            def from_before(b, c):
                pe.wait_ge(s_add, b * 14 + 2 * c)
                need(pe, y1_done, b * 7 + c - 1)
                for k in range(CT):
                    last = mm(ps_yo[:, k * CH:(k + 1) * CH], state[:, k * P:(k + 1) * P],
                              bc[:, 1, c * CH:(c + 1) * CH], start=True, stop=True)
                last.then_inc(yo_full, 1)

            def new_state(b, c, h):
                if h == 0:
                    pe.wait_ge(xe_done, b * SLOTS + NG * c + NG)
                need(pe, s_add, b * 14 + 2 * c + h)
                mm(ps_s[:, :], gb[:, c % 2, CH:CH + NS],
                   xend[:, h * 16:(h + 1) * 16, :].rearrange("p a b -> p (a b)"), start=True, stop=True)\
                    .then_inc(s_full, 1)

            def body(st):
                b = st.scan
                for use in range(4):
                    aux(b, 0, use)
                exponents(b, 0)
                exponents(b, 1)
                for n in range(SLOTS):
                    c, g = n // NG, n % NG
                    if n + 2 < SLOTS:
                        exponents(b, n + 2)
                    if c + 1 < NC:
                        aux(b, c + 1, g)
                    use_in(st, n)
                    within(b, n)
                    if g == 2 and c > 0:
                        from_before(b, c)
                    if g == 3 and c < NC - 1:
                        new_state(b, c, 0)
                    if g == 0 and c > 0:
                        new_state(b, c - 1, 1)
                use_in(st, SLOTS)

            pe.wait_ge(const_in, N_CONST)
            pe.wait_ge(pro_dve, PRO_DVE)
            pe.wait_ge(pro_act, PRO_ACT)
            use_in(Stage("pro", 0), 0)
            body(Stage("body", 0))
            with pe.Fori(1, nb - 1) as i:
                body(Stage("body", i))
            body(Stage("last", nb - 1))

            def turn(f):
                pe.wait_ge(xa_in, 16 * (f + 1))
                for i in range(KT):
                    need(pe, xl_done, f * KT + i - 1)
                    for t in range(TT):
                        last = tr(ps_t2[i % 2][:, t * P:(t + 1) * P], xa[:, t, i:DM:KT], ident[:, :])
                    last.then_inc(tr_full, 1)

            def gate_up(f):
                pe.wait_ge(xh_done, (f + 1) * KT)
                pe.wait_ge(xl_done, (f + 1) * KT)
                for m in range(FT):
                    for off, banks, full, used in ((0, ps_g, g_full, sg_done), (FI, ps_u, up_full, hf_done)):
                        need(pe, used, f * FT + m - 1)
                        col = off + m * P
                        for k in range(KT):
                            for j, (w, x) in enumerate(((gu_hi, xt_hi), (gu_hi, xt_lo), (gu_lo, xt_hi))):
                                last = mm(banks[m % 2][:, :], w[:, k, col:col + P], x[:, k, :],
                                          start=(k == 0 and j == 0), stop=(k == KT - 1 and j == 2))
                        last.then_inc(full, 1)

            def down(f):
                for tt in range(TT):
                    need(pe, o_chain, (f * TT + tt - 1) * 5 - 3)
                    t = slice(tt * P, (tt + 1) * P)
                    for k in range(FT):
                        if tt == 0:
                            pe.wait_ge(hh_done, f * FT + k + 1)
                            pe.wait_ge(hl_done, f * FT + k + 1)
                        for j, (h, w) in enumerate(((h_hi, dn_hi), (h_hi, dn_lo), (h_lo, dn_hi))):
                            last = mm(ps_n[tt % 2][:, :], h[:, k, t], w[:, k, :],
                                      start=(k == 0 and j == 0), stop=(k == FT - 1 and j == 2))
                    last.then_inc(dn_full, 1)

            def ffn(f, last):
                gate_up(f)
                if not last:
                    turn(f + 1)
                down(f)

            turn(0)
            pe.wait_ge(gw_in, 64)
            ffn(0, False)
            with pe.Fori(1, nb - 1) as f:
                ffn(f, False)
            ffn(nb - 1, True)

        @block.scalar
        def _(act):
            ac = nc.scalar.activation

            def split_hi(b, before):
                act.wait_ge(u_scale, (b + 1) * 5)
                if before is not None:
                    for bk, count in before.last_z():
                        act.wait_ge(in_full[bk], count)
                for k in range(KT):
                    ac(u_hi[:, k, :], u32[:, k, :], ACT.Identity, scale=uscale[:, 0:1]).then_inc(u_hi_done, 1)

            def take_dt(st):
                bk, _, full = st.bank("dt")
                act.wait_ge(in_full[bk], full)
                need(act, dt_dve, st.proj * DT_STEPS)
                ac(dta[:, :], ps_in[bk][0:NH, :], ACT.Identity, bias=dtbias[:, 0:1], scale=uundo[0:NH, 0:1])\
                    .then_inc(in_free[bk], 1)

            def exp_dt(b):
                act.wait_ge(dt_dve, b * DT_STEPS + 1)
                ac(dtb[:, :], dtb[:, :], ACT.Exp).then_inc(dt_act, 1)

            def ln_dt(b):
                act.wait_ge(dt_dve, b * DT_STEPS + 15)
                ac(dtc[:, :], dta[:, :], ACT.Ln).then_inc(dt_act, 1)

            def take_conv(st, name):
                m = CONV_TILES.index(name)
                bk, _, full = st.bank(name)
                act.wait_ge(in_full[bk], full)
                need(act, silu_done, st.proj * 3)
                ac(pre[:, m, :], ps_in[bk][:, :], ACT.Identity, bias=cb[:, m:m + 1], scale=cws[:, m, 3:4])\
                    .then_inc(tap3, 1)

            def silu_all(st):
                b = st.proj
                bk, _, count = st.bank(CONV_TILES[-1])
                act.wait_ge(in_free[bk], count)
                need(act, t_full, b * 32)
                need(act, yo_full, b * 7)
                need(act, xd_done, b * NC)
                ac(bc[:, :, :], pre[:, 0:2, :], ACT.Silu).then_inc(silu_done, 1)
                for h in range(2):
                    ac(xs[:, 4 * h:4 * h + 4, :], pre[:, 2 + 4 * h:6 + 4 * h, :], ACT.Silu).then_inc(silu_done, 1)

            def take_z(st, name):
                bk, _, full = st.bank(name)
                act.wait_ge(in_full[bk], full)
                if st.kind == "body" and name == "z0":
                    ob, _, ofull = st.bank("o3")
                    act.wait_ge(in_full[ob], ofull)
                ac(zg[:, int(name[1]), :], ps_in[bk][:, :], ACT.Silu, scale=uundo[:, 0:1]).then_inc(in_free[bk], 1)

            def use_in(st, slot):
                for name in st.at(slot):
                    if name == "dt":
                        take_dt(st)
                    elif name in CONV_TILES:
                        take_conv(st, name)
                    elif name[0] == "z":
                        if name == "z0":
                            silu_all(st)
                        take_z(st, name)

            def aux(b, c, use):
                act.wait_ge(t_full, b * 32 + c * 4 + use + 1)
                if use < 2:
                    if use == 0:
                        need(act, yd_done, b * SLOTS + NG * (c - 1))
                        need(act, xe_done, b * SLOTS + NG * (c - 1))
                    for h2 in range(2):
                        rows = slice(h2 * CH, (h2 + 1) * CH)
                        src = ps_t[0:CH, :].rearrange("p (q h d) -> p q h d", h=2, d=HD)[:, :, h2, :]
                        last = ac(xpad[rows, c % 2, 16 * use:16 * use + 16, h2 * HD:(h2 + 1) * HD], src, ACT.Copy)
                elif use == 2:
                    need(act, m_done, b * SLOTS + NG * (c - 1))
                    need(act, s_full, b * 14 + 2 * max(c - 1, 0))
                    need(act, sd_done, b * 6 + min(max(c - 2, 0), 6))
                    for h2 in range(2):
                        ac(gb[h2 * CH:(h2 + 1) * CH, c % 2, :], ps_t[0:CH, 0:CH + NS], ACT.Copy)
                    last = ac(dec[:, c % 2, :, :].rearrange("p q h -> p h q"),
                              ps_t[:, CH + NS:CH + NS + 2 * NP].rearrange("p (h q) -> p h q", h=2), ACT.Exp)
                else:
                    need(act, y1_done, b * 7 + max(c - 2, 0))
                    last = ac(ebc[:, c % 2, :, :].rearrange("p a b -> p (a b)"), ps_t[:, :], ACT.Exp)
                last.then_inc(t_free, 1)

            def exp_group(b, n):
                act.wait_ge(d_full, b * SLOTS + n + 1)
                need(act, m_done, b * SLOTS + n - 3)
                need(act, xe_done, b * SLOTS + n - 3)
                ac(decay[:, n % NG, :, :].rearrange("p a b -> p (a b)"), ps_d[n % 2][:, :], ACT.Exp).then_inc(e_done, 1)

            def body(st):
                b = st.scan
                for use in range(4):
                    aux(b, 0, use)
                exp_group(b, 0)
                exp_group(b, 1)
                for n in range(SLOTS):
                    c, g = n // NG, n % NG
                    if n == 2 and st.proj is not None:
                        split_hi(st.proj, st.before())
                    if n + 2 < SLOTS:
                        exp_group(b, n + 2)
                    if c + 1 < NC:
                        aux(b, c + 1, g)
                    use_in(st, n)
                    if st.proj is not None and n == 7:
                        exp_dt(st.proj)
                    if st.proj is not None and n == 10:
                        ln_dt(st.proj)
                use_in(st, SLOTS)

            act.wait_ge(const_in, N_CONST)
            act.wait_ge(pro_pool, 1)
            ac(aneg[:, :], aneg[:, :], ACT.Exp).then_inc(pro_act, 1)
            act.wait_ge(pro_dve, W_SCALED)
            for k in range(KT):
                ac(w_hi[:, k, :], w_src[k], ACT.Identity, scale=w_in_scale).then_inc(pro_act, 1)
            split_hi(0, None)
            pro = Stage("pro", 0)
            take_dt(pro)
            exp_dt(0)
            act.wait_ge(pro_dve, PRO_DVE)
            take_conv(pro, "B")
            take_conv(pro, "C")
            ln_dt(0)
            for i in range(CT):
                take_conv(pro, f"x{i}")
            silu_all(pro)
            for i in range(CT):
                take_z(pro, f"z{i}")
            body(Stage("body", 0))
            with act.Fori(1, nb - 1) as i:
                body(Stage("body", i))
            body(Stage("last", nb - 1))

            def turn(f):
                for i in range(KT):
                    act.wait_ge(tr_full, f * KT + i + 1)
                    if i == 0:
                        need(act, up_full, f * FT)
                    ac(xt_hi[:, i, :], ps_t2[i % 2][:, :], ACT.Copy, scale=1024.0).then_inc(xh_done, 1)

            def hidden(f):
                for m in range(FT + 1):
                    if m < FT:
                        act.wait_ge(g_full, f * FT + m + 1)
                        need(act, hf_done, f * FT + m - 1)
                        ac(sg[:, m % 2, :], ps_g[m % 2][:, :], ACT.Silu, scale=gate_undo).then_inc(sg_done, 1)
                    if m >= 1:
                        act.wait_ge(hf_done, f * FT + m)
                        if m == 1:
                            need(act, dn_full, f * TT)
                        ac(h_hi[:, m - 1, :], hf[:, (m - 1) % 2, :], ACT.Copy).then_inc(hh_done, 1)

            def squares(f):
                for tt in range(TT):
                    act.wait_ge(dn_full, f * TT + tt + 1)
                    need(act, ms_done, f * TT + tt - 1)
                    need(act, ss_done, f * TT + tt)
                    ac(junk[:, :], ps_n[tt % 2][:, :], ACT.Square, scale=down_undo,
                       accum_out=ss2[:, tt % 2:tt % 2 + 1]).then_inc(ss_done, 1)

            def ffn(f, last):
                hidden(f)
                if not last:
                    turn(f + 1)
                squares(f)

            turn(0)
            ffn(0, False)
            with act.Fori(1, nb - 1) as f:
                ffn(f, False)
            ffn(nb - 1, True)

        @block.vector
        def _(dve):
            v = nc.vector

            def measure_u(b):
                dve.wait_ge(u_in, (b + 1) * 16)
                need(dve, u_all, b)
                v.tensor_reduce(umax[:, :], u32[:, :, :], AX.XY, ALU.max, apply_absolute_value=True).then_inc(u_max, 1)

            def scale_u(b, before):
                ch = Chain(dve, u_scale, 5, b)
                dve.wait_ge(u_all, b + 1)
                if before is not None:
                    for bk, count in before.last_z():
                        dve.wait_ge(in_free[bk], count)
                ch.step(v.tensor_scalar(utmp[:, 0:1], umax_all[:, :], 1e-30, None, ALU.max))
                ch.step(v.tensor_scalar(utmp[:, 1:2].bitcast(I32), utmp[:, 0:1].bitcast(I32), 0x7F800000, None,
                                        ALU.bitwise_and))
                ch.step(v.reciprocal(utmp[:, 0:1], utmp[:, 1:2]))
                v.tensor_scalar(uscale[:, :], utmp[:, 0:1], 2.0 ** 14, None, ALU.mult)
                ch.step(v.tensor_scalar(uundo[:, :], utmp[:, 1:2], w_in_undo, 2.0 ** -14, ALU.mult, ALU.mult))
                ch.step(v.tensor_scalar(cws[:, :, :], cw[:, :, :], uundo[:, 0:1], None, ALU.mult))
                ch.end()

            def split_lo(b):
                for k in range(KT):
                    dve.wait_ge(u_hi_done, b * KT + k + 1)
                    v.scalar_tensor_tensor(u_lo[:, k, :], u32[:, k, :], uscale[:, 0:1], u_hi[:, k, :],
                                           ALU.mult, ALU.subtract).then_inc(u_lo_done, 1)

            def taps(st, name):
                m = CONV_TILES.index(name)
                bk, _, _ = st.bank(name)
                at = st.proj * 20 + 2 * m
                dve.wait_ge(tap3, st.proj * 10 + m + 1)
                for j, k in enumerate((2, 1, 0)):
                    d = 3 - k
                    if j:
                        dve.wait_ge(conv_chain, at + j)
                    ins = v.scalar_tensor_tensor(pre[:, m, d:L], ps_in[bk][:, 0:L - d], cws[:, m, k:k + 1],
                                                 pre[:, m, d:L], ALU.mult, ALU.add)
                    ins.then_inc(conv_chain if j < 2 else in_free[bk], 1)

            def dt_first(st):
                bk, free, _ = st.bank("dt")
                dve.wait_ge(in_free[bk], free + 1)
                need(dve, dt_act, st.proj * 2)
                v.scalar_tensor_tensor(dtb[:, :], dta[:, :], -1.0, dta[:, :], ALU.mult, ALU.min).then_inc(dt_dve, 1)

            def dt_second(b):
                ch = Chain(dve, dt_dve, DT_STEPS, b)
                ch.k = 1
                dve.wait_ge(dt_act, b * 2 + 1)
                ch.step(v.tensor_scalar(dtc[:, :], dtb[:, :], 2.0, None, ALU.add))
                ch.step(v.reciprocal(dtd[:, :], dtc[:, :]))
                ch.step(v.tensor_tensor(dtb[:, :], dtb[:, :], dtd[:, :], ALU.mult))
                ch.step(v.tensor_tensor(dtc[:, :], dtb[:, :], dtb[:, :], ALU.mult))
                ch.step(v.tensor_scalar(dtd[:, :], dtc[:, :], LOG1P[7], LOG1P[6], ALU.mult, ALU.add))
                ch.step(v.tensor_tensor(dtd[:, :], dtd[:, :], dtc[:, :], ALU.mult))
                for k in range(5, 0, -1):
                    ch.step(v.scalar_tensor_tensor(dtd[:, :], dtd[:, :], LOG1P[k], dtc[:, :], ALU.add, ALU.mult))
                ch.step(v.scalar_tensor_tensor(dtd[:, :], dtd[:, :], LOG1P[0], dtb[:, :], ALU.add, ALU.mult))
                ch.step(v.scalar_tensor_tensor(dtd[:, :], dta[:, :], 0.0, dtd[:, :], ALU.max, ALU.add))
                ch.step(v.tensor_scalar(dta[:, :], dtd[:, :], 1e-18, None, ALU.max))
                assert ch.k == 15
                ch.step(v.tensor_scalar(dtb[:, :], dtd[:, :], aneg[:, 0:1], None, ALU.mult))
                ch.step(v.tensor_tensor_scan(dte[:, :], mask[:, :], dtb[:, :], 0.0, ALU.mult, ALU.add))
                need(dve, parts_out, b * 48)
                ch.step(v.tensor_copy(cs_parts[:, 0, :], dte[:, :]))
                ch.step(v.tensor_tensor(dtf[:, :], dte[:, :], cs_parts[:, 0, :], ALU.subtract))
                ch.step(v.tensor_copy(cs_parts[:, 1, :], dtf[:, :]))
                v.tensor_tensor(cs_parts[:, 2, :], dtf[:, :], cs_parts[:, 1, :], ALU.subtract)

            def dt_third(b):
                ch = Chain(dve, dt_dve, DT_STEPS, b)
                ch.k = 20
                dve.wait_ge(dt_act, b * 2 + 2)
                ch.step(v.tensor_tensor(dtc[:, :], dtc[:, :], dte[:, :], ALU.subtract))
                ch.step(v.tensor_copy(ld_parts[:, 0, :], dtc[:, :]))
                ch.step(v.tensor_tensor(dtf[:, :], dtc[:, :], ld_parts[:, 0, :], ALU.subtract))
                ch.step(v.tensor_copy(ld_parts[:, 1, :], dtf[:, :]))
                ch.step(v.tensor_tensor(ld_parts[:, 2, :], dtf[:, :], ld_parts[:, 1, :], ALU.subtract))
                ch.end()

            def decode(b, k):
                kind, i = fw_units[k]
                ch = Chain(dve, fw_chain, 36, b)
                ch.k = 6 * k
                dve.wait_ge(fw_in, (b * 6 + k + 1) * 32)
                src = fw_words[:, :]
                col = 0 if kind == "g" else 1
                ch.step(v.tensor_scalar(fw_words[:, :], src, shift[:, col:col + 1], None, ALU.logical_shift_right))
                at = 4 * i if kind == "g" else 0
                for dst, top, bits in ((fw_mag, 9, 0x0E00), (fw_sign, 12, 0x8000)):
                    by = top - at
                    op = ALU.logical_shift_left if by >= 0 else ALU.logical_shift_right
                    ch.step(v.tensor_scalar(dst[:, :], fw_words[:, :], abs(by), bits, op, ALU.bitwise_and))
                ch.step(v.tensor_tensor(fw_mag[:, :], fw_mag[:, :], fw_sign[:, :], ALU.bitwise_or))
                ch.step(v.scalar_tensor_tensor(fw_w[:, :], fw_mag[:, :].bitcast(F16)[:, 0:2 * DEC:2],
                                               gu_in_scale if kind == "g" else dn_in_scale, fw_scale[:, :],
                                               ALU.mult, ALU.mult))
                need(dve, fw_out, (b * 6 + k) * 32)
                ch.step(v.tensor_copy(fw_hi[:, :], fw_w[:, :]))
                v.tensor_tensor(fw_lo[:, :], fw_w[:, :], fw_hi[:, :], ALU.subtract).then_inc(fw_done, 1)

            def mixing(b, n):
                c = n // NG
                dve.wait_ge(e_done, b * SLOTS + n + 1)
                if n % NG == 0:
                    dve.wait_ge(t_free, b * 32 + c * 4 + 3)
                need(dve, yd_done, b * SLOTS + n - 1)
                v.tensor_tensor(mix[:, n % 2, :, :], decay[:, n % NG, :, :],
                                gb[:, c % 2, 0:CH].unsqueeze(1).broadcast_to([P, CT, CH]), ALU.mult).then_inc(m_done, 1)

            def add_state(b, c, h):
                cols = slice(h * 512, (h + 1) * 512)
                dve.wait_ge(s_full, b * 14 + 2 * c + h + 1)
                if c == 0:
                    need(dve, yo_full, b * 7)
                    v.tensor_copy(state[:, cols], ps_s[:, :]).then_inc(s_add, 1)
                else:
                    dve.wait_ge(sd_done, b * 6 + c)
                    dve.wait_ge(yo_full, b * 7 + c)
                    v.tensor_tensor(state[:, cols], ps_s[:, :], state_d[:, cols], ALU.add).then_inc(s_add, 1)

            def flat(ap):
                return ap.rearrange("p a b -> p (a b)")

            def y_before(b, c):
                if c > 0:
                    dve.wait_ge(yo_full, b * 7 + c)
                    dve.wait_ge(t_free, b * 32 + c * 4 + 4)
                    need(dve, y2_done, b * 7 + c - 1)
                    v.tensor_tensor(flat(yoff[:, :, :]), ps_yo[:, :], flat(ebc[:, c % 2, :, :]), ALU.mult).then_inc(y1_done, 1)
                    dve.wait_ge(y1_done, b * 7 + c)
                    dve.wait_ge(xd_done, b * NC + c + 1)
                    v.tensor_tensor(y[:, c % 2, :, :], y[:, c % 2, :, :], yoff[:, :, :], ALU.add).then_inc(y2_done, 1)

            def y_all(b, c):
                dve.wait_ge(yd_done, b * SLOTS + NG * (c + 1))
                dve.wait_ge(xd_done, b * NC + c + 1)
                need(dve, y2_done, b * 7 + c)
                v.tensor_tensor(flat(y[:, c % 2, :, :]), ps_yd[:, :], flat(y[:, c % 2, :, :]), ALU.add).then_inc(y_done, 1)

            def mean_square(st, tt):
                bk, _, full = st.bank(f"q{tt}")
                dve.wait_ge(in_full[bk], full)
                need(dve, rinv_done, st.scan * TT)
                v.tensor_scalar(msv[:, tt:tt + 1], ps_in[bk][:, 0:1], 1.0 / DI, 1e-5, ALU.mult, ALU.add)\
                    .then_inc(in_free[bk], 1)

            def norm_tile(st, tt):
                b = st.scan
                bk, _, full = st.bank(f"o{tt}")
                i = tt % 2
                ch = Chain(dve, ln_chain, 12, b)
                ch.k = 3 * tt
                dve.wait_ge(in_full[bk], full)
                dve.wait_ge(rinv_done, b * TT + tt + 1)
                dve.wait_ge(res_in[i], b * 32 + 16 * (tt // 2) + 16)
                v.scalar_tensor_tensor(res[:, i, :], ps_in[bk][:, :], rinv[:, tt:tt + 1], res[:, i, :],
                                       ALU.mult, ALU.add).then_inc(in_free[bk], 1)
                dve.wait_ge(in_free[bk], full)
                ch.step(v.bn_stats(bn[:, i, :], res[:, i, :]), settled)
                ch.step(v.bn_aggr(mv[:, i, :], bn[:, i, :]))
                v.tensor_scalar(mv[:, i, 1:2], mv[:, i, 1:2], 1e-5, None, ALU.add).then_inc(ln_chain, 1)

            def norm_tile_end(st, tt):
                b, i = st.scan, tt % 2
                dve.wait_ge(rstd_done, b * TT + tt + 1)
                v.tensor_scalar(res[:, i, :], res[:, i, :], mv[:, i, 0:1], rstd[:, i:i + 1],
                                ALU.subtract, ALU.mult).then_inc(x1_done, 1)

            def use_in(st, slot):
                for name in st.at(slot):
                    if name in CONV_TILES:
                        taps(st, name)
                    elif name[0] == "q":
                        mean_square(st, int(name[1]))
                    elif name[0] == "o":
                        norm_tile(st, int(name[1]))

            def body(st):
                b = st.scan
                for n in range(SLOTS):
                    c, g = n // NG, n % NG
                    if n == 1 and st.proj is not None:
                        scale_u(st.proj, st.before())
                    if n == 2 and st.proj is not None:
                        split_lo(st.proj)
                    mixing(b, n)
                    if g == 0 and c > 0:
                        y_all(b, c - 1)
                        add_state(b, c - 1, 0)
                    if g == 1 and c > 0:
                        add_state(b, c - 1, 1)
                    if g == 3:
                        y_before(b, c)
                    if n > 0:
                        use_in(st, n - 1)
                    for tt in range(TT - 1):
                        if f"o{tt}" in st.at(n - 2):
                            norm_tile_end(st, tt)
                    if st.proj is not None:
                        if n == 6:
                            dt_first(st)
                        if n == 8:
                            dt_second(st.proj)
                        if n == 12:
                            dt_third(st.proj)
                        if n == 28:
                            measure_u(b + 2)
                    if n in FW_SLOT:
                        decode(b, FW_SLOT[n])
                y_all(b, NC - 1)
                use_in(st, SLOTS - 1)
                use_in(st, SLOTS)
                norm_tile_end(st, TT - 1)

            ch = Chain(dve, pro_dve, PRO_DVE, 0)
            v.memset(ones[:, :], 1.0)
            v.memset(half[:, :], -0.5)
            dve.wait_ge(const_in, N_CONST)
            measure_u(0)
            dve.wait_ge(w_in_in, KT * 16)
            for j, src in enumerate(w_src):
                v.tensor_reduce(wmax[:, j:j + 1], src, AX.X, ALU.max, apply_absolute_value=True)
            v.tensor_reduce(maxes[:, 1:2], scales_once[:, 0:GU_SCALES], AX.X, ALU.max)
            ch.step(v.tensor_reduce(maxes[:, 2:3], scales_once[:, GU_SCALES:ALL_SCALES], AX.X, ALU.max))
            ch.step(v.tensor_reduce(maxes[:, 0:1], wmax[:, :], AX.X, ALU.max))
            assert ch.k == MAXES_READY
            dve.wait_ge(pro_pool, 2)
            ch.step(v.tensor_scalar(maxes[:, :], maxes_all[:, :], 1e-30, None, ALU.max))
            ch.step(v.tensor_scalar(pow2[:, :].bitcast(I32), maxes[:, :].bitcast(I32), 0x7F800000, None, ALU.bitwise_and))
            ch.step(v.reciprocal(inv2[:, :], pow2[:, :]))
            v.tensor_scalar(w_in_scale, inv2[:, 0:1], 2.0 ** 14, None, ALU.mult)
            v.tensor_scalar(w_in_undo, pow2[:, 0:1], 2.0 ** -14, None, ALU.mult)
            v.tensor_scalar(gu_in_scale, inv2[:, 1:2], 2.0 ** 25, None, ALU.mult)
            v.tensor_scalar(dn_in_scale, inv2[:, 2:3], 2.0 ** 25, None, ALU.mult)
            v.tensor_scalar(gate_undo, pow2[:, 1:2], 2.0 ** -21, None, ALU.mult)
            v.tensor_scalar(up_undo, inv2[:, 1:2], 2.0 ** -31, None, ALU.mult)
            ch.step(v.tensor_scalar(scratch1, pow2[:, 1:2], pow2[:, 1:2], 0.5, ALU.mult, ALU.mult))
            assert ch.k == W_SCALED
            v.tensor_scalar(down_undo, scratch1, pow2[:, 2:3], None, ALU.mult)
            dve.wait_ge(pro_act, 1)
            v.tensor_scalar(aneg[:, :], aneg[:, :], -1.0, None, ALU.mult)
            for k in range(CT):
                v.tensor_scalar(w_out[:, k, :], w_out[:, k, :], normw[:, k:k + 1], None, ALU.mult)
            for k in range(KT):
                dve.wait_ge(pro_act, 2 + k)
                ins = v.scalar_tensor_tensor(w_lo[:, k, :], w_src[k], w_in_scale, w_hi[:, k, :],
                                             ALU.mult, ALU.subtract)
            ch.step(ins)
            ch.end()
            scale_u(0, None)
            split_lo(0)
            pro = Stage("pro", 0)
            dt_first(pro)
            dt_second(0)
            taps(pro, "B")
            taps(pro, "C")
            dt_third(0)
            for i in range(CT):
                taps(pro, f"x{i}")
            measure_u(1)
            body(Stage("body", 0))
            with dve.Fori(1, nb - 1) as i:
                body(Stage("body", i))
            body(Stage("last", nb - 1))

            def turn(f):
                for i in range(KT):
                    dve.wait_ge(xh_done, f * KT + i + 1)
                    v.scalar_tensor_tensor(xt_lo[:, i, :], ps_t2[i % 2][:, :], 1024.0, xt_hi[:, i, :],
                                           ALU.mult, ALU.subtract).then_inc(xl_done, 1)

            def hidden(f):
                for m in range(FT):
                    dve.wait_ge(up_full, f * FT + m + 1)
                    dve.wait_ge(sg_done, f * FT + m + 1)
                    need(dve, hh_done, f * FT + m - 1)
                    need(dve, hl_done, f * FT + m - 1)
                    v.scalar_tensor_tensor(hf[:, m % 2, :], ps_u[m % 2][:, :], up_undo, sg[:, m % 2, :],
                                           ALU.mult, ALU.mult).then_inc(hf_done, 1)

            def norms(f):
                for tt in range(TT):
                    i = tt % 2
                    ch = Chain(dve, o_chain, 20, f)
                    ch.k = 5 * tt
                    dve.wait_ge(ss_done, f * TT + tt + 1)
                    v.tensor_scalar(ms2[:, i:i + 1], ss2[:, i:i + 1], 1.0 / DM, 1e-6, ALU.mult, ALU.add).then_inc(ms_done, 1)
                    dve.wait_ge(ri_done, f * TT + tt + 1)
                    ch.step(v.tensor_scalar(rk2[:, i:i + 1], ri2[:, i:i + 1], down_undo, None, ALU.mult))
                    dve.wait_ge(xr_in[i], f * 32 + 16 * (tt // 2) + 16)
                    ch.step(v.scalar_tensor_tensor(xr[:, i, :], ps_n[i][:, :], rk2[:, i:i + 1], xr[:, i, :],
                                                   ALU.mult, ALU.add))
                    ch.step(v.bn_stats(bn2[:, i, :], xr[:, i, :]), settled)
                    ch.step(v.bn_aggr(mv2[:, i, :], bn2[:, i, :]))
                    v.tensor_scalar(mv2[:, i, 1:2], mv2[:, i, 1:2], 1e-5, None, ALU.add).then_inc(o_chain, 1)
                    dve.wait_ge(rs_done, f * TT + tt + 1)
                    v.tensor_scalar(xr[:, i, :], xr[:, i, :], mv2[:, i, 0:1], rs2[:, i:i + 1],
                                    ALU.subtract, ALU.mult).then_inc(o_done, 1)

            def ffn(f, last):
                hidden(f)
                if not last:
                    turn(f + 1)
                norms(f)

            turn(0)
            ffn(0, False)
            with dve.Fori(1, nb - 1) as f:
                ffn(f, False)
            ffn(nb - 1, True)

        @block.gpsimd
        def _(pool):
            g_ = nc.gpsimd

            def reduce_u(b):
                pool.wait_ge(u_max, b + 1)
                need(pool, u_scale, b * 5)
                settled(pool)
                g_.partition_all_reduce(umax_all[:, :], umax[:, :], P, RMAX).then_inc(u_all, 1)

            def to_end(b, n):
                c, g = n // NG, n % NG
                pool.wait_ge(e_done, b * SLOTS + n + 1)
                pool.wait_ge(t_free, b * 32 + c * 4 + 2)
                if g == 0:
                    need(pool, s_full, b * 14 + 2 * c)
                g_.tensor_tensor(xend[:, g:NP:NG, :], xpad[:, c % 2, g:NP:NG, :],
                                 decay[:, g, :, CH - 1:CH].broadcast_to([P, CT, 2 * HD]), ALU.mult).then_inc(xe_done, 1)

            def decay_state(b, c):
                pool.wait_ge(s_add, b * 14 + 2 * c)
                pool.wait_ge(t_free, b * 32 + c * 4 + 3)
                g_.tensor_tensor(state_d[:, :].rearrange("p (q d) -> p q d", d=HD),
                                 state[:, :].rearrange("p (q d) -> p q d", d=HD),
                                 dec[:, c % 2, :, :].rearrange("p q h -> p (q h)").unsqueeze(2).broadcast_to([P, NH, HD]),
                                 ALU.mult).then_inc(sd_done, 1)

            def skip_term(b, c):
                pool.wait_ge(silu_done, (b + 1) * 3)
                need(pool, gate_done, b * NC + c - 1)
                g_.tensor_tensor(y[:, c % 2, :, :], xs[:, :, c * CH:(c + 1) * CH],
                                 dskip[:, :].unsqueeze(2).broadcast_to([P, CT, CH]), ALU.mult).then_inc(xd_done, 1)

            def gate(st, c):
                b, t = st.scan, slice(c * CH, (c + 1) * CH)
                pool.wait_ge(y_done, b * NC + c + 1)
                if c == 0:
                    for bk, count in st.before().last_z():
                        pool.wait_ge(in_free[bk], count)
                g_.tensor_tensor(zg[:, :, t], y[:, c % 2, :, :], zg[:, :, t], ALU.mult).then_inc(gate_done, 1)
                pool.wait_ge(gate_done, b * NC + c + 1)
                ch = Chain(pool, sum_chain, 4 * NC, b)
                ch.k = 4 * c
                ch.step(g_.tensor_tensor(sq[:, :, :], zg[:, :, t], zg[:, :, t], ALU.mult))
                ch.step(g_.tensor_tensor(sq[:, 0:4, :], sq[:, 0:4, :], sq[:, 4:8, :], ALU.add))
                ch.step(g_.tensor_tensor(sq[:, 0:2, :], sq[:, 0:2, :], sq[:, 2:4, :], ALU.add))
                ch.step(g_.tensor_tensor(ssum[:, t], sq[:, 0, :], sq[:, 1, :], ALU.add))

            def root(st, tt):
                bk, _, count = st.bank(f"q{tt}")
                pool.wait_ge(in_free[bk], count)
                g_.tensor_tensor(rinv[:, tt:tt + 1], msv[:, tt:tt + 1], half[:, :], ALU.pow).then_inc(rinv_done, 1)

            def ln_root(b, tt):
                pool.wait_ge(ln_chain, b * 12 + 3 * tt + 3)
                g_.tensor_tensor(rstd[:, tt % 2:tt % 2 + 1], mv[:, tt % 2, 1:2], half[:, :], ALU.pow).then_inc(rstd_done, 1)

            def body(st):
                b = st.scan
                skip_term(b, 0)
                for n in range(SLOTS):
                    c, g = n // NG, n % NG
                    if n == 29 and st.proj is not None:
                        reduce_u(b + 2)
                    to_end(b, n)
                    if g == 1 and 1 <= c < NC - 1:
                        decay_state(b, c)
                    if g == 1 and c > 0:
                        gate(st, c - 1)
                    if g == 2 and c + 1 < NC:
                        skip_term(b, c + 1)
                    for tt in range(TT):
                        if n > 0 and f"q{tt}" in st.at(n - 1):
                            root(st, tt)
                        if n > 0 and f"o{tt}" in st.at(n - 1):
                            ln_root(b, tt)
                gate(st, NC - 1)
                root(st, TT - 1)
                ln_root(b, TT - 1)

            g_.memset(xpad[:, :, :, :], 0.0).then_inc(pro_pool, 1)
            reduce_u(0)
            pool.wait_ge(pro_dve, MAXES_READY)
            g_.partition_all_reduce(maxes_all[:, :], maxes[:, :], P, RMAX).then_inc(pro_pool, 1)
            reduce_u(1)
            body(Stage("body", 0))
            with pool.Fori(1, nb - 1) as i:
                body(Stage("body", i))
            body(Stage("last", nb - 1))

            def hidden(f):
                for m in range(FT):
                    pool.wait_ge(hh_done, f * FT + m + 1)
                    if m == 0:
                        need(pool, dn_full, f * TT)
                    g_.tensor_tensor(h_lo[:, m, :], hf[:, m % 2, :], h_hi[:, m, :], ALU.subtract).then_inc(hl_done, 1)

            def roots(f):
                for tt in range(TT):
                    i = tt % 2
                    pool.wait_ge(ms_done, f * TT + tt + 1)
                    g_.tensor_tensor(ri2[:, i:i + 1], ms2[:, i:i + 1], half[:, :], ALU.pow).then_inc(ri_done, 1)
                    pool.wait_ge(o_chain, f * 20 + 5 * tt + 5)
                    g_.tensor_tensor(rs2[:, i:i + 1], mv2[:, i, 1:2], half[:, :], ALU.pow).then_inc(rs_done, 1)

            def ffn(f):
                hidden(f)
                roots(f)

            ffn(0)
            with pool.Fori(1, nb - 1) as f:
                ffn(f)
            ffn(nb - 1)


def kernel(L0_attn_u, L0_attn_in_proj_w, L0_attn_conv_w, L0_attn_conv_b, L0_attn_dt_bias, L0_attn_A_log,
           L0_attn_D, L0_attn_norm_weight, L0_attn_out_proj_w, L0_ffn_gate_up_packed, L0_ffn_gate_up_scales,
           L0_ffn_down_packed, L0_ffn_down_scales):
    import concourse.bacc as bacc
    from concourse.bass_utils import run_bass_kernel_spmd

    arrays = lay_out(*(np.asarray(a) for a in (
        L0_attn_u, L0_attn_in_proj_w, L0_attn_conv_w, L0_attn_conv_b, L0_attn_dt_bias, L0_attn_A_log, L0_attn_D,
        L0_attn_norm_weight, L0_attn_out_proj_w, L0_ffn_gate_up_packed, L0_ffn_gate_up_scales, L0_ffn_down_packed,
        L0_ffn_down_scales)))
    nc = bacc.Bacc("TRN2", target_bir_lowering=False, num_devices=1, dynamic_dma_scratch_size=1024)
    args = [nc.dram_tensor(n, a.shape, mybir.dt.from_np(a.dtype), kind="ExternalInput").ap() for n, a in arrays.items()]
    args.append(nc.dram_tensor("out", [NB * L, DM], F32, kind="ExternalOutput").ap())
    build(nc, *args)
    result = run_bass_kernel_spmd(nc, [arrays], core_ids=[0])
    return result.results[0]["out"].reshape(NB, L, DM)


def lay_out(u, w_in, conv_w, conv_b, dt_bias, a_log, d, norm_w, w_out, gu, gu_s, dn, dn_s):
    c = np.ascontiguousarray

    def bf16_bits(a):
        return (c(a, np.float32).view(np.uint32) >> 16).astype(np.uint16)

    h2, tile, g = np.meshgrid(range(2), range(CT), range(NG), indexing="ij")
    heads = (8 * tile + 2 * g + h2).ravel()
    zs, xb, ds = w_in[:DI], w_in[DI:2 * DI + 2 * NS], w_in[2 * DI + 2 * NS:]
    w_rows = np.concatenate([ds[heads], xb[DI:], xb[:DI], zs])
    order = np.concatenate([np.arange(DI, DI + 2 * NS), np.arange(DI)])
    tokens = u.reshape(NB * L, DM)
    sel = np.zeros((2, NH, CT, P), np.float32)
    for q, h in enumerate(heads):
        sel[:, q, h // 8, (h % 8) * HD:(h % 8 + 1) * HD] = 1
    rhs = np.zeros((24 + CH, NP, CH), np.float32)
    for r in range(3):
        for k in range(CT):
            rhs[8 * r + k, NG * k:NG * k + NG] = 1
    rhs[24:] = np.where(np.arange(CH)[None, None, :] < np.arange(CH)[:, None, None], NEG, 0)
    lhs = np.zeros((94, NG, 2, CH), np.float32)
    dec = np.zeros((6, 2, P), np.float32)
    for r in range(3):
        for h in range(2):
            lhs[2 * r + h, :, h] = 1
            dec[2 * r + h, h] = 1
    lhs[30:] = np.eye(CH)[:, None, None, :]
    mask = np.broadcast_to(np.arange(L) % CH != 0, (NH, L))
    p = np.arange(P)
    return {
        "u_t": c(np.concatenate([tokens.T, np.zeros((DM, L), u.dtype)], 1)),
        "u_tok": c(tokens),
        "w_in_t": c(w_rows.T),
        "conv_w": c(conv_w[order].reshape(2 + CT, P, TAPS).transpose(1, 0, 2)),
        "conv_b": c(conv_b[order].reshape(2 + CT, P).T),
        "dt_bias": c(dt_bias[heads][:, None]),
        "a_log": c(a_log[heads][:, None]),
        "d_skip": c(np.repeat(d, HD).reshape(CT, P).T),
        "norm_w": c(norm_w.reshape(CT, P).T),
        "w_out_t": c(w_out.T),
        "gu_words": c(np.repeat(gu.T, 2, axis=0)),
        "gu_scales": c(np.repeat(gu_s, P // KT, axis=0)),
        "dn_words": c(np.repeat(dn.T, 8, axis=0).reshape(FT, P, DM).transpose(1, 0, 2)),
        "dn_scales": c(np.broadcast_to(dn_s, (P, FT, DM))),
        "all_scales": c(np.concatenate([gu_s.reshape(P, -1), dn_s.reshape(P, -1)], 1)),
        "c_sel": bf16_bits(sel.reshape(P, CT, P)),
        "c_rhs": bf16_bits(rhs),
        "c_lhs": bf16_bits(lhs.reshape(94, NG, P)),
        "c_dec": bf16_bits(dec),
        "c_ident": np.eye(P, dtype=np.float32),
        "c_mask": bf16_bits(mask),
        "c_shift": c(np.stack([16 * (p % 2), 4 * (p % 8)], 1)).astype(np.int32),
    }
```

```python
from contextlib import ExitStack

import numpy as np

import concourse.bass as bass
from concourse import mybir

ALU = mybir.AluOpType
ACT = mybir.ActivationFunctionType
AX = mybir.AxisListType
F32 = mybir.dt.float32
F16 = mybir.dt.float16
BF16 = mybir.dt.bfloat16
I32 = mybir.dt.int32
U16 = mybir.dt.uint16
RMAX = bass.bass_isa.ReduceOp.max

P = 128
NB = 8
L = 512
DM = 512
KT = DM // P
DI = 1024
CT = DI // P
NH = 64
HD = DI // NH
NS = 128
NP = NH // 2
CH = 64
NC = L // CH
NG = 4
LH = L // 2
SLOTS = NC * NG
TT = L // P
TAPS = 4
IN_COLS = NH + 2 * NS + 2 * DI
FI = 1408
FT = FI // P
GU_SCALES = KT * 2 * FI // P
ALL_SCALES = GU_SCALES + FT * DM // P
MAXES_READY, W_SCALED, PRO_DVE, PRO_ACT = 2, 6, 7, 1 + KT
DT_STEPS = 25
DT_PART = [1, 3, 7, 12, 16]
DT_SLOT = {9: 0, 11: 1, 13: 2, 17: 3, 19: 4}
SPLIT_SLOT = {k + 1: (k,) for k in range(KT)}
DEC = 352
NEG = -1.0e30
LOG1P = [2.0 / (2 * k + 1) for k in range(8)]

HEAD = ["a0", "z1", "z2", "e0", "a1", "e1", "z3", "a2", "a3", "e2", "z4", "z5", "z6", "z7"]
TAIL = {"pro": ["x7", "z0"] + HEAD, "body": ["x7", "z0", "o3", "q3"] + HEAD, "last": ["o3", "q3"]}
AUX_ORDER = (0, 2, 1, 3)
PRO_USES = [(0, "dt"), (0, "B"), (0, "C")] + [(0, f"x{i}") for i in range(CT - 1)]
BODY_USES = [(5, "dt"), (7, "B"), (9, "C"), (11, "x0"), (12, "q0"), (14, "o0"), (15, "x1"), (17, "x2"),
             (19, "x3"), (20, "q1"), (22, "o1"), (23, "x4"), (25, "x5"), (27, "x6"), (28, "q2"), (30, "o2")]
LAST_USES = [(12, "q0"), (14, "o0"), (20, "q1"), (22, "o1"), (28, "q2"), (30, "o2")]
CONV_TILES = ["B", "C"] + [f"x{i}" for i in range(CT)]
IN_COL = {"dt": 0, "B": NH, "C": NH + NS}
IN_COL |= {f"x{i}": NH + 2 * NS + i * P for i in range(CT)}
IN_COL |= {f"z{i}": NH + 2 * NS + DI + i * P for i in range(CT)}


def need(eng, sem, value):
    if isinstance(value, int) and value <= 0:
        return
    eng.wait_ge(sem, value)


def banks_of(uses):
    return [i % 2 for i in range(len(uses))]


class Stage:

    def __init__(self, kind, b):
        self.kind = kind
        self.scan = b if kind != "pro" else None
        self.proj = {"pro": 0, "body": b + 1, "last": None}[kind]
        uses = {"pro": PRO_USES, "body": BODY_USES, "last": LAST_USES}
        uses = {k: u + [(SLOTS, name) for name in TAIL[k] if name[0] not in "ae" and name != "q3"] for k, u in uses.items()}
        self.uses, self.tail = uses[kind], TAIL[kind]
        pro, body = [[banks_of(uses[k]).count(i) for i in range(2)] for k in ("pro", "body")]
        self.base = [0, 0] if kind == "pro" else [b * body[i] + pro[i] for i in range(2)]

    def bank(self, name):
        at = [u for _, u in self.uses].index(name)
        banks = banks_of(self.uses)
        count = self.base[banks[at]] + banks[:at].count(banks[at])
        return banks[at], count, count + 1

    def at(self, slot):
        return [u for s, u in self.uses if s == slot]

    def before(self):
        return Stage("pro", 0) if isinstance(self.scan, int) and self.scan == 0 else Stage("body", self.scan - 1)

    def last_z(self):
        found = [self.bank(f"z{i}") for i in (CT - 2, CT - 1)]
        assert found[0][0] != found[1][0]
        return [(bk, full) for bk, _, full in found]


class Chain:

    def __init__(self, eng, sem, per, b):
        self.eng, self.sem, self.per, self.base, self.k = eng, sem, per, b * per, 0

    def step(self, ins, then=None):
        self.k += 1
        ins.then_inc(self.sem, 1)
        self.eng.wait_ge(self.sem, self.base + self.k)
        if then:
            then(self.eng)

    def end(self):
        assert self.k == self.per, (self.k, self.per)


def build(nc, u_t, u_tok, w_in_t, conv_w, conv_b, dt_bias, a_log, d_skip, norm_w, w_out_t,
          gu_words, gu_scales, dn_words, dn_scales, all_scales, c_sel, c_rhs, c_lhs, c_dec, c_ident, c_mask,
          c_shift, out, nb=NB):
    ctx = ExitStack()
    with ctx:
        def sem(name):
            return ctx.enter_context(nc.semaphore(name))

        cs_dram = nc.dram_tensor("cs_dram", [nb, 3 * NH, L], BF16, kind="Internal")
        ld_dram = nc.dram_tensor("ld_dram", [nb, 3, NP, 2, L], BF16, kind="Internal")
        x1_dram = nc.dram_tensor("x1_dram", [nb * L, DM], F32, kind="Internal")
        gu_dram = nc.dram_tensor("gu_dram", [2, KT, P, 2 * FI], F16, kind="Internal")
        dn_dram = nc.dram_tensor("dn_dram", [2, P, FT, DM], F16, kind="Internal")

        def keep(name, shape, dt=F32):
            return ctx.enter_context(nc.sbuf_tensor(name, shape, dt))

        maxes = keep("maxes", [P, 3])
        maxes_all = keep("maxes_all", [P, 3])
        pow2 = keep("pow2", [P, 3])
        inv2 = keep("inv2", [P, 3])
        scal = keep("scal", [P, 8])
        ident = keep("ident", [P, P])
        half = keep("half", [P, 1])
        w_in_scale, w_in_undo = scal[:, 0:1], scal[:, 1:2]
        gu_in_scale, dn_in_scale = scal[:, 2:3], scal[:, 3:4]
        gate_undo, up_undo, down_undo = scal[:, 4:5], scal[:, 5:6], scal[:, 6:7]
        scratch1 = scal[:, 7:8]

        p1 = ExitStack()

        def sb(name, shape, dt=F32):
            return p1.enter_context(nc.sbuf_tensor(name, shape, dt))

        w_hi = sb("w_hi", [P, KT, IN_COLS], F16)
        w_lo = sb("w_lo", [P, KT, IN_COLS], F16)
        w_out = sb("w_out", [P, CT, DM])
        pre = sb("pre", [P, 2 + CT, L])
        bc = sb("bc", [P, 2, L])
        xs = sb("xs", [P, CT, L])
        zg = sb("zg", [P, CT, L])
        u32 = sb("u32", [P, KT, L])
        u_hi = sb("u_hi", [P, KT, L], F16)
        u_lo = sb("u_lo", [P, KT, L], F16)
        res = sb("res", [P, 2, DM])
        rhs_d = sb("rhs_d", [P, 2, NP, CH], BF16)
        lhs_d = sb("lhs_d", [P, 2, NG, 2 * CH], BF16)
        decay = sb("decay", [P, NG, CT, CH])
        mix = sb("mix", [P, NG, CT, CH])
        xpad = sb("xpad", [P, 2, NP, 2 * HD])
        xend = sb("xend", [P, NP, 2 * HD])
        state = sb("state", [P, DI])
        state_d = sb("state_d", [P, DI])
        gb = sb("gb", [P, 2, CH + NS])
        dec = sb("dec", [P, 2, NP, 2])
        ebc = sb("ebc", [P, 2, CT, CH])
        yoff = sb("yoff", [P, CT, CH])
        y = sb("y", [P, 2, CT, CH])
        sq = sb("sq", [P, CT, CH])
        ssum = sb("ssum", [P, L])
        cs12 = sb("cs12", [P, L], BF16)
        cs3 = sb("cs3", [NH, L], BF16)
        cs_parts = sb("cs_parts", [P, 3, LH], BF16)
        ld_parts = sb("ld_parts", [P, 3, LH], BF16)
        dta = sb("dta", [P, LH])
        dtb = sb("dtb", [P, LH])
        dtc = sb("dtc", [P, LH])
        dtd = sb("dtd", [P, LH])
        dte = sb("dte", [P, LH])
        dtf = sb("dtf", [P, LH])
        sel = sb("sel", [P, CT, P], BF16)
        sel_dec = sb("sel_dec", [6, 2, P], BF16)
        mask = sb("mask", [P, LH], BF16)
        cw = sb("cw", [P, 2 + CT, TAPS])
        cws = sb("cws", [P, 2 + CT, TAPS])
        cb = sb("cb", [P, 2 + CT])
        dskip = sb("dskip", [P, CT])
        normw = sb("normw", [P, CT])
        dtbias = sb("dtbias", [NH, 1])
        aneg = sb("aneg", [P, 1])
        ones = sb("ones", [P, 1])
        umax = sb("umax", [P, 1])
        umax_all = sb("umax_all", [P, 1])
        uscale = sb("uscale", [P, 1])
        uundo = sb("uundo", [P, 1])
        utmp = sb("utmp", [P, 2])
        msv = sb("msv", [P, TT])
        rinv = sb("rinv", [P, TT])
        bn = sb("bn", [P, 2, 6])
        mv = sb("mv", [P, 2, 2])
        rstd = sb("rstd", [P, 2])
        wmax = sb("wmax", [P, KT])
        scales_once = sb("scales_once", [P, ALL_SCALES], F16)
        shift = sb("shift", [P, 2], I32)
        fw_words = sb("fw_words", [P, 2, DEC], I32)
        fw_scale = sb("fw_scale", [P, 2, DEC], F16)
        fw_mag = sb("fw_mag", [P, DEC], I32)
        fw_sign = sb("fw_sign", [P, DEC], I32)
        fw_w = sb("fw_w", [P, DEC])
        fw_hi = sb("fw_hi", [P, 2, DEC], F16)
        fw_lo = sb("fw_lo", [P, 2, DEC], F16)
        p1.close()
        rooms = [(pre, 0), (pre, IN_COLS), (zg, 0), (xs, 0)]
        w_src = [t[:, :, :].rearrange("p a b -> p (a b)")[:, at:at + IN_COLS] for t, at in rooms]

        p2 = ExitStack()

        def sb2(name, shape, dt=F32):
            return p2.enter_context(nc.sbuf_tensor(name, shape, dt))

        gu_hi = sb2("gu_hi", [P, KT, 2 * FI], F16)
        gu_lo = sb2("gu_lo", [P, KT, 2 * FI], F16)
        dn_hi = sb2("dn_hi", [P, FT, DM], F16)
        dn_lo = sb2("dn_lo", [P, FT, DM], F16)
        xa = sb2("xa", [P, TT, DM])
        xt_hi = sb2("xt_hi", [P, KT, L], F16)
        xt_lo = sb2("xt_lo", [P, KT, L], F16)
        h_hi = sb2("h_hi", [P, FT, L], F16)
        h_lo = sb2("h_lo", [P, FT, L], F16)
        sg = sb2("sg", [P, 2, L])
        hf = sb2("hf", [P, 2, L])
        xr = sb2("xr", [P, 2, DM])
        junk = sb2("junk", [P, DM])
        ss2 = sb2("ss2", [P, 2])
        ms2 = sb2("ms2", [P, 2])
        ri2 = sb2("ri2", [P, 2])
        rk2 = sb2("rk2", [P, 2])
        bn2 = sb2("bn2", [P, 2, 6])
        mv2 = sb2("mv2", [P, 2, 2])
        rs2 = sb2("rs2", [P, 2])
        p2.close()

        def bank(name):
            return ctx.enter_context(nc.psum_tensor(name, [P, 512], F32))

        ps_in = [bank("ps_in0"), bank("ps_in1")]
        ps_d = [bank("ps_d0"), bank("ps_d1")]
        ps_t, ps_s, ps_yd, ps_yo = bank("ps_t"), bank("ps_s"), bank("ps_yd"), bank("ps_yo")

        const_in = sem("const_in")
        passed = sem("passed")
        w_in_in = sem("w_in_in")
        u_in = sem("u_in")
        res_in = [sem("res_in0"), sem("res_in1")]
        rq_in = [sem("rq_in0"), sem("rq_in1")]
        csp_in = sem("csp_in")
        parts_out = sem("parts_out")
        x1_out = [sem("x1_out0"), sem("x1_out1")]
        fw_in = [sem("fw_in0"), sem("fw_in1")]
        fw_out = [sem("fw_out0"), sem("fw_out1")]
        fw_chain = sem("fw_chain")
        fw_done = sem("fw_done")
        pro_dve = sem("pro_dve")
        pro_act = sem("pro_act")
        pro_pool = sem("pro_pool")
        u_max = sem("u_max")
        u_all = sem("u_all")
        u_scale = sem("u_scale")
        u_hi_done = sem("u_hi_done")
        u_lo_done = sem("u_lo_done")
        in_full = [sem("in_full0"), sem("in_full1")]
        q3_full = sem("q3_full")
        q3_free = sem("q3_free")
        in_free = [sem("in_free0"), sem("in_free1")]
        tap3 = sem("tap3")
        conv_chain = sem("conv_chain")
        silu_done = sem("silu_done")
        dt_act = sem("dt_act")
        dt_dve = sem("dt_dve")
        t_full = sem("t_full")
        t_free = sem("t_free")
        d_full = sem("d_full")
        e_done = sem("e_done")
        m_done = sem("m_done")
        xe_done = sem("xe_done")
        yd_done = sem("yd_done")
        yo_full = sem("yo_full")
        s_full = sem("s_full")
        s_add = sem("s_add")
        sd_done = sem("sd_done")
        xd_done = sem("xd_done")
        y1_done = sem("y1_done")
        y2_done = sem("y2_done")
        y_done = sem("y_done")
        gate_done = sem("gate_done")
        sq_done = sem("sq_done")
        sum_chain = sem("sum_chain")
        rinv_done = sem("rinv_done")
        ln_chain = sem("ln_chain")
        rstd_done = sem("rstd_done")
        x1_done = sem("x1_done")

        gw_in = sem("gw_in")
        xa_in = sem("xa_in")
        xr_in = [sem("xr_in0"), sem("xr_in1")]
        tr_full = sem("tr_full")
        xh_done = sem("xh_done")
        xl_done = sem("xl_done")
        g_full = sem("g_full")
        up_full = sem("up_full")
        sg_done = sem("sg_done")
        hf_done = sem("hf_done")
        hh_done = sem("hh_done")
        hl_done = sem("hl_done")
        dn_full = sem("dn_full")
        ss_done = sem("ss_done")
        ms_done = sem("ms_done")
        ri_done = sem("ri_done")
        o_chain = sem("o_chain")
        rs_done = sem("rs_done")
        o_done = sem("o_done")
        out_out = [sem("out_out0"), sem("out_out1")]

        N_CONST = 16 * 17
        SLICE_G, SLICE_D = 2 * FI // NB, DM // NB
        assert SLICE_G == DEC and FT * SLICE_D == 2 * DEC
        fw_units = [("g", i) for i in range(KT)] + [("d", i) for i in range(2)]
        DECODE_AT = {"body": {21: [(0, 0), (0, 1)], 25: [(0, 2), (0, 3)], 27: [(1, 0), (1, 1)], 29: [(1, 2), (1, 3)]},
                     "last": {n: [(n // 4, n % 4)] for n in range(24)}}
        DECODE_LATE = {"body": [2, 3, 4, 5], "last": []}

        ps_g, ps_u, ps_t2, ps_n = ps_in, ps_d, [ps_t, ps_s], [ps_yd, ps_yo]

        block = ctx.enter_context(nc.Block())

        def settled(eng):
            eng.sem_inc(passed, 1)

        @block.sync
        def _(sp):
            def load_u(b, wait):
                if wait:
                    need(sp, u_hi_done, b * KT)
                    settled(sp)
                    need(sp, u_lo_done, b * KT)
                    settled(sp)
                    need(sp, u_max, b)
                    settled(sp)
                sp.dma_start(u32[:, :, :], u_t.rearrange("(k p) t -> p k t", p=P)[:, :, bass.ds(b * L, L)])\
                  .then_inc(u_in, 16)

            def store_parts(b):
                sp.wait_ge(dt_dve, (b + 1) * DT_STEPS)
                settled(sp)
                for half_ in range(2):
                    t, row = slice(half_ * LH, (half_ + 1) * LH), half_ * NH
                    sp.dma_start(cs_dram[b].rearrange("(r q) t -> q r t", r=3)[:, :, t], cs_parts[row:row + NH, :, :])\
                      .then_inc(parts_out, 16)
                    for h2 in range(2):
                        sp.dma_start(ld_dram[b, :, :, h2, t].rearrange("r q t -> q r t"),
                                     ld_parts[row + h2 * NP:row + (h2 + 1) * NP, :, :]).then_inc(parts_out, 16)

            def load_cs(b):
                sp.wait_ge(parts_out, (b + 1) * 96)
                settled(sp)
                need(sp, t_full, b * 32)
                settled(sp)
                sp.dma_start(cs12[:, :], cs_dram[b, 0:2 * NH, :]).then_inc(csp_in, 16)
                sp.dma_start(cs3[:, :], cs_dram[b, 2 * NH:3 * NH, :]).then_inc(csp_in, 16)

            def load_rows(b, c):
                need(sp, d_full, b * SLOTS + NG * (c - 1))
                settled(sp)
                t = slice(c * CH, (c + 1) * CH)
                sp.dma_start(rhs_d[0:6, c % 2, :, :], cs_dram[b].rearrange("(r q) t -> r q t", q=NP)[:, :, t])\
                  .then_inc(rq_in[c % 2], 16)
                sp.dma_start(lhs_d[6:30, c % 2, :, :].rearrange("r g (h s) -> r (g h) s", h=2),
                             ld_dram[b].rearrange("r (q g) h t -> (r q) (g h) t", g=NG)[:, :, t])\
                  .then_inc(rq_in[c % 2], 16)

            def load_res(b, tt):
                need(sp, x1_out[tt % 2], b * 32 + 16 * (tt // 2))
                settled(sp)
                sp.dma_start(res[:, tt % 2, :], u_tok[bass.ds(b * L + tt * P, P), :]).then_inc(res_in[tt % 2], 16)

            def store_x1(b, tt):
                sp.wait_ge(x1_done, b * TT + tt + 1)
                settled(sp)
                sp.dma_start(x1_dram[bass.ds(b * L + tt * P, P), :], res[:, tt % 2, :]).then_inc(x1_out[tt % 2], 16)

            def load_fw(b, k):
                kind, i = fw_units[k]
                need(sp, fw_done, b * 6 + k - 1)
                settled(sp)
                words, scales = fw_words[:, k % 2, :], fw_scale[:, k % 2, :]
                if kind == "g":
                    cols = bass.ds(b * SLICE_G, DEC)
                    loads = (words, gu_words[:, cols]), (scales, gu_scales[:, cols])
                else:
                    cols = bass.ds(b * SLICE_D + i * (SLICE_D // 2), SLICE_D // 2)
                    loads = [(dst.rearrange("p (g n) -> p g n", g=FT), src[:, :, cols])
                             for dst, src in ((words, dn_words), (scales, dn_scales))]
                for dst, src in loads:
                    sp.dma_start(dst, src).then_inc(fw_in[k % 2], 16)

            def store_fw(b, k):
                kind, i = fw_units[k]
                sp.wait_ge(fw_done, b * 6 + k + 1)
                settled(sp)
                for part, w in enumerate((fw_hi, fw_lo)):
                    if kind == "g":
                        sp.dma_start(gu_dram[part, i][:, bass.ds(b * SLICE_G, DEC)], w[:, k % 2, :]).then_inc(fw_out[k % 2], 16)
                    else:
                        cols = bass.ds(b * SLICE_D + i * (SLICE_D // 2), SLICE_D // 2)
                        sp.dma_start(dn_dram[part][:, :, cols], w[:, k % 2, :].rearrange("p (g n) -> p g n", g=FT)).then_inc(fw_out[k % 2], 16)

            def next_fw(b, k):
                if k + 2 < len(fw_units):
                    load_fw(b, k + 2)
                store_fw(b, k)

            def load_head(b):
                load_cs(b)
                load_rows(b, 0)
                load_rows(b, 1)

            def body(st):
                b = st.scan
                load_res(b, 0)
                load_res(b, 1)
                load_fw(b, 0)
                load_fw(b, 1)
                for n in range(SLOTS):
                    c = n // NG + 2
                    if n == 8 and st.proj is not None:
                        load_u(b + 2, True)
                    if n % NG == 1 and c < NC:
                        load_rows(b, c)
                    if n == 25 and st.proj is not None:
                        store_parts(b + 1)
                    if n == 30 and st.proj is not None:
                        load_head(b + 1)
                    for k, part in DECODE_AT[st.kind].get(n, []):
                        if part == 3:
                            next_fw(b, k)
                    for tt in range(2):
                        if f"o{tt}" in st.at(n):
                            store_x1(b, tt)
                            load_res(b, tt + 2)
                    if "o2" in st.at(n):
                        store_x1(b, 2)
                store_x1(b, 3)
                for k in DECODE_LATE[st.kind]:
                    next_fw(b, k)

            load_u(0, False)
            for k in range(KT):
                sp.dma_start(w_src[k], w_in_t[k * P:(k + 1) * P, :]).then_inc(w_in_in, 16)
            consts = [(cw[:, :, :], conv_w), (cb[:, :], conv_b), (dtbias[:, :], dt_bias), (aneg[:, :], a_log),
                      (dskip[:, :], d_skip), (normw[:, :], norm_w), (sel[:, :, :], c_sel),
                      (sel_dec[:, :, :], c_dec), (ident[:, :], c_ident), (mask[:, :], c_mask), (shift[:, :], c_shift),
                      (w_out[:, :, :], w_out_t.rearrange("(k p) n -> p k n", p=P))]
            consts += [(rhs_d[6:94, i, :, :], c_rhs) for i in range(2)]
            consts += [(lhs_d[:94, i, :, :], c_lhs) for i in range(2)]
            for dst, src in consts:
                if src.dtype == U16:
                    src = src.bitcast(BF16)
                sp.dma_start(dst, src).then_inc(const_in, 16)
            sp.dma_start(scales_once[:, :], all_scales).then_inc(const_in, 16)
            load_u(1, True)
            sp.wait_ge(const_in, N_CONST)
            store_parts(0)
            load_head(0)
            body(Stage("body", 0))
            with sp.Fori(1, nb - 1) as i:
                body(Stage("body", i))
            body(Stage("last", nb - 1))

            for k in range(2):
                sp.wait_ge(fw_out[k], nb * 3 * 32)
                sp.wait_ge(x1_out[k], nb * 32)
            for part, w in enumerate((gu_hi, gu_lo)):
                sp.dma_start(w[:, :, :], gu_dram[part].rearrange("k p n -> p k n")).then_inc(gw_in, 16)

            def load_xa(f):
                need(sp, tr_full, f * KT)
                settled(sp)
                sp.dma_start(xa[:, :, :], x1_dram[bass.ds(f * L, L), :].rearrange("(t p) n -> p t n", p=P)).then_inc(xa_in, 16)

            load_xa(0)
            for part, w in enumerate((dn_hi, dn_lo)):
                sp.dma_start(w[:, :, :], dn_dram[part]).then_inc(gw_in, 16)

            def load_xr(f, tt):
                need(sp, out_out[tt % 2], f * 32 + 16 * (tt // 2))
                settled(sp)
                sp.dma_start(xr[:, tt % 2, :], x1_dram[bass.ds(f * L + tt * P, P), :]).then_inc(xr_in[tt % 2], 16)

            def ffn(f, last):
                load_xr(f, 0)
                load_xr(f, 1)
                if not last:
                    load_xa(f + 1)
                for tt in range(TT):
                    sp.wait_ge(o_done, f * TT + tt + 1)
                    settled(sp)
                    sp.dma_start(out[bass.ds(f * L + tt * P, P), :], xr[:, tt % 2, :]).then_inc(out_out[tt % 2], 16)
                    if tt < 2:
                        load_xr(f, tt + 2)

            ffn(0, False)
            with sp.Fori(1, nb - 1) as f:
                ffn(f, False)
            ffn(nb - 1, True)
            for k in range(2):
                sp.wait_ge(out_out[k], nb * 32)

        @block.tensor
        def _(pe):
            mm, tr = nc.tensor.matmul, nc.tensor.transpose

            def project(st, name):
                bk, free, _ = st.bank(name)
                if name == "dt":
                    pe.wait_ge(u_hi_done, (st.proj + 1) * KT)
                    pe.wait_ge(u_lo_done, (st.proj + 1) * KT)
                need(pe, in_free[bk], free)
                col, m = IN_COL[name], (NH if name == "dt" else P)
                passes = [(w_hi, u_hi), (w_hi, u_lo), (w_lo, u_hi)]
                for k in range(KT):
                    for j, (w, u) in enumerate(passes):
                        last = mm(ps_in[bk][0:m, :], w[:, k, col:col + m], u[:, k, :],
                                  start=(k == 0 and j == 0), stop=(k == KT - 1 and j == 2))
                last.then_inc(in_full[bk], 1)

            def square_sum(st, tt):
                pe.wait_ge(sum_chain, (st.scan * NC + 2 * tt + 2) * 3)
                if tt == TT - 1:
                    pe.wait_ge(y1_done, (st.scan + 1) * 7)
                    mm(ps_yo[:, 0:1], ssum[:, tt * P:(tt + 1) * P], ones[:, :], start=True, stop=True).then_inc(q3_full, 1)
                    return
                bk, free, _ = st.bank(f"q{tt}")
                need(pe, in_free[bk], free)
                mm(ps_in[bk][:, 0:1], ssum[:, tt * P:(tt + 1) * P], ones[:, :], start=True, stop=True)\
                    .then_inc(in_full[bk], 1)

            def out_proj(st, tt):
                bk, free, _ = st.bank(f"o{tt}")
                pe.wait_ge(gate_done, st.scan * NC + 2 * tt + 2)
                need(pe, in_free[bk], free)
                for k in range(CT):
                    last = mm(ps_in[bk][:, :], zg[:, k, tt * P:(tt + 1) * P], w_out[:, k, :],
                              start=(k == 0), stop=(k == CT - 1))
                last.then_inc(in_full[bk], 1)

            def use(st, name):
                if name[0] == "q":
                    square_sum(st, int(name[1]))
                elif name[0] == "o":
                    out_proj(st, int(name[1]))
                else:
                    project(st, name)

            def use_in(st, slot):
                for name in st.at(slot):
                    use(st, name)

            def aux(b, c, at):
                use = AUX_ORDER[at]
                need(pe, t_free, b * 32 + c * 4 + at)
                t = slice(c * CH, (c + 1) * CH)
                if use < 2:
                    pe.wait_ge(silu_done, (b + 1) * 3)
                    settled(pe)
                    for k in range(4):
                        last = tr(ps_t[0:CH, k * P:(k + 1) * P], xs[:, 4 * use + k, t], ident[:, :])
                elif use == 2:
                    mm(ps_t[0:CH, 0:CH], bc[:, 0, t], bc[:, 1, t], start=True, stop=True)
                    tr(ps_t[0:CH, CH:CH + NS], bc[:, 0, t], ident[:, :])
                    pe.wait_ge(rq_in[c % 2], b * 128 + 32 * (c // 2 + 1))
                    for h2 in range(2):
                        last = mm(ps_t[:, CH + NS + h2 * NP:CH + NS + (h2 + 1) * NP], sel_dec[:, h2, :],
                                  rhs_d[0:6, c % 2, :, CH - 1], start=True, stop=True)
                else:
                    pe.wait_ge(csp_in, (b + 1) * 32)
                    for k in range(CT):
                        o = ps_t[:, k * CH:(k + 1) * CH]
                        mm(o, sel[:, k, :], cs12[:, t], start=True, stop=False)
                        last = mm(o, sel[0:NH, k, :], cs3[:, t], start=False, stop=True)
                last.then_inc(t_full, 1)

            def exponents(b, n):
                c, g = n // NG, n % NG
                if g == 0:
                    pe.wait_ge(rq_in[c % 2], b * 128 + 32 * (c // 2 + 1))
                need(pe, e_done, b * SLOTS + n - 1)
                mm(ps_d[n % 2][:, :].rearrange("p (k t) -> p k t", k=CT), lhs_d[0:94, c % 2, g, :],
                   rhs_d[0:94, c % 2, g:NP:NG, :], start=True, stop=True).then_inc(d_full, 1)

            def within(b, n):
                c, g = n // NG, n % NG
                pe.wait_ge(m_done, b * SLOTS + n + 1)
                if g == 0:
                    pe.wait_ge(t_free, b * 32 + c * 4 + 3)
                    need(pe, y_done, b * NC + c)
                for k in range(CT):
                    last = mm(ps_yd[g * 32:(g + 1) * 32, k * CH:(k + 1) * CH], xpad[:, c % 2, k * NG + g, :],
                              mix[:, g, k, :], start=True, stop=True, tile_position=(0, g * 32))
                last.then_inc(yd_done, 1)

            def from_before(b, c):
                pe.wait_ge(s_add, b * 14 + 2 * c)
                need(pe, y1_done, b * 7 + c - 1)
                for k in range(CT):
                    last = mm(ps_yo[:, k * CH:(k + 1) * CH], state[:, k * P:(k + 1) * P],
                              bc[:, 1, c * CH:(c + 1) * CH], start=True, stop=True)
                last.then_inc(yo_full, 1)

            def new_state(b, c):
                pe.wait_ge(xe_done, b * SLOTS + NG * c + NG)
                need(pe, s_add, b * 14 + 2 * c)
                need(pe, y1_done, b * 7 + c)
                if c == 0:
                    need(pe, q3_free, b)
                for h2, to in enumerate((ps_s, ps_yo)):
                    rows = slice(h2 * CH, (h2 + 1) * CH)
                    mm(to[:, :].rearrange("p (q d) -> p q d", d=HD), gb[rows, c % 2, CH:CH + NS], xend[rows, :, h2 * HD:(h2 + 1) * HD],
                       start=True, stop=True).then_inc(s_full, 1)

            def body(st):
                b = st.scan
                for n in range(SLOTS):
                    c, g = n // NG, n % NG
                    if n + 3 < SLOTS:
                        exponents(b, n + 3)
                    if c + 1 < NC:
                        aux(b, c + 1, g)
                    if g == 0 and c > 0:
                        new_state(b, c - 1)
                    use_in(st, n)
                    within(b, n)
                    if g == 1 and c > 0:
                        from_before(b, c)
                tail(st)

            def tail(st):
                for name in st.tail:
                    if name[0] == "a":
                        aux(st.proj, 0, int(name[1]))
                    elif name[0] == "e":
                        exponents(st.proj, int(name[1]))
                    else:
                        use(st, name)

            pe.wait_ge(const_in, N_CONST)
            pe.wait_ge(pro_dve, PRO_DVE)
            pe.wait_ge(pro_act, PRO_ACT)
            pro = Stage("pro", 0)
            use_in(pro, 0)
            tail(pro)
            body(Stage("body", 0))
            with pe.Fori(1, nb - 1) as i:
                body(Stage("body", i))
            body(Stage("last", nb - 1))

            def turn(f):
                pe.wait_ge(xa_in, 16 * (f + 1))
                for i in range(KT):
                    need(pe, xl_done, f * KT + i - 1)
                    for t in range(TT):
                        last = tr(ps_t2[i % 2][:, t * P:(t + 1) * P], xa[:, t, i:DM:KT], ident[:, :])
                    last.then_inc(tr_full, 1)

            def gate_up(f):
                pe.wait_ge(xh_done, (f + 1) * KT)
                pe.wait_ge(xl_done, (f + 1) * KT)
                for m in range(FT):
                    for off, banks, full, used in ((0, ps_g, g_full, sg_done), (FI, ps_u, up_full, hf_done)):
                        need(pe, used, f * FT + m - 1)
                        col = off + m * P
                        for k in range(KT):
                            for j, (w, x) in enumerate(((gu_hi, xt_hi), (gu_hi, xt_lo), (gu_lo, xt_hi))):
                                last = mm(banks[m % 2][:, :], w[:, k, col:col + P], x[:, k, :],
                                          start=(k == 0 and j == 0), stop=(k == KT - 1 and j == 2))
                        last.then_inc(full, 1)

            def down(f):
                for tt in range(TT):
                    need(pe, o_chain, (f * TT + tt - 1) * 5 - 3)
                    t = slice(tt * P, (tt + 1) * P)
                    for k in range(FT):
                        if tt == 0:
                            pe.wait_ge(hh_done, f * FT + k + 1)
                            pe.wait_ge(hl_done, f * FT + k + 1)
                        for j, (h, w) in enumerate(((h_hi, dn_hi), (h_hi, dn_lo), (h_lo, dn_hi))):
                            last = mm(ps_n[tt % 2][:, :], h[:, k, t], w[:, k, :],
                                      start=(k == 0 and j == 0), stop=(k == FT - 1 and j == 2))
                    last.then_inc(dn_full, 1)

            def ffn(f, last):
                gate_up(f)
                if not last:
                    turn(f + 1)
                down(f)

            turn(0)
            pe.wait_ge(gw_in, 64)
            ffn(0, False)
            with pe.Fori(1, nb - 1) as f:
                ffn(f, False)
            ffn(nb - 1, True)

        @block.scalar
        def _(act):
            ac = nc.scalar.activation

            def split_hi(b, before, tiles):
                act.wait_ge(u_scale, (b + 1) * 5)
                if before is not None:
                    for bk, count in before.last_z():
                        act.wait_ge(in_full[bk], count)
                for k in tiles:
                    ac(u_hi[:, k, :], u32[:, k, :], ACT.Identity, scale=uscale[:, 0:1]).then_inc(u_hi_done, 1)

            def take_dt(st):
                bk, _, full = st.bank("dt")
                act.wait_ge(in_full[bk], full)
                need(act, dt_dve, st.proj * DT_STEPS)
                for h in range(2):
                    last = ac(dta[h * NH:(h + 1) * NH, :], ps_in[bk][0:NH, h * LH:(h + 1) * LH], ACT.Identity,
                              bias=dtbias[:, 0:1], scale=uundo[0:NH, 0:1])
                last.then_inc(in_free[bk], 1)

            def exp_dt(b):
                act.wait_ge(dt_dve, b * DT_STEPS + 1)
                ac(dtb[:, :], dtb[:, :], ACT.Exp).then_inc(dt_act, 1)

            def ln_dt(b):
                act.wait_ge(dt_dve, b * DT_STEPS + 15)
                ac(dtc[:, :], dta[:, :], ACT.Ln).then_inc(dt_act, 1)

            def take_conv(st, name):
                m = CONV_TILES.index(name)
                bk, _, full = st.bank(name)
                act.wait_ge(in_full[bk], full)
                need(act, silu_done, st.proj * 3)
                ac(pre[:, m, :], ps_in[bk][:, :], ACT.Identity, bias=cb[:, m:m + 1], scale=cws[:, m, 3:4])\
                    .then_inc(tap3, 1)

            def silu_all(st):
                b = st.proj
                bk, _, count = st.bank(CONV_TILES[-1])
                act.wait_ge(in_free[bk], count)
                need(act, t_full, b * 32)
                need(act, yo_full, b * 7)
                need(act, xd_done, b * NC)
                ac(bc[:, :, :], pre[:, 0:2, :], ACT.Silu).then_inc(silu_done, 1)
                for h in range(2):
                    ac(xs[:, 4 * h:4 * h + 4, :], pre[:, 2 + 4 * h:6 + 4 * h, :], ACT.Silu).then_inc(silu_done, 1)

            def take_z(st, name):
                bk, _, full = st.bank(name)
                act.wait_ge(in_full[bk], full)
                if st.kind == "body" and name == "z0":
                    ob, _, ofull = st.bank("o3")
                    act.wait_ge(in_full[ob], ofull)
                    act.wait_ge(sq_done, (st.scan + 1) * NC)
                ac(zg[:, int(name[1]), :], ps_in[bk][:, :], ACT.Silu, scale=uundo[:, 0:1]).then_inc(in_free[bk], 1)

            def use_in(st, slot):
                for name in st.at(slot):
                    if name == "dt":
                        take_dt(st)
                    elif name in CONV_TILES:
                        take_conv(st, name)

            def aux(b, c, at):
                use = AUX_ORDER[at]
                act.wait_ge(t_full, b * 32 + c * 4 + at + 1)
                if use < 2:
                    if use == 0:
                        need(act, yd_done, b * SLOTS + NG * (c - 1))
                        need(act, xe_done, b * SLOTS + NG * (c - 1))
                    for h2 in range(2):
                        rows = slice(h2 * CH, (h2 + 1) * CH)
                        src = ps_t[0:CH, :].rearrange("p (q h d) -> p q h d", h=2, d=HD)[:, :, h2, :]
                        last = ac(xpad[rows, c % 2, 16 * use:16 * use + 16, h2 * HD:(h2 + 1) * HD], src, ACT.Copy)
                elif use == 2:
                    need(act, m_done, b * SLOTS + NG * (c - 1))
                    need(act, s_full, b * 14 + 2 * max(c - 1, 0))
                    need(act, sd_done, b * 6 + min(max(c - 2, 0), 6))
                    for h2 in range(2):
                        ac(gb[h2 * CH:(h2 + 1) * CH, c % 2, :], ps_t[0:CH, 0:CH + NS], ACT.Copy)
                    last = ac(dec[:, c % 2, :, :].rearrange("p q h -> p h q"),
                              ps_t[:, CH + NS:CH + NS + 2 * NP].rearrange("p (h q) -> p h q", h=2), ACT.Exp)
                else:
                    need(act, y1_done, b * 7 + max(c - 2, 0))
                    last = ac(ebc[:, c % 2, :, :].rearrange("p a b -> p (a b)"), ps_t[:, :], ACT.Exp)
                last.then_inc(t_free, 1)

            def square(b, c):
                act.wait_ge(gate_done, b * NC + c + 1)
                need(act, sum_chain, (b * NC + c) * 3)
                ac(sq[:, :, :], zg[:, :, c * CH:(c + 1) * CH], ACT.Square).then_inc(sq_done, 1)

            def exp_group(b, n):
                act.wait_ge(d_full, b * SLOTS + n + 1)
                need(act, m_done, b * SLOTS + n - 3)
                need(act, xe_done, b * SLOTS + n - 3)
                ac(decay[:, n % NG, :, :].rearrange("p a b -> p (a b)"), ps_d[n % 2][:, :], ACT.Exp).then_inc(e_done, 1)

            def body(st):
                b = st.scan
                for n in range(SLOTS):
                    c, g = n // NG, n % NG
                    if n in SPLIT_SLOT and st.proj is not None:
                        split_hi(st.proj, st.before(), SPLIT_SLOT[n])
                    if n + 3 < SLOTS:
                        exp_group(b, n + 3)
                    if c + 1 < NC:
                        aux(b, c + 1, g)
                    if g == 2 and c > 0:
                        square(b, c - 1)
                    use_in(st, n)
                    if st.proj is not None and n == 7:
                        exp_dt(st.proj)
                    if st.proj is not None and n == 20:
                        ln_dt(st.proj)
                tail(st)

            def tail(st):
                if st.kind == "last":
                    square(st.scan, NC - 1)
                order = list(st.tail)
                if "z3" in order:
                    order.remove("z3")
                    order.insert(order.index("z4"), "z3")
                for name in order:
                    if name in CONV_TILES:
                        take_conv(st, name)
                        if st.kind == "body":
                            square(st.scan, NC - 1)
                        silu_all(st)
                    elif name[0] == "a":
                        aux(st.proj, 0, int(name[1]))
                    elif name[0] == "e":
                        exp_group(st.proj, int(name[1]))
                    elif name[0] == "z":
                        take_z(st, name)

            act.wait_ge(const_in, N_CONST)
            act.wait_ge(pro_pool, 1)
            ac(aneg[:, :], aneg[:, :], ACT.Exp).then_inc(pro_act, 1)
            act.wait_ge(pro_dve, W_SCALED)
            for k in range(KT):
                ac(w_hi[:, k, :], w_src[k], ACT.Identity, scale=w_in_scale).then_inc(pro_act, 1)
            split_hi(0, None, range(KT))
            pro = Stage("pro", 0)
            take_dt(pro)
            exp_dt(0)
            act.wait_ge(pro_dve, PRO_DVE)
            take_conv(pro, "B")
            take_conv(pro, "C")
            ln_dt(0)
            for i in range(CT - 1):
                take_conv(pro, f"x{i}")
            tail(pro)
            body(Stage("body", 0))
            with act.Fori(1, nb - 1) as i:
                body(Stage("body", i))
            body(Stage("last", nb - 1))

            def turn(f):
                for i in range(KT):
                    act.wait_ge(tr_full, f * KT + i + 1)
                    if i == 0:
                        need(act, up_full, f * FT)
                    ac(xt_hi[:, i, :], ps_t2[i % 2][:, :], ACT.Copy, scale=1024.0).then_inc(xh_done, 1)

            def hidden(f):
                for m in range(FT + 1):
                    if m < FT:
                        act.wait_ge(g_full, f * FT + m + 1)
                        need(act, hf_done, f * FT + m - 1)
                        ac(sg[:, m % 2, :], ps_g[m % 2][:, :], ACT.Silu, scale=gate_undo).then_inc(sg_done, 1)
                    if m >= 1:
                        act.wait_ge(hf_done, f * FT + m)
                        if m == 1:
                            need(act, dn_full, f * TT)
                        ac(h_hi[:, m - 1, :], hf[:, (m - 1) % 2, :], ACT.Copy).then_inc(hh_done, 1)

            def squares(f):
                for tt in range(TT):
                    act.wait_ge(dn_full, f * TT + tt + 1)
                    need(act, ms_done, f * TT + tt - 1)
                    need(act, ss_done, f * TT + tt)
                    ac(junk[:, :], ps_n[tt % 2][:, :], ACT.Square, scale=down_undo,
                       accum_out=ss2[:, tt % 2:tt % 2 + 1]).then_inc(ss_done, 1)

            def ffn(f, last):
                hidden(f)
                if not last:
                    turn(f + 1)
                squares(f)

            turn(0)
            ffn(0, False)
            with act.Fori(1, nb - 1) as f:
                ffn(f, False)
            ffn(nb - 1, True)

        @block.vector
        def _(dve):
            v = nc.vector

            def measure_u(b):
                dve.wait_ge(u_in, (b + 1) * 16)
                need(dve, u_all, b)
                v.tensor_reduce(umax[:, :], u32[:, :, :], AX.XY, ALU.max, apply_absolute_value=True).then_inc(u_max, 1)

            def scale_u(b, before):
                ch = Chain(dve, u_scale, 5, b)
                dve.wait_ge(u_all, b + 1)
                if before is not None:
                    for bk, count in before.last_z():
                        dve.wait_ge(in_free[bk], count)
                ch.step(v.tensor_scalar(utmp[:, 0:1], umax_all[:, :], 1e-30, None, ALU.max))
                ch.step(v.tensor_scalar(utmp[:, 1:2].bitcast(I32), utmp[:, 0:1].bitcast(I32), 0x7F800000, None,
                                        ALU.bitwise_and))
                ch.step(v.reciprocal(utmp[:, 0:1], utmp[:, 1:2]))
                v.tensor_scalar(uscale[:, :], utmp[:, 0:1], 2.0 ** 14, None, ALU.mult)
                ch.step(v.tensor_scalar(uundo[:, :], utmp[:, 1:2], w_in_undo, 2.0 ** -14, ALU.mult, ALU.mult))
                ch.step(v.tensor_scalar(cws[:, :, :], cw[:, :, :], uundo[:, 0:1], None, ALU.mult))
                ch.end()

            def split_lo(b, tiles):
                for k in tiles:
                    dve.wait_ge(u_hi_done, b * KT + k + 1)
                    v.scalar_tensor_tensor(u_lo[:, k, :], u32[:, k, :], uscale[:, 0:1], u_hi[:, k, :],
                                           ALU.mult, ALU.subtract).then_inc(u_lo_done, 1)

            def taps(st, name):
                m = CONV_TILES.index(name)
                bk, _, _ = st.bank(name)
                at = st.proj * 20 + 2 * m
                dve.wait_ge(tap3, st.proj * 10 + m + 1)
                for j, k in enumerate((2, 1, 0)):
                    d = 3 - k
                    if j:
                        dve.wait_ge(conv_chain, at + j)
                    ins = v.scalar_tensor_tensor(pre[:, m, d:L], ps_in[bk][:, 0:L - d], cws[:, m, k:k + 1],
                                                 pre[:, m, d:L], ALU.mult, ALU.add)
                    ins.then_inc(conv_chain if j < 2 else in_free[bk], 1)

            def dt_first(st):
                bk, free, _ = st.bank("dt")
                dve.wait_ge(in_free[bk], free + 1)
                need(dve, dt_act, st.proj * 2)
                v.scalar_tensor_tensor(dtb[:, :], dta[:, :], -1.0, dta[:, :], ALU.mult, ALU.min).then_inc(dt_dve, 1)

            def dt_second(b, part):
                ch = Chain(dve, dt_dve, DT_STEPS, b)
                ch.k = DT_PART[part]
                if part == 0:
                    dve.wait_ge(dt_act, b * 2 + 1)
                    ch.step(v.tensor_scalar(dtc[:, :], dtb[:, :], 2.0, None, ALU.add))
                    ch.step(v.reciprocal(dtd[:, :], dtc[:, :]))
                elif part == 1:
                    ch.step(v.tensor_tensor(dtb[:, :], dtb[:, :], dtd[:, :], ALU.mult))
                    ch.step(v.tensor_tensor(dtc[:, :], dtb[:, :], dtb[:, :], ALU.mult))
                    ch.step(v.tensor_scalar(dtd[:, :], dtc[:, :], LOG1P[7], LOG1P[6], ALU.mult, ALU.add))
                    ch.step(v.tensor_tensor(dtd[:, :], dtd[:, :], dtc[:, :], ALU.mult))
                elif part == 2:
                    for k in range(5, 0, -1):
                        ch.step(v.scalar_tensor_tensor(dtd[:, :], dtd[:, :], LOG1P[k], dtc[:, :], ALU.add, ALU.mult))
                elif part == 3:
                    ch.step(v.scalar_tensor_tensor(dtd[:, :], dtd[:, :], LOG1P[0], dtb[:, :], ALU.add, ALU.mult))
                    ch.step(v.scalar_tensor_tensor(dtd[:, :], dta[:, :], 0.0, dtd[:, :], ALU.max, ALU.add))
                    ch.step(v.tensor_scalar(dta[:, :], dtd[:, :], 1e-18, None, ALU.max))
                    ch.step(v.tensor_scalar(dtb[:, :], dtd[:, :], aneg[:, 0:1], None, ALU.mult))
                else:
                    ch.step(v.tensor_tensor_scan(dte[:, :], mask[:, :], dtb[:, :], 0.0, ALU.mult, ALU.add))
                    need(dve, parts_out, b * 96)
                    ch.step(v.tensor_copy(cs_parts[:, 0, :], dte[:, :]))
                    ch.step(v.tensor_tensor(dtf[:, :], dte[:, :], cs_parts[:, 0, :], ALU.subtract))
                    ch.step(v.tensor_copy(cs_parts[:, 1, :], dtf[:, :]))
                    v.tensor_tensor(cs_parts[:, 2, :], dtf[:, :], cs_parts[:, 1, :], ALU.subtract)
                assert part == 4 or ch.k == DT_PART[part + 1]

            def dt_third(b):
                ch = Chain(dve, dt_dve, DT_STEPS, b)
                ch.k = 20
                dve.wait_ge(dt_act, b * 2 + 2)
                ch.step(v.tensor_tensor(dtc[:, :], dtc[:, :], dte[:, :], ALU.subtract))
                ch.step(v.tensor_copy(ld_parts[:, 0, :], dtc[:, :]))
                ch.step(v.tensor_tensor(dtf[:, :], dtc[:, :], ld_parts[:, 0, :], ALU.subtract))
                ch.step(v.tensor_copy(ld_parts[:, 1, :], dtf[:, :]))
                ch.step(v.tensor_tensor(ld_parts[:, 2, :], dtf[:, :], ld_parts[:, 1, :], ALU.subtract))
                ch.end()

            def decode(b, k, part):
                kind, i = fw_units[k]
                words = fw_words[:, k % 2, :]
                ch = Chain(dve, fw_chain, 36, b)
                ch.k = 6 * k + (0, 1, 4, 5)[part]
                if part == 0:
                    dve.wait_ge(fw_in[k % 2], (b * 3 + k // 2 + 1) * 32)
                    col = 0 if kind == "g" else 1
                    ch.step(v.tensor_scalar(words, words, shift[:, col:col + 1], None,
                                            ALU.logical_shift_right))
                elif part == 1:
                    at = 4 * i if kind == "g" else 0
                    for dst, top, bits in ((fw_mag, 9, 0x0E00), (fw_sign, 12, 0x8000)):
                        by = top - at
                        op = ALU.logical_shift_left if by >= 0 else ALU.logical_shift_right
                        ch.step(v.tensor_scalar(dst[:, :], words, abs(by), bits, op, ALU.bitwise_and))
                    ch.step(v.tensor_tensor(fw_mag[:, :], fw_mag[:, :], fw_sign[:, :], ALU.bitwise_or))
                elif part == 2:
                    ch.step(v.scalar_tensor_tensor(fw_w[:, :], fw_mag[:, :].bitcast(F16)[:, 0:2 * DEC:2],
                                                   gu_in_scale if kind == "g" else dn_in_scale, fw_scale[:, k % 2, :],
                                                   ALU.mult, ALU.mult))
                else:
                    need(dve, fw_out[k % 2], (b * 3 + k // 2) * 32)
                    ch.step(v.tensor_copy(fw_hi[:, k % 2, :], fw_w[:, :]))
                    v.tensor_tensor(fw_lo[:, k % 2, :], fw_w[:, :], fw_hi[:, k % 2, :], ALU.subtract).then_inc(fw_done, 1)

            def mixing(b, n):
                c = n // NG
                dve.wait_ge(e_done, b * SLOTS + n + 1)
                if n % NG == 0:
                    dve.wait_ge(t_free, b * 32 + c * 4 + 2)
                need(dve, yd_done, b * SLOTS + n - 3)
                v.tensor_tensor(mix[:, n % NG, :, :], decay[:, n % NG, :, :],
                                gb[:, c % 2, 0:CH].unsqueeze(1).broadcast_to([P, CT, CH]), ALU.mult).then_inc(m_done, 1)

            def add_state(b, c, h2):
                def part(ap):
                    return ap.rearrange("p (q h d) -> p q h d", h=2, d=HD)[:, :, h2, :]

                new = (ps_s, ps_yo)[h2][:, :].rearrange("p (q d) -> p q d", d=HD)
                dve.wait_ge(s_full, b * 14 + 2 * c + h2 + 1)
                if c == 0:
                    need(dve, yo_full, b * 7)
                    v.tensor_copy(part(state[:, :]), new).then_inc(s_add, 1)
                else:
                    dve.wait_ge(sd_done, b * 6 + c)
                    dve.wait_ge(yo_full, b * 7 + c)
                    v.tensor_tensor(part(state[:, :]), new, part(state_d[:, :]), ALU.add).then_inc(s_add, 1)

            def flat(ap):
                return ap.rearrange("p a b -> p (a b)")

            def y_before(b, c):
                if c > 0:
                    dve.wait_ge(yo_full, b * 7 + c)
                    dve.wait_ge(t_free, b * 32 + c * 4 + 4)
                    need(dve, y2_done, b * 7 + c - 1)
                    v.tensor_tensor(flat(yoff[:, :, :]), ps_yo[:, :], flat(ebc[:, c % 2, :, :]), ALU.mult).then_inc(y1_done, 1)
                    dve.wait_ge(y1_done, b * 7 + c)
                    dve.wait_ge(xd_done, b * NC + c + 1)
                    v.tensor_tensor(y[:, c % 2, :, :], y[:, c % 2, :, :], yoff[:, :, :], ALU.add).then_inc(y2_done, 1)

            def y_all(b, c):
                dve.wait_ge(yd_done, b * SLOTS + NG * (c + 1))
                dve.wait_ge(xd_done, b * NC + c + 1)
                need(dve, y2_done, b * 7 + c)
                v.tensor_tensor(flat(y[:, c % 2, :, :]), ps_yd[:, :], flat(y[:, c % 2, :, :]), ALU.add).then_inc(y_done, 1)

            def mean_square(st, tt):
                if tt == TT - 1:
                    full, count, free, src = q3_full, st.scan + 1, q3_free, ps_yo
                else:
                    bk, _, count = st.bank(f"q{tt}")
                    full, free, src = in_full[bk], in_free[bk], ps_in[bk]
                dve.wait_ge(full, count)
                need(dve, rinv_done, st.scan * TT)
                v.tensor_scalar(msv[:, tt:tt + 1], src[:, 0:1], 1.0 / DI, 1e-5, ALU.mult, ALU.add).then_inc(free, 1)

            def norm_tile(st, tt):
                b = st.scan
                bk, _, full = st.bank(f"o{tt}")
                i = tt % 2
                ch = Chain(dve, ln_chain, 12, b)
                ch.k = 3 * tt
                dve.wait_ge(in_full[bk], full)
                dve.wait_ge(rinv_done, b * TT + tt + 1)
                dve.wait_ge(res_in[i], b * 32 + 16 * (tt // 2) + 16)
                v.scalar_tensor_tensor(res[:, i, :], ps_in[bk][:, :], rinv[:, tt:tt + 1], res[:, i, :],
                                       ALU.mult, ALU.add).then_inc(in_free[bk], 1)
                dve.wait_ge(in_free[bk], full)
                ch.step(v.bn_stats(bn[:, i, :], res[:, i, :]), settled)
                ch.step(v.bn_aggr(mv[:, i, :], bn[:, i, :]))
                v.tensor_scalar(mv[:, i, 1:2], mv[:, i, 1:2], 1e-5, None, ALU.add).then_inc(ln_chain, 1)

            def norm_tile_end(st, tt):
                b, i = st.scan, tt % 2
                dve.wait_ge(rstd_done, b * TT + tt + 1)
                v.tensor_scalar(res[:, i, :], res[:, i, :], mv[:, i, 0:1], rstd[:, i:i + 1],
                                ALU.subtract, ALU.mult).then_inc(x1_done, 1)

            def use_in(st, slot):
                for name in st.at(slot):
                    if name in CONV_TILES:
                        taps(st, name)
                    elif name[0] == "q":
                        mean_square(st, int(name[1]))
                    elif name[0] == "o":
                        if int(name[1]) == TT - 1:
                            mean_square(st, TT - 1)
                        norm_tile(st, int(name[1]))

            def body(st):
                b = st.scan
                mixing(b, 0)
                mixing(b, 1)
                for n in range(SLOTS):
                    c, g = n // NG, n % NG
                    if n == 0 and st.proj is not None:
                        scale_u(st.proj, st.before())
                    if g == 0 and c > 0:
                        y_all(b, c - 1)
                    if n + 2 < SLOTS:
                        mixing(b, n + 2)
                    if g == 0 and c > 0:
                        add_state(b, c - 1, 0)
                        add_state(b, c - 1, 1)
                    if n in SPLIT_SLOT and st.proj is not None:
                        split_lo(st.proj, SPLIT_SLOT[n])
                    if g == 2:
                        y_before(b, c)
                    if n > 0:
                        use_in(st, n - 1)
                    for tt in range(TT - 2):
                        if f"o{tt}" in st.at(n - 2):
                            norm_tile_end(st, tt)
                    if st.proj is not None:
                        if n == 6:
                            dt_first(st)
                        if n in DT_SLOT:
                            dt_second(st.proj, DT_SLOT[n])
                        if n == 23:
                            dt_third(st.proj)
                    for k, part in DECODE_AT[st.kind].get(n, []):
                        decode(b, k, part)
                y_all(b, NC - 1)
                norm_tile_end(st, TT - 2)
                use_in(st, SLOTS - 1)
                use_in(st, SLOTS)
                if st.proj is not None:
                    measure_u(b + 2)
                norm_tile_end(st, TT - 1)
                for k in DECODE_LATE[st.kind]:
                    for part in range(4):
                        decode(b, k, part)

            ch = Chain(dve, pro_dve, PRO_DVE, 0)
            v.memset(ones[:, :], 1.0)
            v.memset(half[:, :], -0.5)
            dve.wait_ge(const_in, N_CONST)
            measure_u(0)
            dve.wait_ge(w_in_in, KT * 16)
            for j, src in enumerate(w_src):
                v.tensor_reduce(wmax[:, j:j + 1], src, AX.X, ALU.max, apply_absolute_value=True)
            v.tensor_reduce(maxes[:, 1:2], scales_once[:, 0:GU_SCALES], AX.X, ALU.max)
            ch.step(v.tensor_reduce(maxes[:, 2:3], scales_once[:, GU_SCALES:ALL_SCALES], AX.X, ALU.max))
            ch.step(v.tensor_reduce(maxes[:, 0:1], wmax[:, :], AX.X, ALU.max))
            assert ch.k == MAXES_READY
            dve.wait_ge(pro_pool, 2)
            ch.step(v.tensor_scalar(maxes[:, :], maxes_all[:, :], 1e-30, None, ALU.max))
            ch.step(v.tensor_scalar(pow2[:, :].bitcast(I32), maxes[:, :].bitcast(I32), 0x7F800000, None, ALU.bitwise_and))
            ch.step(v.reciprocal(inv2[:, :], pow2[:, :]))
            v.tensor_scalar(w_in_scale, inv2[:, 0:1], 2.0 ** 14, None, ALU.mult)
            v.tensor_scalar(w_in_undo, pow2[:, 0:1], 2.0 ** -14, None, ALU.mult)
            v.tensor_scalar(gu_in_scale, inv2[:, 1:2], 2.0 ** 25, None, ALU.mult)
            v.tensor_scalar(dn_in_scale, inv2[:, 2:3], 2.0 ** 25, None, ALU.mult)
            v.tensor_scalar(gate_undo, pow2[:, 1:2], 2.0 ** -21, None, ALU.mult)
            v.tensor_scalar(up_undo, inv2[:, 1:2], 2.0 ** -31, None, ALU.mult)
            ch.step(v.tensor_scalar(scratch1, pow2[:, 1:2], pow2[:, 1:2], 0.5, ALU.mult, ALU.mult))
            assert ch.k == W_SCALED
            v.tensor_scalar(down_undo, scratch1, pow2[:, 2:3], None, ALU.mult)
            dve.wait_ge(pro_act, 1)
            v.tensor_scalar(aneg[:, :], aneg[:, :], -1.0, None, ALU.mult)
            for k in range(CT):
                v.tensor_scalar(w_out[:, k, :], w_out[:, k, :], normw[:, k:k + 1], None, ALU.mult)
            for k in range(KT):
                dve.wait_ge(pro_act, 2 + k)
                ins = v.scalar_tensor_tensor(w_lo[:, k, :], w_src[k], w_in_scale, w_hi[:, k, :],
                                             ALU.mult, ALU.subtract)
            ch.step(ins)
            ch.end()
            scale_u(0, None)
            split_lo(0, range(KT))
            pro = Stage("pro", 0)
            dt_first(pro)
            for part in range(len(DT_PART)):
                dt_second(0, part)
            taps(pro, "B")
            taps(pro, "C")
            dt_third(0)
            for i in range(CT):
                taps(pro, f"x{i}")
            measure_u(1)
            body(Stage("body", 0))
            with dve.Fori(1, nb - 1) as i:
                body(Stage("body", i))
            body(Stage("last", nb - 1))

            def turn(f):
                for i in range(KT):
                    dve.wait_ge(xh_done, f * KT + i + 1)
                    v.scalar_tensor_tensor(xt_lo[:, i, :], ps_t2[i % 2][:, :], 1024.0, xt_hi[:, i, :],
                                           ALU.mult, ALU.subtract).then_inc(xl_done, 1)

            def hidden(f):
                for m in range(FT):
                    dve.wait_ge(up_full, f * FT + m + 1)
                    dve.wait_ge(sg_done, f * FT + m + 1)
                    need(dve, hh_done, f * FT + m - 1)
                    need(dve, hl_done, f * FT + m - 1)
                    v.scalar_tensor_tensor(hf[:, m % 2, :], ps_u[m % 2][:, :], up_undo, sg[:, m % 2, :],
                                           ALU.mult, ALU.mult).then_inc(hf_done, 1)

            def norms(f):
                for tt in range(TT):
                    i = tt % 2
                    ch = Chain(dve, o_chain, 20, f)
                    ch.k = 5 * tt
                    dve.wait_ge(ss_done, f * TT + tt + 1)
                    v.tensor_scalar(ms2[:, i:i + 1], ss2[:, i:i + 1], 1.0 / DM, 1e-6, ALU.mult, ALU.add).then_inc(ms_done, 1)
                    dve.wait_ge(ri_done, f * TT + tt + 1)
                    ch.step(v.tensor_scalar(rk2[:, i:i + 1], ri2[:, i:i + 1], down_undo, None, ALU.mult))
                    dve.wait_ge(xr_in[i], f * 32 + 16 * (tt // 2) + 16)
                    ch.step(v.scalar_tensor_tensor(xr[:, i, :], ps_n[i][:, :], rk2[:, i:i + 1], xr[:, i, :],
                                                   ALU.mult, ALU.add))
                    ch.step(v.bn_stats(bn2[:, i, :], xr[:, i, :]), settled)
                    ch.step(v.bn_aggr(mv2[:, i, :], bn2[:, i, :]))
                    v.tensor_scalar(mv2[:, i, 1:2], mv2[:, i, 1:2], 1e-5, None, ALU.add).then_inc(o_chain, 1)
                    dve.wait_ge(rs_done, f * TT + tt + 1)
                    v.tensor_scalar(xr[:, i, :], xr[:, i, :], mv2[:, i, 0:1], rs2[:, i:i + 1],
                                    ALU.subtract, ALU.mult).then_inc(o_done, 1)

            def ffn(f, last):
                hidden(f)
                if not last:
                    turn(f + 1)
                norms(f)

            turn(0)
            ffn(0, False)
            with dve.Fori(1, nb - 1) as f:
                ffn(f, False)
            ffn(nb - 1, True)

        @block.gpsimd
        def _(pool):
            g_ = nc.gpsimd

            def reduce_u(b):
                pool.wait_ge(u_max, b + 1)
                need(pool, u_scale, b * 5)
                settled(pool)
                g_.partition_all_reduce(umax_all[:, :], umax[:, :], P, RMAX).then_inc(u_all, 1)

            def to_end(b, n):
                c, g = n // NG, n % NG
                pool.wait_ge(e_done, b * SLOTS + n + 1)
                pool.wait_ge(t_free, b * 32 + c * 4 + 3)
                if g == 0:
                    need(pool, s_full, b * 14 + 2 * c)
                g_.tensor_tensor(xend[:, g:NP:NG, :], xpad[:, c % 2, g:NP:NG, :],
                                 decay[:, g, :, CH - 1:CH].broadcast_to([P, CT, 2 * HD]), ALU.mult).then_inc(xe_done, 1)

            def decay_state(b, c):
                pool.wait_ge(s_add, b * 14 + 2 * c)
                pool.wait_ge(t_free, b * 32 + c * 4 + 2)
                g_.tensor_tensor(state_d[:, :].rearrange("p (q d) -> p q d", d=HD),
                                 state[:, :].rearrange("p (q d) -> p q d", d=HD),
                                 dec[:, c % 2, :, :].rearrange("p q h -> p (q h)").unsqueeze(2).broadcast_to([P, NH, HD]),
                                 ALU.mult).then_inc(sd_done, 1)

            def skip_term(b, c):
                pool.wait_ge(silu_done, (b + 1) * 3)
                need(pool, gate_done, b * NC + c - 1)
                g_.tensor_tensor(y[:, c % 2, :, :], xs[:, :, c * CH:(c + 1) * CH],
                                 dskip[:, :].unsqueeze(2).broadcast_to([P, CT, CH]), ALU.mult).then_inc(xd_done, 1)

            def gate(st, c):
                b, t = st.scan, slice(c * CH, (c + 1) * CH)
                pool.wait_ge(y_done, b * NC + c + 1)
                if c == 0:
                    for bk, count in st.before().last_z():
                        pool.wait_ge(in_free[bk], count)
                g_.tensor_tensor(zg[:, :, t], y[:, c % 2, :, :], zg[:, :, t], ALU.mult).then_inc(gate_done, 1)

            def sum_squares(b, c):
                t = slice(c * CH, (c + 1) * CH)
                ch = Chain(pool, sum_chain, 3 * NC, b)
                ch.k = 3 * c
                pool.wait_ge(sq_done, b * NC + c + 1)
                ch.step(g_.tensor_tensor(sq[:, 0:4, :], sq[:, 0:4, :], sq[:, 4:8, :], ALU.add))
                ch.step(g_.tensor_tensor(sq[:, 0:2, :], sq[:, 0:2, :], sq[:, 2:4, :], ALU.add))
                ch.step(g_.tensor_tensor(ssum[:, t], sq[:, 0, :], sq[:, 1, :], ALU.add))

            def root(st, tt):
                if tt == TT - 1:
                    pool.wait_ge(q3_free, st.scan + 1)
                else:
                    bk, _, count = st.bank(f"q{tt}")
                    pool.wait_ge(in_free[bk], count)
                g_.tensor_tensor(rinv[:, tt:tt + 1], msv[:, tt:tt + 1], half[:, :], ALU.pow).then_inc(rinv_done, 1)

            def ln_root(b, tt):
                pool.wait_ge(ln_chain, b * 12 + 3 * tt + 3)
                g_.tensor_tensor(rstd[:, tt % 2:tt % 2 + 1], mv[:, tt % 2, 1:2], half[:, :], ALU.pow).then_inc(rstd_done, 1)

            def body(st):
                b = st.scan
                skip_term(b, 0)
                for n in range(SLOTS):
                    c, g = n // NG, n % NG
                    if g == 0:
                        to_end(b, n)
                    if g < NG - 1:
                        to_end(b, n + 1)
                    if g == 1 and c > 0:
                        gate(st, c - 1)
                    if g == 1 and 1 <= c < NC - 1:
                        decay_state(b, c)
                    if g == 2 and c + 1 < NC:
                        skip_term(b, c + 1)
                    if g == 3 and c > 0:
                        sum_squares(b, c - 1)
                    for tt in range(TT):
                        if n > 0 and f"q{tt}" in st.at(n - 1):
                            root(st, tt)
                        if n > 0 and f"o{tt}" in st.at(n - 1):
                            ln_root(b, tt)
                gate(st, NC - 1)
                sum_squares(b, NC - 1)
                root(st, TT - 1)
                ln_root(b, TT - 1)
                if st.proj is not None:
                    reduce_u(b + 2)

            g_.memset(xpad[:, :, :, :], 0.0).then_inc(pro_pool, 1)
            reduce_u(0)
            pool.wait_ge(pro_dve, MAXES_READY)
            g_.partition_all_reduce(maxes_all[:, :], maxes[:, :], P, RMAX).then_inc(pro_pool, 1)
            reduce_u(1)
            body(Stage("body", 0))
            with pool.Fori(1, nb - 1) as i:
                body(Stage("body", i))
            body(Stage("last", nb - 1))

            def hidden(f):
                for m in range(FT):
                    pool.wait_ge(hh_done, f * FT + m + 1)
                    if m == 0:
                        need(pool, dn_full, f * TT)
                    g_.tensor_tensor(h_lo[:, m, :], hf[:, m % 2, :], h_hi[:, m, :], ALU.subtract).then_inc(hl_done, 1)

            def roots(f):
                for tt in range(TT):
                    i = tt % 2
                    pool.wait_ge(ms_done, f * TT + tt + 1)
                    g_.tensor_tensor(ri2[:, i:i + 1], ms2[:, i:i + 1], half[:, :], ALU.pow).then_inc(ri_done, 1)
                    pool.wait_ge(o_chain, f * 20 + 5 * tt + 5)
                    g_.tensor_tensor(rs2[:, i:i + 1], mv2[:, i, 1:2], half[:, :], ALU.pow).then_inc(rs_done, 1)

            def ffn(f):
                hidden(f)
                roots(f)

            ffn(0)
            with pool.Fori(1, nb - 1) as f:
                ffn(f)
            ffn(nb - 1)


def kernel(L0_attn_u, L0_attn_in_proj_w, L0_attn_conv_w, L0_attn_conv_b, L0_attn_dt_bias, L0_attn_A_log,
           L0_attn_D, L0_attn_norm_weight, L0_attn_out_proj_w, L0_ffn_gate_up_packed, L0_ffn_gate_up_scales,
           L0_ffn_down_packed, L0_ffn_down_scales):
    import concourse.bacc as bacc
    from concourse.bass_utils import run_bass_kernel_spmd

    arrays = lay_out(*(np.asarray(a) for a in (
        L0_attn_u, L0_attn_in_proj_w, L0_attn_conv_w, L0_attn_conv_b, L0_attn_dt_bias, L0_attn_A_log, L0_attn_D,
        L0_attn_norm_weight, L0_attn_out_proj_w, L0_ffn_gate_up_packed, L0_ffn_gate_up_scales, L0_ffn_down_packed,
        L0_ffn_down_scales)))
    nc = bacc.Bacc("TRN2", target_bir_lowering=False, num_devices=1, dynamic_dma_scratch_size=1024)
    args = [nc.dram_tensor(n, a.shape, mybir.dt.from_np(a.dtype), kind="ExternalInput").ap() for n, a in arrays.items()]
    args.append(nc.dram_tensor("out", [NB * L, DM], F32, kind="ExternalOutput").ap())
    build(nc, *args)
    result = run_bass_kernel_spmd(nc, [arrays], core_ids=[0])
    return result.results[0]["out"].reshape(NB, L, DM)


def lay_out(u, w_in, conv_w, conv_b, dt_bias, a_log, d, norm_w, w_out, gu, gu_s, dn, dn_s):
    c = np.ascontiguousarray

    def bf16_bits(a):
        return (c(a, np.float32).view(np.uint32) >> 16).astype(np.uint16)

    h2, tile, g = np.meshgrid(range(2), range(CT), range(NG), indexing="ij")
    heads = (8 * tile + 2 * g + h2).ravel()
    zs, xb, ds = w_in[:DI], w_in[DI:2 * DI + 2 * NS], w_in[2 * DI + 2 * NS:]
    w_rows = np.concatenate([ds[heads], xb[DI:], xb[:DI], zs])
    order = np.concatenate([np.arange(DI, DI + 2 * NS), np.arange(DI)])
    tokens = u.reshape(NB * L, DM)
    sel = np.zeros((2, NH, CT, P), np.float32)
    for q, h in enumerate(heads):
        sel[:, q, h // 8, (h % 8) * HD:(h % 8 + 1) * HD] = 1
    rhs = np.zeros((24 + CH, NP, CH), np.float32)
    for r in range(3):
        for k in range(CT):
            rhs[8 * r + k, NG * k:NG * k + NG] = 1
    rhs[24:] = np.where(np.arange(CH)[None, None, :] < np.arange(CH)[:, None, None], NEG, 0)
    lhs = np.zeros((94, NG, 2, CH), np.float32)
    dec = np.zeros((6, 2, P), np.float32)
    for r in range(3):
        for h in range(2):
            lhs[2 * r + h, :, h] = 1
            dec[2 * r + h, h] = 1
    lhs[30:] = np.eye(CH)[:, None, None, :]
    mask = np.broadcast_to(np.arange(LH) % CH != 0, (P, LH))
    p = np.arange(P)
    return {
        "u_t": c(np.concatenate([tokens.T, np.zeros((DM, L), u.dtype)], 1)),
        "u_tok": c(tokens),
        "w_in_t": c(w_rows.T),
        "conv_w": c(conv_w[order].reshape(2 + CT, P, TAPS).transpose(1, 0, 2)),
        "conv_b": c(conv_b[order].reshape(2 + CT, P).T),
        "dt_bias": c(dt_bias[heads][:, None]),
        "a_log": c(np.tile(a_log[heads], 2)[:, None]),
        "d_skip": c(np.repeat(d, HD).reshape(CT, P).T),
        "norm_w": c(norm_w.reshape(CT, P).T),
        "w_out_t": c(w_out.T),
        "gu_words": c(np.repeat(gu.T, 2, axis=0)),
        "gu_scales": c(np.repeat(gu_s, P // KT, axis=0)),
        "dn_words": c(np.repeat(dn.T, 8, axis=0).reshape(FT, P, DM).transpose(1, 0, 2)),
        "dn_scales": c(np.broadcast_to(dn_s, (P, FT, DM))),
        "all_scales": c(np.concatenate([gu_s.reshape(P, -1), dn_s.reshape(P, -1)], 1)),
        "c_sel": bf16_bits(sel.reshape(P, CT, P)),
        "c_rhs": bf16_bits(rhs),
        "c_lhs": bf16_bits(lhs.reshape(94, NG, P)),
        "c_dec": bf16_bits(dec),
        "c_ident": np.eye(P, dtype=np.float32),
        "c_mask": bf16_bits(mask),
        "c_shift": c(np.stack([16 * (p % 2), 4 * (p % 8)], 1)).astype(np.int32),
    }
```

```python
from contextlib import ExitStack

import numpy as np

import concourse.bass as bass
from concourse import mybir

ALU = mybir.AluOpType
ACT = mybir.ActivationFunctionType
AX = mybir.AxisListType
F32 = mybir.dt.float32
F16 = mybir.dt.float16
BF16 = mybir.dt.bfloat16
I32 = mybir.dt.int32
U16 = mybir.dt.uint16
RMAX = bass.bass_isa.ReduceOp.max

P = 128
NB = 8
L = 512
DM = 512
KT = DM // P
DI = 1024
CT = DI // P
NH = 64
HD = DI // NH
NS = 128
NP = NH // 2
CH = 64
NC = L // CH
NG = 4
LH = L // 2
SLOTS = NC * NG
TT = L // P
TAPS = 4
IN_COLS = NH + 2 * NS + 2 * DI
FI = 1408
FT = FI // P
GU_SCALES = KT * 2 * FI // P
ALL_SCALES = GU_SCALES + FT * DM // P
MAXES_READY, W_SCALED = 2, 6
XB_COLS = NH + 2 * NS + DI
W_BLOCKS = [(0, NH + 2 * NS)] + [(NH + 2 * NS + i * 4 * P, 4 * P) for i in range(2 * DI // (4 * P))]
W_NEEDED = {"dt": 1, "x0": 2, "x4": 3, "z0": 4, "z4": 5}
DT_STEPS = 25
DT_PART = [1, 3, 7, 12, 16]
DT_SLOT = {9: 0, 11: 1, 13: 2, 17: 3, 19: 4}
SPLIT_SLOT = {k + 1: (k,) for k in range(KT)}
DEC = 352
NEG = -1.0e30
LOG1P = [2.0 / (2 * k + 1) for k in range(8)]

HEAD = ["a0", "z1", "z2", "e0", "a1", "e1", "z3", "a2", "a3", "e2", "z4", "z5", "z6", "z7"]
TAIL = {"pro": ["x7", "z0"] + HEAD, "body": ["x7", "z0", "o3", "q3"] + HEAD, "last": ["o3", "q3"]}
AUX_ORDER = (0, 2, 1, 3)
PRO_USES = [(0, "dt"), (0, "B"), (0, "C")] + [(0, f"x{i}") for i in range(CT - 1)]
BODY_USES = [(5, "dt"), (7, "B"), (9, "C"), (11, "x0"), (12, "q0"), (14, "o0"), (15, "x1"), (17, "x2"),
             (19, "x3"), (20, "q1"), (22, "o1"), (23, "x4"), (25, "x5"), (27, "x6"), (28, "q2"), (30, "o2")]
LAST_USES = [(12, "q0"), (14, "o0"), (20, "q1"), (22, "o1"), (28, "q2"), (30, "o2")]
CONV_TILES = ["B", "C"] + [f"x{i}" for i in range(CT)]
IN_COL = {"dt": 0, "B": NH, "C": NH + NS}
IN_COL |= {f"x{i}": NH + 2 * NS + i * P for i in range(CT)}
IN_COL |= {f"z{i}": NH + 2 * NS + DI + i * P for i in range(CT)}


def need(eng, sem, value):
    if isinstance(value, int) and value <= 0:
        return
    eng.wait_ge(sem, value)


def banks_of(uses):
    return [i % 2 for i in range(len(uses))]


class Stage:

    def __init__(self, kind, b):
        self.kind = kind
        self.scan = b if kind != "pro" else None
        self.proj = {"pro": 0, "body": b + 1, "last": None}[kind]
        uses = {"pro": PRO_USES, "body": BODY_USES, "last": LAST_USES}
        uses = {k: u + [(SLOTS, name) for name in TAIL[k] if name[0] not in "ae" and name != "q3"] for k, u in uses.items()}
        self.uses, self.tail = uses[kind], TAIL[kind]
        pro, body = [[banks_of(uses[k]).count(i) for i in range(2)] for k in ("pro", "body")]
        self.base = [0, 0] if kind == "pro" else [b * body[i] + pro[i] for i in range(2)]

    def bank(self, name):
        at = [u for _, u in self.uses].index(name)
        banks = banks_of(self.uses)
        count = self.base[banks[at]] + banks[:at].count(banks[at])
        return banks[at], count, count + 1

    def at(self, slot):
        return [u for s, u in self.uses if s == slot]

    def before(self):
        return Stage("pro", 0) if isinstance(self.scan, int) and self.scan == 0 else Stage("body", self.scan - 1)

    def last_z(self):
        found = [self.bank(f"z{i}") for i in (CT - 2, CT - 1)]
        assert found[0][0] != found[1][0]
        return [(bk, full) for bk, _, full in found]


class Chain:

    def __init__(self, eng, sem, per, b):
        self.eng, self.sem, self.per, self.base, self.k = eng, sem, per, b * per, 0

    def step(self, ins, then=None):
        self.k += 1
        ins.then_inc(self.sem, 1)
        self.eng.wait_ge(self.sem, self.base + self.k)
        if then:
            then(self.eng)

    def end(self):
        assert self.k == self.per, (self.k, self.per)


def build(nc, u_t, u_tok, w_in_t, conv_w, conv_b, dt_bias, a_log, d_skip, norm_w, w_out_t,
          gu_words, gu_scales, dn_words, dn_scales, all_scales, c_sel, c_rhs, c_lhs, c_dec, c_ident, c_mask,
          c_shift, out, nb=NB):
    ctx = ExitStack()
    with ctx:
        def sem(name):
            return ctx.enter_context(nc.semaphore(name))

        cs_dram = nc.dram_tensor("cs_dram", [nb, 3 * NH, L], BF16, kind="Internal")
        ld_dram = nc.dram_tensor("ld_dram", [nb, 3, NP, 2, L], BF16, kind="Internal")
        x1_dram = nc.dram_tensor("x1_dram", [nb * L, DM], F32, kind="Internal")
        gu_dram = nc.dram_tensor("gu_dram", [KT, P, 2 * FI], F16, kind="Internal")
        dn_dram = nc.dram_tensor("dn_dram", [2, P, FT, DM], F16, kind="Internal")

        def keep(name, shape, dt=F32):
            return ctx.enter_context(nc.sbuf_tensor(name, shape, dt))

        maxes = keep("maxes", [P, 3])
        maxes_all = keep("maxes_all", [P, 3])
        pow2 = keep("pow2", [P, 3])
        inv2 = keep("inv2", [P, 3])
        scal = keep("scal", [P, 8])
        ident = keep("ident", [P, P])
        half = keep("half", [P, 1])
        w_in_scale, w_in_undo = scal[:, 0:1], scal[:, 1:2]
        up_factor, dn_in_scale, down_undo = scal[:, 2:3], scal[:, 3:4], scal[:, 6:7]
        scratch1 = scal[:, 7:8]

        p1 = ExitStack()

        def sb(name, shape, dt=F32):
            return p1.enter_context(nc.sbuf_tensor(name, shape, dt))

        w_hi = sb("w_hi", [P, KT, IN_COLS], F16)
        w_lo = sb("w_lo", [P, KT, IN_COLS], F16)
        pre = sb("pre", [P, 2 + CT, L])
        u32 = sb("u32", [P, KT, L])
        u_hi = sb("u_hi", [P, KT, L], F16)
        u_lo = sb("u_lo", [P, KT, L], F16)
        dta = sb("dta", [P, LH])
        dtb = sb("dtb", [P, LH])
        dtc = sb("dtc", [P, LH])
        dtd = sb("dtd", [P, LH])
        dte = sb("dte", [P, LH])
        dtf = sb("dtf", [P, LH])
        cs_parts = sb("cs_parts", [P, 3, LH], BF16)
        ld_parts = sb("ld_parts", [P, 3, LH], BF16)
        w_out = sb("w_out", [P, CT, DM])
        bc = sb("bc", [P, 2, L])
        xs = sb("xs", [P, CT, L])
        zg = sb("zg", [P, CT, L])
        res = sb("res", [P, 2, DM])
        rhs_d = sb("rhs_d", [P, 2, NP, CH], BF16)
        lhs_d = sb("lhs_d", [P, 2, NG, 2 * CH], BF16)
        decay = sb("decay", [P, NG, CT, CH])
        mix = sb("mix", [P, NG, CT, CH])
        xpad = sb("xpad", [P, 2, NP, 2 * HD])
        xend = sb("xend", [P, NP, 2 * HD])
        state = sb("state", [P, DI])
        state_d = sb("state_d", [P, DI])
        gb = sb("gb", [P, 2, CH + NS])
        dec = sb("dec", [P, 2, NP, 2])
        ebc = sb("ebc", [P, 2, CT, CH])
        yoff = sb("yoff", [P, CT, CH])
        y = sb("y", [P, 2, CT, CH])
        sq = sb("sq", [P, CT, CH])
        ssum = sb("ssum", [P, L])
        cs12 = sb("cs12", [P, L], BF16)
        cs3 = sb("cs3", [NH, L], BF16)
        sel = sb("sel", [P, CT, P], BF16)
        sel_dec = sb("sel_dec", [6, 2, P], BF16)
        mask = sb("mask", [P, LH], BF16)
        cw = sb("cw", [P, 2 + CT, TAPS])
        cws = sb("cws", [P, 2 + CT, TAPS])
        cb = sb("cb", [P, 2 + CT])
        dskip = sb("dskip", [P, CT])
        normw = sb("normw", [P, CT])
        dtbias = sb("dtbias", [NH, 1])
        aneg = sb("aneg", [P, 1])
        ones = sb("ones", [P, 1])
        umax = sb("umax", [P, 1])
        umax_all = sb("umax_all", [P, 1])
        uscale = sb("uscale", [P, 1])
        uundo = sb("uundo", [P, 1])
        utmp = sb("utmp", [P, 2])
        msv = sb("msv", [P, TT])
        rinv = sb("rinv", [P, TT])
        bn = sb("bn", [P, 2, 6])
        mv = sb("mv", [P, 2, 2])
        rstd = sb("rstd", [P, 2])
        wmax = sb("wmax", [P, 2 * KT])
        scales_once = sb("scales_once", [P, ALL_SCALES], F16)
        shift = sb("shift", [P, 1], I32)
        fw_words = sb("fw_words", [P, 2, DEC], I32)
        fw_scale = sb("fw_scale", [P, 2, DEC], F16)
        fw_mag = sb("fw_mag", [P, DEC], I32)
        fw_sign = sb("fw_sign", [P, DEC], I32)
        fw_w = sb("fw_w", [P, DEC])
        fw_hi = sb("fw_hi", [P, 2, DEC], F16)
        fw_lo = sb("fw_lo", [P, 2, DEC], F16)
        p1.close()
        rooms = [(xs, k * XB_COLS) for k in range(KT - 1)] + [(pre, (CT - 1) * L)]
        w_xb, w_z = [[t[:, :, :].rearrange("p a b -> p (a b)")[:, at:at + n] for t, at in places]
                     for n, places in ((XB_COLS, rooms), (DI, [(zg, k * DI) for k in range(KT)]))]
        assert (KT - 1) * XB_COLS <= CT * L and XB_COLS <= 3 * L

        def w_src(k, col, n):
            return w_xb[k][:, col:col + n] if col < XB_COLS else w_z[k][:, col - XB_COLS:col - XB_COLS + n]

        p2 = ExitStack()

        def sb2(name, shape, dt=F32):
            return p2.enter_context(nc.sbuf_tensor(name, shape, dt))

        gu_w = sb2("gu_w", [P, KT, 2 * FI], F16)
        dn_hi = sb2("dn_hi", [P, FT, DM], F16)
        dn_lo = sb2("dn_lo", [P, FT, DM], F16)
        xa = sb2("xa", [P, TT, DM])
        xt_hi = sb2("xt_hi", [P, KT, L], F16)
        xt_lo = sb2("xt_lo", [P, KT, L], F16)
        gs16 = sb2("gs16", [P, KT, 2 * FT], F16)
        gs = sb2("gs", [P, KT, 2 * FT])
        gate_sum = sb2("gate_sum", [P, 2, L])
        up_sum = sb2("up_sum", [P, 2, L])
        gate_part = sb2("gate_part", [P, 2, L])
        up_part = sb2("up_part", [P, 2, L])
        h_hi = sb2("h_hi", [P, FT, L], F16)
        h_lo = sb2("h_lo", [P, FT, L], F16)
        sg = sb2("sg", [P, 2, L])
        hf = sb2("hf", [P, 2, L])
        xr = sb2("xr", [P, 2, DM])
        junk = sb2("junk", [P, DM])
        ss2 = sb2("ss2", [P, 2])
        ms2 = sb2("ms2", [P, 2])
        ri2 = sb2("ri2", [P, 2])
        rk2 = sb2("rk2", [P, 2])
        bn2 = sb2("bn2", [P, 2, 6])
        mv2 = sb2("mv2", [P, 2, 2])
        rs2 = sb2("rs2", [P, 2])
        p2.close()

        def bank(name):
            return ctx.enter_context(nc.psum_tensor(name, [P, 512], F32))

        ps_in = [bank("ps_in0"), bank("ps_in1")]
        ps_d = [bank("ps_d0"), bank("ps_d1")]
        ps_t, ps_s, ps_yd, ps_yo = bank("ps_t"), bank("ps_s"), bank("ps_yd"), bank("ps_yo")

        small_in = sem("small_in")
        const_in = sem("const_in")
        passed = sem("passed")
        w_xb_in = sem("w_xb_in")
        w_z_in = [sem(f"w_z_in{k}") for k in range(KT)]
        w_out_in = sem("w_out_in")
        w_out_done = sem("w_out_done")
        w_hi_done = sem("w_hi_done")
        w_lo_done = sem("w_lo_done")
        u_in = sem("u_in")
        res_in = [sem("res_in0"), sem("res_in1")]
        rq_in = [sem("rq_in0"), sem("rq_in1")]
        csp_in = sem("csp_in")
        parts_out = sem("parts_out")
        x1_out = [sem("x1_out0"), sem("x1_out1")]
        fw_in = [sem("fw_in0"), sem("fw_in1")]
        fw_out = [sem("fw_out0"), sem("fw_out1")]
        fw_chain = sem("fw_chain")
        fw_done = sem("fw_done")
        pro_dve = sem("pro_dve")
        pro_act = sem("pro_act")
        pro_pool = sem("pro_pool")
        u_max = sem("u_max")
        u_all = sem("u_all")
        u_scale = sem("u_scale")
        u_hi_done = sem("u_hi_done")
        u_lo_done = sem("u_lo_done")
        in_full = [sem("in_full0"), sem("in_full1")]
        q3_full = sem("q3_full")
        q3_free = sem("q3_free")
        in_free = [sem("in_free0"), sem("in_free1")]
        tap3 = sem("tap3")
        conv_chain = sem("conv_chain")
        silu_done = sem("silu_done")
        dt_act = sem("dt_act")
        dt_dve = sem("dt_dve")
        t_full = sem("t_full")
        t_free = sem("t_free")
        d_full = sem("d_full")
        e_done = sem("e_done")
        m_done = sem("m_done")
        xe_done = sem("xe_done")
        yd_done = sem("yd_done")
        yo_full = sem("yo_full")
        s_full = sem("s_full")
        s_add = sem("s_add")
        sd_done = sem("sd_done")
        xd_done = sem("xd_done")
        y1_done = sem("y1_done")
        y2_done = sem("y2_done")
        y_done = sem("y_done")
        gate_done = sem("gate_done")
        sq_done = sem("sq_done")
        sum_chain = sem("sum_chain")
        rinv_done = sem("rinv_done")
        ln_chain = sem("ln_chain")
        rstd_done = sem("rstd_done")
        x1_done = sem("x1_done")

        gw_in = sem("gw_in")
        xa_in = sem("xa_in")
        xr_in = [sem("xr_in0"), sem("xr_in1")]
        tr_full = sem("tr_full")
        xh_done = sem("xh_done")
        xl_done = sem("xl_done")
        gs_in = sem("gs_in")
        gs_done = sem("gs_done")
        gu_full = sem("gu_full")
        act_read = sem("act_read")
        dve_read = sem("dve_read")
        part_done = sem("part_done")
        sg_done = sem("sg_done")
        hf_done = sem("hf_done")
        hh_done = sem("hh_done")
        hl_done = sem("hl_done")
        dn_full = sem("dn_full")
        ss_done = sem("ss_done")
        ms_done = sem("ms_done")
        ri_done = sem("ri_done")
        o_chain = sem("o_chain")
        rs_done = sem("rs_done")
        o_done = sem("o_done")
        out_out = [sem("out_out0"), sem("out_out1")]

        W_STEPS = KT + 2
        N_GW = 16 * (W_STEPS + 3)
        FW_DMA, FW_STEPS = 16 * 4, 4 * KT + 6 * 2

        def fw_dmas(k):
            return 16 * (k // 2 + 1) + 16 * (k >= KT)

        GU_ORDER = [("g", 0), ("g", 1), ("u", 0), ("u", 1), ("g", 2), ("u", 2), ("g", 3), ("u", 3)]

        N_SMALL, N_CONST = 16 * 5, 16 * 11
        SLICE_G, SLICE_D = 2 * FI // NB, DM // NB
        assert SLICE_G == DEC and FT * SLICE_D == 2 * DEC
        fw_units = [("g", i) for i in range(KT)] + [("d", i) for i in range(2)]
        DECODE_AT = {"body": {21: [(0, 0), (0, 1)], 25: [(0, 2), (0, 3)], 27: [(1, 0), (1, 1)], 29: [(1, 2), (1, 3)]},
                     "last": {n: [(n // 4, n % 4)] for n in range(24)}}
        DECODE_LATE = {"body": [2, 3, 4, 5], "last": []}

        ps_t2, ps_n = ps_d, [ps_yd, ps_yo]
        ps_gu = [ps_yd] + ps_d + ps_in + [ps_t, ps_s, ps_yo]

        block = ctx.enter_context(nc.Block())

        def settled(eng):
            eng.sem_inc(passed, 1)

        @block.sync
        def _(sp):
            def load_u(b, wait):
                if wait:
                    need(sp, u_hi_done, b * KT)
                    settled(sp)
                    need(sp, u_lo_done, b * KT)
                    settled(sp)
                    need(sp, u_max, b)
                    settled(sp)
                sp.dma_start(u32[:, :, :], u_t.rearrange("(k p) t -> p k t", p=P)[:, :, bass.ds(b * L, L)])\
                  .then_inc(u_in, 16)

            def store_parts(b):
                sp.wait_ge(dt_dve, (b + 1) * DT_STEPS)
                settled(sp)
                for token_half in range(2):
                    t, row = slice(token_half * LH, (token_half + 1) * LH), token_half * NH
                    sp.dma_start(cs_dram[b].rearrange("(r q) t -> q r t", r=3)[:, :, t], cs_parts[row:row + NH, :, :])\
                      .then_inc(parts_out, 16)
                    for h2 in range(2):
                        sp.dma_start(ld_dram[b, :, :, h2, t].rearrange("r q t -> q r t"),
                                     ld_parts[row + h2 * NP:row + (h2 + 1) * NP, :, :]).then_inc(parts_out, 16)

            def load_cs(b):
                sp.wait_ge(parts_out, (b + 1) * 96)
                settled(sp)
                need(sp, t_full, b * 32)
                settled(sp)
                sp.dma_start(cs12[:, :], cs_dram[b, 0:2 * NH, :]).then_inc(csp_in, 16)
                sp.dma_start(cs3[:, :], cs_dram[b, 2 * NH:3 * NH, :]).then_inc(csp_in, 16)

            def load_rows(b, c):
                need(sp, d_full, b * SLOTS + NG * (c - 1))
                settled(sp)
                t = slice(c * CH, (c + 1) * CH)
                sp.dma_start(rhs_d[0:6, c % 2, :, :], cs_dram[b].rearrange("(r q) t -> r q t", q=NP)[:, :, t])\
                  .then_inc(rq_in[c % 2], 16)
                sp.dma_start(lhs_d[6:30, c % 2, :, :].rearrange("r g (h s) -> r (g h) s", h=2),
                             ld_dram[b].rearrange("r (q g) h t -> (r q) (g h) t", g=NG)[:, :, t])\
                  .then_inc(rq_in[c % 2], 16)

            def load_res(b, tt):
                need(sp, x1_out[tt % 2], b * 32 + 16 * (tt // 2))
                settled(sp)
                sp.dma_start(res[:, tt % 2, :], u_tok[bass.ds(b * L + tt * P, P), :]).then_inc(res_in[tt % 2], 16)

            def store_x1(b, tt):
                sp.wait_ge(x1_done, b * TT + tt + 1)
                settled(sp)
                sp.dma_start(x1_dram[bass.ds(b * L + tt * P, P), :], res[:, tt % 2, :]).then_inc(x1_out[tt % 2], 16)

            def load_fw(b, k):
                kind, i = fw_units[k]
                need(sp, fw_done, b * 6 + k - 1)
                settled(sp)
                words, scales = fw_words[:, k % 2, :], fw_scale[:, k % 2, :]
                if kind == "g":
                    loads = [(words, gu_words[i * P:(i + 1) * P, bass.ds(b * SLICE_G, DEC)])]
                else:
                    cols = bass.ds(b * SLICE_D + i * (SLICE_D // 2), SLICE_D // 2)
                    loads = [(dst.rearrange("p (g n) -> p g n", g=FT), src[:, :, cols])
                             for dst, src in ((words, dn_words), (scales, dn_scales))]
                for dst, src in loads:
                    sp.dma_start(dst, src).then_inc(fw_in[k % 2], 16)

            def store_fw(b, k):
                kind, i = fw_units[k]
                sp.wait_ge(fw_done, b * 6 + k + 1)
                settled(sp)
                if kind == "g":
                    sp.dma_start(gu_dram[i][:, bass.ds(b * SLICE_G, DEC)], fw_hi[:, k % 2, :]).then_inc(fw_out[k % 2], 16)
                    return
                cols = bass.ds(b * SLICE_D + i * (SLICE_D // 2), SLICE_D // 2)
                for part, w in enumerate((fw_hi, fw_lo)):
                    sp.dma_start(dn_dram[part][:, :, cols], w[:, k % 2, :].rearrange("p (g n) -> p g n", g=FT))\
                      .then_inc(fw_out[k % 2], 16)

            def next_fw(b, k):
                if k + 2 < len(fw_units):
                    load_fw(b, k + 2)
                store_fw(b, k)

            def load_head(b):
                load_cs(b)
                load_rows(b, 0)
                load_rows(b, 1)

            def room_free(last):
                for bk, full in last.before().last_z():
                    sp.wait_ge(in_full[bk], full)
                sp.wait_ge(silu_done, nb * 3)
                sp.wait_ge(u_max, nb + 1)
                sp.wait_ge(parts_out, nb * 96)

            def load_weights(step):
                if step < KT:
                    cols = slice(0, SLICE_G * (nb - 1))
                    sp.dma_start(gu_w[:, step, cols], gu_dram[step][:, cols]).then_inc(gw_in, 16)
                else:
                    part, cols = step - KT, slice(0, SLICE_D * (nb - 1))
                    sp.dma_start((dn_hi, dn_lo)[part][:, :, cols], dn_dram[part][:, :, cols]).then_inc(gw_in, 16)

            def load_last_slices():
                cols = slice(SLICE_G * (nb - 1), SLICE_G * nb)
                sp.dma_start(gu_w[:, :, cols], gu_dram.rearrange("k p n -> p k n")[:, :, cols]).then_inc(gw_in, 16)
                cols = slice(SLICE_D * (nb - 1), SLICE_D * nb)
                for part in range(2):
                    sp.dma_start((dn_hi, dn_lo)[part][:, :, cols], dn_dram[part][:, :, cols]).then_inc(gw_in, 16)

            def load_xa(f):
                need(sp, tr_full, f * KT)
                settled(sp)
                sp.dma_start(xa[:, :, :], x1_dram[bass.ds(f * L, L), :].rearrange("(t p) n -> p t n", p=P)).then_inc(xa_in, 16)

            def ahead(st, n):
                if n == 2:
                    room_free(st)
                    for k in range(2):
                        sp.wait_ge(fw_out[k], (nb - 1) * FW_DMA)
                    sp.dma_start(gs16[:, :, :], gu_scales).then_inc(gs_in, 16)
                if 2 <= n < 2 + W_STEPS:
                    load_weights(n - 2)
                if n == 2 + W_STEPS:
                    for k in range(2):
                        sp.wait_ge(x1_out[k], 32)
                    load_xa(0)
                if n == 26:
                    for k in range(2):
                        sp.wait_ge(fw_out[k], nb * FW_DMA)
                    load_last_slices()

            def body(st):
                b = st.scan
                load_res(b, 0)
                load_res(b, 1)
                load_fw(b, 0)
                load_fw(b, 1)
                for n in range(SLOTS):
                    c = n // NG + 2
                    if n == 8 and st.proj is not None:
                        load_u(b + 2, True)
                    if st.kind == "last":
                        ahead(st, n)
                    if n % NG == 1 and c < NC:
                        load_rows(b, c)
                    if n == 25 and st.proj is not None:
                        store_parts(b + 1)
                    if n == 30 and st.proj is not None:
                        load_head(b + 1)
                    for k, part in DECODE_AT[st.kind].get(n, []):
                        if part == 3:
                            next_fw(b, k)
                    for tt in range(2):
                        if f"o{tt}" in st.at(n):
                            store_x1(b, tt)
                            load_res(b, tt + 2)
                    if "o2" in st.at(n):
                        store_x1(b, 2)
                store_x1(b, 3)
                for k in DECODE_LATE[st.kind]:
                    next_fw(b, k)

            for k in range(KT):
                sp.dma_start(w_xb[k], w_in_t[k * P:(k + 1) * P, 0:XB_COLS]).then_inc(w_xb_in, 16)
            load_u(0, False)
            small = [(scales_once[:, :], all_scales), (cw[:, :, :], conv_w), (cb[:, :], conv_b),
                     (dtbias[:, :], dt_bias), (aneg[:, :], a_log)]
            later = [(dskip[:, :], d_skip), (normw[:, :], norm_w), (sel[:, :, :], c_sel),
                     (sel_dec[:, :, :], c_dec), (ident[:, :], c_ident), (mask[:, :], c_mask), (shift[:, :], c_shift)]
            later += [(rhs_d[6:94, i, :, :], c_rhs) for i in range(2)]
            later += [(lhs_d[:94, i, :, :], c_lhs) for i in range(2)]
            for dst, src in small:
                sp.dma_start(dst, src).then_inc(small_in, 16)
            for k in range(KT):
                sp.dma_start(w_z[k], w_in_t[k * P:(k + 1) * P, XB_COLS:IN_COLS]).then_inc(w_z_in[k], 16)
            for dst, src in later:
                if src.dtype == U16:
                    src = src.bitcast(BF16)
                sp.dma_start(dst, src).then_inc(const_in, 16)
            sp.dma_start(w_out[:, :, :], w_out_t.rearrange("(k p) n -> p k n", p=P)).then_inc(w_out_in, 16)
            load_u(1, True)
            sp.wait_ge(const_in, N_CONST)
            store_parts(0)
            load_head(0)
            body(Stage("body", 0))
            with sp.Fori(1, nb - 1) as i:
                body(Stage("body", i))
            body(Stage("last", nb - 1))

            for k in range(2):
                sp.wait_ge(x1_out[k], nb * 32)

            def load_xr(f, tt):
                need(sp, out_out[tt % 2], f * 32 + 16 * (tt // 2))
                settled(sp)
                sp.dma_start(xr[:, tt % 2, :], x1_dram[bass.ds(f * L + tt * P, P), :]).then_inc(xr_in[tt % 2], 16)

            def ffn(f, last):
                load_xr(f, 0)
                load_xr(f, 1)
                if not last:
                    load_xa(f + 1)
                for tt in range(TT):
                    sp.wait_ge(o_done, f * TT + tt + 1)
                    settled(sp)
                    sp.dma_start(out[bass.ds(f * L + tt * P, P), :], xr[:, tt % 2, :]).then_inc(out_out[tt % 2], 16)
                    if tt < 2:
                        load_xr(f, tt + 2)

            ffn(0, False)
            with sp.Fori(1, nb - 1) as f:
                ffn(f, False)
            ffn(nb - 1, True)
            for k in range(2):
                sp.wait_ge(out_out[k], nb * 32)

        @block.tensor
        def _(pe):
            mm, tr = nc.tensor.matmul, nc.tensor.transpose

            def project(st, name):
                bk, free, _ = st.bank(name)
                if name == "dt":
                    pe.wait_ge(u_hi_done, (st.proj + 1) * KT)
                    pe.wait_ge(u_lo_done, (st.proj + 1) * KT)
                if st.kind == "pro" and name in W_NEEDED:
                    pe.wait_ge(w_hi_done, KT * W_NEEDED[name])
                    pe.wait_ge(w_lo_done, KT * W_NEEDED[name])
                need(pe, in_free[bk], free)
                col, m = IN_COL[name], (NH if name == "dt" else P)
                passes = [(w_hi, u_hi), (w_hi, u_lo), (w_lo, u_hi)]
                for k in range(KT):
                    for j, (w, u) in enumerate(passes):
                        last = mm(ps_in[bk][0:m, :], w[:, k, col:col + m], u[:, k, :],
                                  start=(k == 0 and j == 0), stop=(k == KT - 1 and j == 2))
                last.then_inc(in_full[bk], 1)

            def square_sum(st, tt):
                pe.wait_ge(sum_chain, (st.scan * NC + 2 * tt + 2) * 3)
                if tt == TT - 1:
                    pe.wait_ge(y1_done, (st.scan + 1) * 7)
                    mm(ps_yo[:, 0:1], ssum[:, tt * P:(tt + 1) * P], ones[:, :], start=True, stop=True).then_inc(q3_full, 1)
                    return
                bk, free, _ = st.bank(f"q{tt}")
                need(pe, in_free[bk], free)
                mm(ps_in[bk][:, 0:1], ssum[:, tt * P:(tt + 1) * P], ones[:, :], start=True, stop=True)\
                    .then_inc(in_full[bk], 1)

            def out_proj(st, tt):
                bk, free, _ = st.bank(f"o{tt}")
                pe.wait_ge(gate_done, st.scan * NC + 2 * tt + 2)
                need(pe, in_free[bk], free)
                for k in range(CT):
                    last = mm(ps_in[bk][:, :], zg[:, k, tt * P:(tt + 1) * P], w_out[:, k, :],
                              start=(k == 0), stop=(k == CT - 1))
                last.then_inc(in_full[bk], 1)

            def use(st, name):
                if name[0] == "q":
                    square_sum(st, int(name[1]))
                elif name[0] == "o":
                    out_proj(st, int(name[1]))
                else:
                    project(st, name)

            def use_in(st, slot):
                for name in st.at(slot):
                    use(st, name)

            def aux(b, c, at):
                use = AUX_ORDER[at]
                need(pe, t_free, b * 32 + c * 4 + at)
                t = slice(c * CH, (c + 1) * CH)
                if use < 2:
                    pe.wait_ge(silu_done, (b + 1) * 3)
                    settled(pe)
                    for k in range(4):
                        last = tr(ps_t[0:CH, k * P:(k + 1) * P], xs[:, 4 * use + k, t], ident[:, :])
                elif use == 2:
                    mm(ps_t[0:CH, 0:CH], bc[:, 0, t], bc[:, 1, t], start=True, stop=True)
                    tr(ps_t[0:CH, CH:CH + NS], bc[:, 0, t], ident[:, :])
                    pe.wait_ge(rq_in[c % 2], b * 128 + 32 * (c // 2 + 1))
                    for h2 in range(2):
                        last = mm(ps_t[:, CH + NS + h2 * NP:CH + NS + (h2 + 1) * NP], sel_dec[:, h2, :],
                                  rhs_d[0:6, c % 2, :, CH - 1], start=True, stop=True)
                else:
                    pe.wait_ge(csp_in, (b + 1) * 32)
                    for k in range(CT):
                        o = ps_t[:, k * CH:(k + 1) * CH]
                        mm(o, sel[:, k, :], cs12[:, t], start=True, stop=False)
                        last = mm(o, sel[0:NH, k, :], cs3[:, t], start=False, stop=True)
                last.then_inc(t_full, 1)

            def exponents(b, n):
                c, g = n // NG, n % NG
                if g == 0:
                    pe.wait_ge(rq_in[c % 2], b * 128 + 32 * (c // 2 + 1))
                need(pe, e_done, b * SLOTS + n - 1)
                mm(ps_d[n % 2][:, :].rearrange("p (k t) -> p k t", k=CT), lhs_d[0:94, c % 2, g, :],
                   rhs_d[0:94, c % 2, g:NP:NG, :], start=True, stop=True).then_inc(d_full, 1)

            def within(b, n):
                c, g = n // NG, n % NG
                pe.wait_ge(m_done, b * SLOTS + n + 1)
                if g == 0:
                    pe.wait_ge(t_free, b * 32 + c * 4 + 3)
                    need(pe, y_done, b * NC + c)
                for k in range(CT):
                    last = mm(ps_yd[g * 32:(g + 1) * 32, k * CH:(k + 1) * CH], xpad[:, c % 2, k * NG + g, :],
                              mix[:, g, k, :], start=True, stop=True, tile_position=(0, g * 32))
                last.then_inc(yd_done, 1)

            def from_before(b, c):
                pe.wait_ge(s_add, b * 14 + 2 * c)
                need(pe, y1_done, b * 7 + c - 1)
                for k in range(CT):
                    last = mm(ps_yo[:, k * CH:(k + 1) * CH], state[:, k * P:(k + 1) * P],
                              bc[:, 1, c * CH:(c + 1) * CH], start=True, stop=True)
                last.then_inc(yo_full, 1)

            def new_state(b, c):
                pe.wait_ge(xe_done, b * SLOTS + NG * c + NG)
                need(pe, s_add, b * 14 + 2 * c)
                need(pe, y1_done, b * 7 + c)
                if c == 0:
                    need(pe, q3_free, b)
                for h2, to in enumerate((ps_s, ps_yo)):
                    rows = slice(h2 * CH, (h2 + 1) * CH)
                    mm(to[:, :].rearrange("p (q d) -> p q d", d=HD), gb[rows, c % 2, CH:CH + NS], xend[rows, :, h2 * HD:(h2 + 1) * HD],
                       start=True, stop=True).then_inc(s_full, 1)

            def turn(f, tiles):
                pe.wait_ge(xa_in, 16 * (f + 1))
                for i in tiles:
                    need(pe, xl_done, f * KT + i - 1)
                    for t in range(TT):
                        last = tr(ps_t2[i % 2][:, t * P:(t + 1) * P], xa[:, t, i * P:(i + 1) * P], ident[:, :])
                    last.then_inc(tr_full, 1)

            def body(st):
                b = st.scan
                for n in range(SLOTS):
                    c, g = n // NG, n % NG
                    if n + 3 < SLOTS:
                        exponents(b, n + 3)
                    if c + 1 < NC:
                        aux(b, c + 1, g)
                    if g == 0 and c > 0:
                        new_state(b, c - 1)
                    use_in(st, n)
                    within(b, n)
                    if g == 1 and c > 0:
                        from_before(b, c)
                tail(st)

            def tail(st):
                if st.kind == "last":
                    pe.wait_ge(e_done, nb * SLOTS)
                    turn(0, range(KT))
                for name in st.tail:
                    if name[0] == "a":
                        aux(st.proj, 0, int(name[1]))
                    elif name[0] == "e":
                        exponents(st.proj, int(name[1]))
                    else:
                        use(st, name)

            pro = Stage("pro", 0)
            use_in(pro, 0)
            pe.wait_ge(const_in, N_CONST)
            tail(pro)
            pe.wait_ge(w_out_done, 1)
            body(Stage("body", 0))
            with pe.Fori(1, nb - 1) as i:
                body(Stage("body", i))
            body(Stage("last", nb - 1))

            def gate_up(f):
                pe.wait_ge(xh_done, (f + 1) * KT)
                pe.wait_ge(xl_done, (f + 1) * KT)
                for m in range(FT):
                    for e, (which, g) in enumerate(GU_ORDER):
                        need(pe, act_read if e < 4 else dve_read, (f * FT + m - 1) * 4 + e % 4 + 1)
                        if m == 0 and e in (0, 7):
                            need(pe, o_chain, (f * TT - (2 if e == 0 else 1)) * 5 + 2)
                        col = (FI if which == "u" else 0) + m * P
                        for j, x in enumerate((xt_hi, xt_lo)):
                            last = mm(ps_gu[e][:, :], gu_w[:, g, col:col + P], x[:, g, :], start=(j == 0), stop=(j == 1))
                        last.then_inc(gu_full, 1)

            def turn_next(f, last, tiles):
                if not last:
                    pe.wait_ge(act_read, (f + 1) * FT * 4 - 1)
                    turn(f + 1, tiles)

            def down(f, final):
                for tt in range(TT):
                    if tt == 1:
                        turn_next(f, final, (2, 3))
                    if tt == 0:
                        pe.wait_ge(act_read, (f + 1) * FT * 4 - 3)
                    if tt == 1:
                        pe.wait_ge(dve_read, (f + 1) * FT * 4)
                    need(pe, o_chain, (f * TT + tt - 1) * 5 - 3)
                    t = slice(tt * P, (tt + 1) * P)
                    for k in range(FT):
                        if tt == 0:
                            pe.wait_ge(hh_done, f * FT + k + 1)
                            pe.wait_ge(hl_done, f * FT + k + 1)
                        for j, (h, w) in enumerate(((h_hi, dn_hi), (h_hi, dn_lo), (h_lo, dn_hi))):
                            last = mm(ps_n[tt % 2][:, :], h[:, k, t], w[:, k, :],
                                      start=(k == 0 and j == 0), stop=(k == FT - 1 and j == 2))
                    last.then_inc(dn_full, 1)

            def ffn(f, last):
                gate_up(f)
                turn_next(f, last, (0, 1))
                down(f, last)

            end = Stage("last", nb - 1)
            pe.wait_ge(t_free, nb * 32)
            pe.wait_ge(s_add, nb * 14)
            for name in ("o2", "o3"):
                bk, _, full = end.bank(name)
                pe.wait_ge(in_free[bk], full)
            pe.wait_ge(y_done, nb * NC)
            pe.wait_ge(q3_free, nb)
            pe.wait_ge(gw_in, N_GW)
            ffn(0, False)
            with pe.Fori(1, nb - 1) as f:
                ffn(f, False)
            ffn(nb - 1, True)

        @block.scalar
        def _(act):
            ac = nc.scalar.activation

            def split_hi(b, before, tiles):
                act.wait_ge(u_scale, (b + 1) * 5)
                if before is not None:
                    for bk, count in before.last_z():
                        act.wait_ge(in_full[bk], count)
                for k in tiles:
                    ac(u_hi[:, k, :], u32[:, k, :], ACT.Identity, scale=uscale[:, 0:1]).then_inc(u_hi_done, 1)

            def take_dt(st):
                bk, _, full = st.bank("dt")
                act.wait_ge(in_full[bk], full)
                need(act, dt_dve, st.proj * DT_STEPS)
                for h in range(2):
                    last = ac(dta[h * NH:(h + 1) * NH, :], ps_in[bk][0:NH, h * LH:(h + 1) * LH], ACT.Identity,
                              bias=dtbias[:, 0:1], scale=uundo[0:NH, 0:1])
                last.then_inc(in_free[bk], 1)

            def exp_dt(b):
                act.wait_ge(dt_dve, b * DT_STEPS + 1)
                ac(dtb[:, :], dtb[:, :], ACT.Exp).then_inc(dt_act, 1)

            def ln_dt(b):
                act.wait_ge(dt_dve, b * DT_STEPS + 15)
                ac(dtc[:, :], dta[:, :], ACT.Ln).then_inc(dt_act, 1)

            def take_conv(st, name):
                m = CONV_TILES.index(name)
                bk, _, full = st.bank(name)
                act.wait_ge(in_full[bk], full)
                need(act, silu_done, st.proj * 3)
                ac(pre[:, m, :], ps_in[bk][:, :], ACT.Identity, bias=cb[:, m:m + 1], scale=cws[:, m, 3:4])\
                    .then_inc(tap3, 1)

            def silu_all(st):
                b = st.proj
                bk, _, count = st.bank(CONV_TILES[-1])
                act.wait_ge(in_free[bk], count)
                need(act, t_full, b * 32)
                need(act, yo_full, b * 7)
                need(act, xd_done, b * NC)
                ac(bc[:, :, :], pre[:, 0:2, :], ACT.Silu).then_inc(silu_done, 1)
                for h in range(2):
                    ac(xs[:, 4 * h:4 * h + 4, :], pre[:, 2 + 4 * h:6 + 4 * h, :], ACT.Silu).then_inc(silu_done, 1)

            def take_z(st, name):
                bk, _, full = st.bank(name)
                act.wait_ge(in_full[bk], full)
                if st.kind == "pro" and name == "z0":
                    act.wait_ge(w_lo_done, KT * len(W_BLOCKS))
                if st.kind == "body" and name == "z0":
                    ob, _, ofull = st.bank("o3")
                    act.wait_ge(in_full[ob], ofull)
                    act.wait_ge(sq_done, (st.scan + 1) * NC)
                ac(zg[:, int(name[1]), :], ps_in[bk][:, :], ACT.Silu, scale=uundo[:, 0:1]).then_inc(in_free[bk], 1)

            def use_in(st, slot):
                for name in st.at(slot):
                    if name == "dt":
                        take_dt(st)
                    elif name in CONV_TILES:
                        take_conv(st, name)

            def aux(b, c, at):
                use = AUX_ORDER[at]
                act.wait_ge(t_full, b * 32 + c * 4 + at + 1)
                if use < 2:
                    if use == 0:
                        need(act, yd_done, b * SLOTS + NG * (c - 1))
                        need(act, xe_done, b * SLOTS + NG * (c - 1))
                    for h2 in range(2):
                        rows = slice(h2 * CH, (h2 + 1) * CH)
                        src = ps_t[0:CH, :].rearrange("p (q h d) -> p q h d", h=2, d=HD)[:, :, h2, :]
                        last = ac(xpad[rows, c % 2, 16 * use:16 * use + 16, h2 * HD:(h2 + 1) * HD], src, ACT.Copy)
                elif use == 2:
                    need(act, m_done, b * SLOTS + NG * (c - 1))
                    need(act, s_full, b * 14 + 2 * max(c - 1, 0))
                    need(act, sd_done, b * 6 + min(max(c - 2, 0), 6))
                    for h2 in range(2):
                        ac(gb[h2 * CH:(h2 + 1) * CH, c % 2, :], ps_t[0:CH, 0:CH + NS], ACT.Copy)
                    last = ac(dec[:, c % 2, :, :].rearrange("p q h -> p h q"),
                              ps_t[:, CH + NS:CH + NS + 2 * NP].rearrange("p (h q) -> p h q", h=2), ACT.Exp)
                else:
                    need(act, y1_done, b * 7 + max(c - 2, 0))
                    last = ac(ebc[:, c % 2, :, :].rearrange("p a b -> p (a b)"), ps_t[:, :], ACT.Exp)
                last.then_inc(t_free, 1)

            def square(b, c):
                act.wait_ge(gate_done, b * NC + c + 1)
                need(act, sum_chain, (b * NC + c) * 3)
                ac(sq[:, :, :], zg[:, :, c * CH:(c + 1) * CH], ACT.Square).then_inc(sq_done, 1)

            def exp_group(b, n):
                act.wait_ge(d_full, b * SLOTS + n + 1)
                need(act, m_done, b * SLOTS + n - 3)
                need(act, xe_done, b * SLOTS + n - 3)
                ac(decay[:, n % NG, :, :].rearrange("p a b -> p (a b)"), ps_d[n % 2][:, :], ACT.Exp).then_inc(e_done, 1)

            def body(st):
                b = st.scan
                for n in range(SLOTS):
                    c, g = n // NG, n % NG
                    if n in SPLIT_SLOT and st.proj is not None:
                        split_hi(st.proj, st.before(), SPLIT_SLOT[n])
                    if n + 3 < SLOTS:
                        exp_group(b, n + 3)
                    if c + 1 < NC:
                        aux(b, c + 1, g)
                    if g == 2 and c > 0:
                        square(b, c - 1)
                    use_in(st, n)
                    if st.proj is not None and n == 7:
                        exp_dt(st.proj)
                    if st.proj is not None and n == 20:
                        ln_dt(st.proj)
                tail(st)

            def turn(f, tiles):
                for i in tiles:
                    act.wait_ge(tr_full, f * KT + i + 1)
                    if i == 0:
                        need(act, gu_full, f * FT * 8)
                    ac(xt_hi[:, i, :], ps_t2[i % 2][:, :], ACT.Copy, scale=1024.0).then_inc(xh_done, 1)

            def tail(st):
                if st.kind == "last":
                    act.wait_ge(dt_dve, nb * DT_STEPS)
                    turn(0, range(KT))
                    square(st.scan, NC - 1)
                order = list(st.tail)
                if "z3" in order:
                    order.remove("z3")
                    order.insert(order.index("z4"), "z3")
                for name in order:
                    if name in CONV_TILES:
                        take_conv(st, name)
                        if st.kind == "body":
                            square(st.scan, NC - 1)
                        silu_all(st)
                    elif name[0] == "a":
                        aux(st.proj, 0, int(name[1]))
                    elif name[0] == "e":
                        exp_group(st.proj, int(name[1]))
                    elif name[0] == "z":
                        take_z(st, name)

            def weights_hi(block):
                col, n = W_BLOCKS[block]
                for k in range(KT):
                    ac(w_hi[:, k, col:col + n], w_src(k, col, n), ACT.Identity, scale=w_in_scale).then_inc(w_hi_done, 1)

            act.wait_ge(small_in, N_SMALL)
            ac(aneg[:, :], aneg[:, :], ACT.Exp).then_inc(pro_act, 1)
            act.wait_ge(pro_dve, W_SCALED)
            weights_hi(0)
            split_hi(0, None, range(KT))
            weights_hi(1)
            pro = Stage("pro", 0)
            take_dt(pro)
            exp_dt(0)
            take_conv(pro, "B")
            take_conv(pro, "C")
            weights_hi(2)
            for i in range(CT - 1):
                if i == 5:
                    act.wait_ge(w_lo_done, KT * 3)
                take_conv(pro, f"x{i}")
                if i == 2:
                    ln_dt(0)
                if i in (3, 5):
                    weights_hi(i // 2 + 2)
            act.wait_ge(const_in, N_CONST)
            act.wait_ge(pro_pool, 1)
            tail(pro)
            body(Stage("body", 0))
            with act.Fori(1, nb - 1) as i:
                body(Stage("body", i))
            body(Stage("last", nb - 1))

            def read(f, m, e, dst):
                which, g = GU_ORDER[e]
                act.wait_ge(gu_full, (f * FT + m) * 8 + e + 1)
                ch = (FT if which == "u" else 0) + m
                ac(dst[:, m % 2, :], ps_gu[e][:, :], ACT.Identity, scale=gs[:, g, ch:ch + 1]).then_inc(act_read, 1)

            def hidden(f, first):
                for m in range(FT + 2):
                    at = f * FT + m
                    if m < FT:
                        need(act, sg_done, at - 1)
                        read(f, m, 0, gate_sum)
                        need(act, part_done, (at - 2) * 2 + 1)
                        read(f, m, 1, gate_part)
                        need(act, hf_done, at - 1)
                        read(f, m, 2, up_sum)
                        need(act, part_done, (at - 1) * 2)
                        read(f, m, 3, up_part)
                    if m == 1 and first:
                        for k in range(2):
                            act.wait_ge(x1_out[k], nb * 32)
                    if 1 <= m <= FT:
                        act.wait_ge(dve_read, (at - 1) * 4 + 3)
                        need(act, hf_done, at - 2)
                        ac(sg[:, (m - 1) % 2, :], gate_sum[:, (m - 1) % 2, :], ACT.Silu).then_inc(sg_done, 1)
                    if m >= 2:
                        act.wait_ge(hf_done, at - 1)
                        if m == 2:
                            need(act, dn_full, f * TT)
                        ac(h_hi[:, m - 2, :], hf[:, (m - 2) % 2, :], ACT.Copy).then_inc(hh_done, 1)

            def squares(f, last):
                for tt in range(TT):
                    if tt == 1 and not last:
                        turn(f + 1, (2, 3))
                    act.wait_ge(dn_full, f * TT + tt + 1)
                    need(act, ms_done, f * TT + tt - 1)
                    need(act, ss_done, f * TT + tt)
                    ac(junk[:, :], ps_n[tt % 2][:, :], ACT.Square, scale=down_undo,
                       accum_out=ss2[:, tt % 2:tt % 2 + 1]).then_inc(ss_done, 1)

            def ffn(f, first, last):
                hidden(f, first)
                if not last:
                    turn(f + 1, (0, 1))
                squares(f, last)

            act.wait_ge(gs_done, 1)
            ffn(0, True, False)
            with act.Fori(1, nb - 1) as f:
                ffn(f, False, False)
            ffn(nb - 1, False, True)

        @block.vector
        def _(dve):
            v = nc.vector

            def measure_u(b):
                dve.wait_ge(u_in, (b + 1) * 16)
                need(dve, u_all, b)
                v.tensor_reduce(umax[:, :], u32[:, :, :], AX.XY, ALU.max, apply_absolute_value=True).then_inc(u_max, 1)

            def scale_u(b, before):
                ch = Chain(dve, u_scale, 5, b)
                dve.wait_ge(u_all, b + 1)
                if before is not None:
                    for bk, count in before.last_z():
                        dve.wait_ge(in_free[bk], count)
                ch.step(v.tensor_scalar(utmp[:, 0:1], umax_all[:, :], 1e-30, None, ALU.max))
                ch.step(v.tensor_scalar(utmp[:, 1:2].bitcast(I32), utmp[:, 0:1].bitcast(I32), 0x7F800000, None,
                                        ALU.bitwise_and))
                ch.step(v.reciprocal(utmp[:, 0:1], utmp[:, 1:2]))
                v.tensor_scalar(uscale[:, :], utmp[:, 0:1], 2.0 ** 14, None, ALU.mult)
                ch.step(v.tensor_scalar(uundo[:, :], utmp[:, 1:2], w_in_undo, 2.0 ** -14, ALU.mult, ALU.mult))
                ch.step(v.tensor_scalar(cws[:, :, :], cw[:, :, :], uundo[:, 0:1], None, ALU.mult))
                ch.end()

            def split_lo(b, tiles):
                for k in tiles:
                    dve.wait_ge(u_hi_done, b * KT + k + 1)
                    v.scalar_tensor_tensor(u_lo[:, k, :], u32[:, k, :], uscale[:, 0:1], u_hi[:, k, :],
                                           ALU.mult, ALU.subtract).then_inc(u_lo_done, 1)

            def taps(st, name):
                m = CONV_TILES.index(name)
                bk, _, _ = st.bank(name)
                at = st.proj * 20 + 2 * m
                dve.wait_ge(tap3, st.proj * 10 + m + 1)
                for j, k in enumerate((2, 1, 0)):
                    d = 3 - k
                    if j:
                        dve.wait_ge(conv_chain, at + j)
                    ins = v.scalar_tensor_tensor(pre[:, m, d:L], ps_in[bk][:, 0:L - d], cws[:, m, k:k + 1],
                                                 pre[:, m, d:L], ALU.mult, ALU.add)
                    ins.then_inc(conv_chain if j < 2 else in_free[bk], 1)

            def dt_first(st):
                bk, free, _ = st.bank("dt")
                dve.wait_ge(in_free[bk], free + 1)
                need(dve, dt_act, st.proj * 2)
                v.scalar_tensor_tensor(dtb[:, :], dta[:, :], -1.0, dta[:, :], ALU.mult, ALU.min).then_inc(dt_dve, 1)

            def dt_second(b, part):
                ch = Chain(dve, dt_dve, DT_STEPS, b)
                ch.k = DT_PART[part]
                if part == 0:
                    dve.wait_ge(dt_act, b * 2 + 1)
                    ch.step(v.tensor_scalar(dtc[:, :], dtb[:, :], 2.0, None, ALU.add))
                    ch.step(v.reciprocal(dtd[:, :], dtc[:, :]))
                elif part == 1:
                    ch.step(v.tensor_tensor(dtb[:, :], dtb[:, :], dtd[:, :], ALU.mult))
                    ch.step(v.tensor_tensor(dtc[:, :], dtb[:, :], dtb[:, :], ALU.mult))
                    ch.step(v.tensor_scalar(dtd[:, :], dtc[:, :], LOG1P[7], LOG1P[6], ALU.mult, ALU.add))
                    ch.step(v.tensor_tensor(dtd[:, :], dtd[:, :], dtc[:, :], ALU.mult))
                elif part == 2:
                    for k in range(5, 0, -1):
                        ch.step(v.scalar_tensor_tensor(dtd[:, :], dtd[:, :], LOG1P[k], dtc[:, :], ALU.add, ALU.mult))
                elif part == 3:
                    ch.step(v.scalar_tensor_tensor(dtd[:, :], dtd[:, :], LOG1P[0], dtb[:, :], ALU.add, ALU.mult))
                    ch.step(v.scalar_tensor_tensor(dtd[:, :], dta[:, :], 0.0, dtd[:, :], ALU.max, ALU.add))
                    ch.step(v.tensor_scalar(dta[:, :], dtd[:, :], 1e-18, None, ALU.max))
                    ch.step(v.tensor_scalar(dtb[:, :], dtd[:, :], aneg[:, 0:1], None, ALU.mult))
                else:
                    ch.step(v.tensor_tensor_scan(dte[:, :], mask[:, :], dtb[:, :], 0.0, ALU.mult, ALU.add))
                    need(dve, parts_out, b * 96)
                    ch.step(v.tensor_copy(cs_parts[:, 0, :], dte[:, :]))
                    ch.step(v.tensor_tensor(dtf[:, :], dte[:, :], cs_parts[:, 0, :], ALU.subtract))
                    ch.step(v.tensor_copy(cs_parts[:, 1, :], dtf[:, :]))
                    v.tensor_tensor(cs_parts[:, 2, :], dtf[:, :], cs_parts[:, 1, :], ALU.subtract)
                assert part == 4 or ch.k == DT_PART[part + 1]

            def dt_third(b):
                ch = Chain(dve, dt_dve, DT_STEPS, b)
                ch.k = 20
                dve.wait_ge(dt_act, b * 2 + 2)
                ch.step(v.tensor_tensor(dtc[:, :], dtc[:, :], dte[:, :], ALU.subtract))
                ch.step(v.tensor_copy(ld_parts[:, 0, :], dtc[:, :]))
                ch.step(v.tensor_tensor(dtf[:, :], dtc[:, :], ld_parts[:, 0, :], ALU.subtract))
                ch.step(v.tensor_copy(ld_parts[:, 1, :], dtf[:, :]))
                ch.step(v.tensor_tensor(ld_parts[:, 2, :], dtf[:, :], ld_parts[:, 1, :], ALU.subtract))
                ch.end()

            def decode(b, k, part):
                kind, i = fw_units[k]
                words = fw_words[:, k % 2, :]
                ch = Chain(dve, fw_chain, FW_STEPS, b)
                ch.k = min(k, KT) * 4 + max(k - KT, 0) * 6 + (0, 1, 4, 5)[part]
                if part == 0:
                    dve.wait_ge(fw_in[k % 2], b * FW_DMA + fw_dmas(k))
                    ch.step(v.tensor_scalar(words, words, shift[:, 0:1], None, ALU.logical_shift_right))
                elif part == 1:
                    for dst, by, bits in ((fw_mag, 9, 0x0E00), (fw_sign, 12, 0x8000)):
                        ch.step(v.tensor_scalar(dst[:, :], words, by, bits, ALU.logical_shift_left, ALU.bitwise_and))
                    ch.step(v.tensor_tensor(fw_mag[:, :], fw_mag[:, :], fw_sign[:, :], ALU.bitwise_or))
                elif part == 2 and kind == "g":
                    need(dve, fw_out[k % 2], b * FW_DMA + 16 * (k // 2))
                    v.tensor_scalar(fw_hi[:, k % 2, :], fw_mag[:, :].bitcast(F16)[:, 0:2 * DEC:2], 2.0 ** 14, None,
                                    ALU.mult).then_inc(fw_done, 1)
                elif part == 2:
                    ch.step(v.scalar_tensor_tensor(fw_w[:, :], fw_mag[:, :].bitcast(F16)[:, 0:2 * DEC:2], dn_in_scale,
                                                   fw_scale[:, k % 2, :], ALU.mult, ALU.mult))
                elif kind == "d":
                    need(dve, fw_out[k % 2], b * FW_DMA + 16 * (k // 2))
                    ch.step(v.tensor_copy(fw_hi[:, k % 2, :], fw_w[:, :]))
                    v.tensor_tensor(fw_lo[:, k % 2, :], fw_w[:, :], fw_hi[:, k % 2, :], ALU.subtract).then_inc(fw_done, 1)

            def mixing(b, n):
                c = n // NG
                dve.wait_ge(e_done, b * SLOTS + n + 1)
                if n % NG == 0:
                    dve.wait_ge(t_free, b * 32 + c * 4 + 2)
                need(dve, yd_done, b * SLOTS + n - 3)
                v.tensor_tensor(mix[:, n % NG, :, :], decay[:, n % NG, :, :],
                                gb[:, c % 2, 0:CH].unsqueeze(1).broadcast_to([P, CT, CH]), ALU.mult).then_inc(m_done, 1)

            def add_state(b, c, h2):
                def part(ap):
                    return ap.rearrange("p (q h d) -> p q h d", h=2, d=HD)[:, :, h2, :]

                new = (ps_s, ps_yo)[h2][:, :].rearrange("p (q d) -> p q d", d=HD)
                dve.wait_ge(s_full, b * 14 + 2 * c + h2 + 1)
                if c == 0:
                    need(dve, yo_full, b * 7)
                    v.tensor_copy(part(state[:, :]), new).then_inc(s_add, 1)
                else:
                    dve.wait_ge(sd_done, b * 6 + c)
                    dve.wait_ge(yo_full, b * 7 + c)
                    v.tensor_tensor(part(state[:, :]), new, part(state_d[:, :]), ALU.add).then_inc(s_add, 1)

            def flat(ap):
                return ap.rearrange("p a b -> p (a b)")

            def y_before(b, c):
                if c > 0:
                    dve.wait_ge(yo_full, b * 7 + c)
                    dve.wait_ge(t_free, b * 32 + c * 4 + 4)
                    need(dve, y2_done, b * 7 + c - 1)
                    v.tensor_tensor(flat(yoff[:, :, :]), ps_yo[:, :], flat(ebc[:, c % 2, :, :]), ALU.mult).then_inc(y1_done, 1)
                    dve.wait_ge(y1_done, b * 7 + c)
                    dve.wait_ge(xd_done, b * NC + c + 1)
                    v.tensor_tensor(y[:, c % 2, :, :], y[:, c % 2, :, :], yoff[:, :, :], ALU.add).then_inc(y2_done, 1)

            def y_all(b, c):
                dve.wait_ge(yd_done, b * SLOTS + NG * (c + 1))
                dve.wait_ge(xd_done, b * NC + c + 1)
                need(dve, y2_done, b * 7 + c)
                v.tensor_tensor(flat(y[:, c % 2, :, :]), ps_yd[:, :], flat(y[:, c % 2, :, :]), ALU.add).then_inc(y_done, 1)

            def mean_square(st, tt):
                if tt == TT - 1:
                    full, count, free, src = q3_full, st.scan + 1, q3_free, ps_yo
                else:
                    bk, _, count = st.bank(f"q{tt}")
                    full, free, src = in_full[bk], in_free[bk], ps_in[bk]
                dve.wait_ge(full, count)
                need(dve, rinv_done, st.scan * TT)
                v.tensor_scalar(msv[:, tt:tt + 1], src[:, 0:1], 1.0 / DI, 1e-5, ALU.mult, ALU.add).then_inc(free, 1)

            def norm_tile(st, tt):
                b = st.scan
                bk, _, full = st.bank(f"o{tt}")
                i = tt % 2
                ch = Chain(dve, ln_chain, 12, b)
                ch.k = 3 * tt
                dve.wait_ge(in_full[bk], full)
                dve.wait_ge(rinv_done, b * TT + tt + 1)
                dve.wait_ge(res_in[i], b * 32 + 16 * (tt // 2) + 16)
                v.scalar_tensor_tensor(res[:, i, :], ps_in[bk][:, :], rinv[:, tt:tt + 1], res[:, i, :],
                                       ALU.mult, ALU.add).then_inc(in_free[bk], 1)
                dve.wait_ge(in_free[bk], full)
                ch.step(v.bn_stats(bn[:, i, :], res[:, i, :]), settled)
                ch.step(v.bn_aggr(mv[:, i, :], bn[:, i, :]))
                v.tensor_scalar(mv[:, i, 1:2], mv[:, i, 1:2], 1e-5, None, ALU.add).then_inc(ln_chain, 1)

            def norm_tile_end(st, tt):
                b, i = st.scan, tt % 2
                dve.wait_ge(rstd_done, b * TT + tt + 1)
                v.tensor_scalar(res[:, i, :], res[:, i, :], mv[:, i, 0:1], rstd[:, i:i + 1],
                                ALU.subtract, ALU.mult).then_inc(x1_done, 1)

            def use_in(st, slot):
                for name in st.at(slot):
                    if name in CONV_TILES:
                        taps(st, name)
                    elif name[0] == "q":
                        mean_square(st, int(name[1]))
                    elif name[0] == "o":
                        if int(name[1]) == TT - 1:
                            mean_square(st, TT - 1)
                        norm_tile(st, int(name[1]))

            def turn(f, tiles):
                for i in tiles:
                    dve.wait_ge(xh_done, f * KT + i + 1)
                    v.scalar_tensor_tensor(xt_lo[:, i, :], ps_t2[i % 2][:, :], 1024.0, xt_hi[:, i, :],
                                           ALU.mult, ALU.subtract).then_inc(xl_done, 1)

            def body(st):
                b = st.scan
                mixing(b, 0)
                mixing(b, 1)
                for n in range(SLOTS):
                    c, g = n // NG, n % NG
                    if n == 0 and st.proj is not None:
                        scale_u(st.proj, st.before())
                    if g == 0 and c > 0:
                        y_all(b, c - 1)
                    if n + 2 < SLOTS:
                        mixing(b, n + 2)
                    if g == 0 and c > 0:
                        add_state(b, c - 1, 0)
                        add_state(b, c - 1, 1)
                    if n in SPLIT_SLOT and st.proj is not None:
                        split_lo(st.proj, SPLIT_SLOT[n])
                    if g == 2:
                        y_before(b, c)
                    if n > 0:
                        use_in(st, n - 1)
                    for tt in range(TT - 2):
                        if f"o{tt}" in st.at(n - 2):
                            norm_tile_end(st, tt)
                    if st.proj is not None:
                        if n == 6:
                            dt_first(st)
                        if n in DT_SLOT:
                            dt_second(st.proj, DT_SLOT[n])
                        if n == 23:
                            dt_third(st.proj)
                    for k, part in DECODE_AT[st.kind].get(n, []):
                        decode(b, k, part)
                y_all(b, NC - 1)
                norm_tile_end(st, TT - 2)
                use_in(st, SLOTS - 1)
                if st.kind == "last":
                    dve.wait_ge(parts_out, nb * 96)
                    turn(0, range(KT))
                    dve.wait_ge(gs_in, 16)
                    v.tensor_scalar(gs[:, :, 0:FT], gs16[:, :, 0:FT], 2.0 ** -10, None, ALU.mult)
                    v.tensor_scalar(gs[:, :, FT:2 * FT], gs16[:, :, FT:2 * FT], up_factor, inv2[:, 1:2],
                                    ALU.mult, ALU.mult).then_inc(gs_done, 1)
                use_in(st, SLOTS)
                if st.proj is not None:
                    measure_u(b + 2)
                norm_tile_end(st, TT - 1)
                for k in DECODE_LATE[st.kind]:
                    for part in range(4):
                        decode(b, k, part)

            ch = Chain(dve, pro_dve, W_SCALED, 0)
            v.memset(ones[:, :], 1.0)
            v.memset(half[:, :], -0.5)
            dve.wait_ge(w_xb_in, KT * 16)
            for k in range(KT):
                v.tensor_reduce(wmax[:, k:k + 1], w_xb[k], AX.X, ALU.max, apply_absolute_value=True)
            measure_u(0)
            for k in range(KT):
                dve.wait_ge(w_z_in[k], 16)
                v.tensor_reduce(wmax[:, KT + k:KT + k + 1], w_z[k], AX.X, ALU.max, apply_absolute_value=True)
            dve.wait_ge(small_in, N_SMALL)
            v.tensor_reduce(maxes[:, 1:2], scales_once[:, 0:GU_SCALES], AX.X, ALU.max)
            ch.step(v.tensor_reduce(maxes[:, 2:3], scales_once[:, GU_SCALES:ALL_SCALES], AX.X, ALU.max))
            ch.step(v.tensor_reduce(maxes[:, 0:1], wmax[:, :], AX.X, ALU.max))
            assert ch.k == MAXES_READY
            dve.wait_ge(pro_pool, 2)
            v.tensor_scalar(maxes[:, 0:1], maxes_all[:, 0:1], 1e-30, None, ALU.max)
            ch.step(v.tensor_scalar(maxes[:, 1:3], maxes_all[:, 1:3], 2.0 ** -24, None, ALU.max))
            ch.step(v.tensor_scalar(pow2[:, :].bitcast(I32), maxes[:, :].bitcast(I32), 0x7F800000, None, ALU.bitwise_and))
            ch.step(v.reciprocal(inv2[:, :], pow2[:, :]))
            v.tensor_scalar(w_in_scale, inv2[:, 0:1], 2.0 ** 14, None, ALU.mult)
            v.tensor_scalar(w_in_undo, pow2[:, 0:1], 2.0 ** -14, None, ALU.mult)
            v.tensor_scalar(dn_in_scale, inv2[:, 2:3], 2.0 ** 25, None, ALU.mult)
            v.tensor_scalar(up_factor, inv2[:, 1:2], 2.0 ** -20, None, ALU.mult)
            ch.step(v.tensor_scalar(scratch1, pow2[:, 1:2], pow2[:, 1:2], 0.5, ALU.mult, ALU.mult))
            assert ch.k == W_SCALED
            v.tensor_scalar(down_undo, scratch1, pow2[:, 2:3], None, ALU.mult)
            dve.wait_ge(pro_act, 1)
            v.tensor_scalar(aneg[:, :], aneg[:, :], -1.0, None, ALU.mult)
            assert ch.k == W_SCALED

            def weights_lo(block):
                col, n = W_BLOCKS[block]
                for k in range(KT):
                    dve.wait_ge(w_hi_done, KT * block + k + 1)
                    v.scalar_tensor_tensor(w_lo[:, k, col:col + n], w_src(k, col, n), w_in_scale,
                                           w_hi[:, k, col:col + n], ALU.mult, ALU.subtract).then_inc(w_lo_done, 1)

            scale_u(0, None)
            weights_lo(0)
            split_lo(0, range(KT))
            weights_lo(1)
            pro = Stage("pro", 0)
            dt_first(pro)
            taps(pro, "B")
            dt_second(0, 0)
            taps(pro, "C")
            dve.wait_ge(const_in, N_CONST)
            dt_second(0, 1)
            weights_lo(2)
            for i in range(CT):
                if i < 3:
                    dt_second(0, 2 + i)
                if i == 3:
                    dt_third(0)
                taps(pro, f"x{i}")
                if i in (3, 5):
                    weights_lo(i // 2 + 2)
            measure_u(1)
            dve.wait_ge(w_out_in, 16)
            for k in range(CT):
                last = v.tensor_scalar(w_out[:, k, :], w_out[:, k, :], normw[:, k:k + 1], None, ALU.mult)
            last.then_inc(w_out_done, 1)
            body(Stage("body", 0))
            with dve.Fori(1, nb - 1) as i:
                body(Stage("body", i))
            body(Stage("last", nb - 1))

            def read(f, m, e):
                which, g = GU_ORDER[e]
                at = f * FT + m
                dve.wait_ge(gu_full, at * 8 + e + 1)
                if g == 2:
                    dve.wait_ge(part_done, at * 2 + 1 + (which == "u"))
                else:
                    dve.wait_ge(dve_read, at * 4 + e - 5)
                acc = (up_sum if which == "u" else gate_sum)[:, m % 2, :]
                ch = (FT if which == "u" else 0) + m
                v.scalar_tensor_tensor(acc, ps_gu[e][:, :], gs[:, g, ch:ch + 1], acc, ALU.mult, ALU.add)\
                    .then_inc(dve_read, 1)

            def hidden(f, first):
                for m in range(FT + 1):
                    if m < FT:
                        read(f, m, 4)
                        read(f, m, 5)
                    if m == 1 and not first:
                        normed(f - 1, TT - 1)
                    if m >= 1:
                        at = f * FT + m - 1
                        dve.wait_ge(dve_read, at * 4 + 4)
                        dve.wait_ge(sg_done, at + 1)
                        need(dve, hh_done, at - 1)
                        need(dve, hl_done, at - 1)
                        v.tensor_tensor(hf[:, (m - 1) % 2, :], up_sum[:, (m - 1) % 2, :], sg[:, (m - 1) % 2, :],
                                        ALU.mult).then_inc(hf_done, 1)
                    if m < FT:
                        read(f, m, 6)
                        read(f, m, 7)

            def mean_square2(f, tt):
                i = tt % 2
                dve.wait_ge(ss_done, f * TT + tt + 1)
                v.tensor_scalar(ms2[:, i:i + 1], ss2[:, i:i + 1], 1.0 / DM, 1e-6, ALU.mult, ALU.add).then_inc(ms_done, 1)

            def residual(f, tt):
                i = tt % 2
                ch = Chain(dve, o_chain, 20, f)
                ch.k = 5 * tt
                dve.wait_ge(ri_done, f * TT + tt + 1)
                ch.step(v.tensor_scalar(rk2[:, i:i + 1], ri2[:, i:i + 1], down_undo, None, ALU.mult))
                dve.wait_ge(xr_in[i], f * 32 + 16 * (tt // 2) + 16)
                ch.step(v.scalar_tensor_tensor(xr[:, i, :], ps_n[i][:, :], rk2[:, i:i + 1], xr[:, i, :],
                                               ALU.mult, ALU.add))
                ch.step(v.bn_stats(bn2[:, i, :], xr[:, i, :]), settled)
                ch.step(v.bn_aggr(mv2[:, i, :], bn2[:, i, :]))
                v.tensor_scalar(mv2[:, i, 1:2], mv2[:, i, 1:2], 1e-5, None, ALU.add).then_inc(o_chain, 1)

            def normed(f, tt):
                i = tt % 2
                dve.wait_ge(rs_done, f * TT + tt + 1)
                v.tensor_scalar(xr[:, i, :], xr[:, i, :], mv2[:, i, 0:1], rs2[:, i:i + 1],
                                ALU.subtract, ALU.mult).then_inc(o_done, 1)

            def norms(f, last):
                for tt in range(TT):
                    if tt == 1 and not last:
                        turn(f + 1, (2, 3))
                    mean_square2(f, tt)
                    residual(f, tt)
                    if tt < TT - 1:
                        normed(f, tt)

            def ffn(f, first, last):
                hidden(f, first)
                if not last:
                    turn(f + 1, (0, 1))
                norms(f, last)

            ffn(0, True, False)
            with dve.Fori(1, nb - 1) as f:
                ffn(f, False, False)
            ffn(nb - 1, False, True)
            normed(nb - 1, TT - 1)

        @block.gpsimd
        def _(pool):
            g_ = nc.gpsimd

            def reduce_u(b):
                pool.wait_ge(u_max, b + 1)
                need(pool, u_scale, b * 5)
                settled(pool)
                g_.partition_all_reduce(umax_all[:, :], umax[:, :], P, RMAX).then_inc(u_all, 1)

            def to_end(b, n):
                c, g = n // NG, n % NG
                pool.wait_ge(e_done, b * SLOTS + n + 1)
                pool.wait_ge(t_free, b * 32 + c * 4 + 3)
                if g == 0:
                    need(pool, s_full, b * 14 + 2 * c)
                g_.tensor_tensor(xend[:, g:NP:NG, :], xpad[:, c % 2, g:NP:NG, :],
                                 decay[:, g, :, CH - 1:CH].broadcast_to([P, CT, 2 * HD]), ALU.mult).then_inc(xe_done, 1)

            def decay_state(b, c):
                pool.wait_ge(s_add, b * 14 + 2 * c)
                pool.wait_ge(t_free, b * 32 + c * 4 + 2)
                g_.tensor_tensor(state_d[:, :].rearrange("p (q d) -> p q d", d=HD),
                                 state[:, :].rearrange("p (q d) -> p q d", d=HD),
                                 dec[:, c % 2, :, :].rearrange("p q h -> p (q h)").unsqueeze(2).broadcast_to([P, NH, HD]),
                                 ALU.mult).then_inc(sd_done, 1)

            def skip_term(b, c):
                pool.wait_ge(silu_done, (b + 1) * 3)
                need(pool, gate_done, b * NC + c - 1)
                g_.tensor_tensor(y[:, c % 2, :, :], xs[:, :, c * CH:(c + 1) * CH],
                                 dskip[:, :].unsqueeze(2).broadcast_to([P, CT, CH]), ALU.mult).then_inc(xd_done, 1)

            def gate(st, c):
                b, t = st.scan, slice(c * CH, (c + 1) * CH)
                pool.wait_ge(y_done, b * NC + c + 1)
                if c == 0:
                    for bk, count in st.before().last_z():
                        pool.wait_ge(in_free[bk], count)
                g_.tensor_tensor(zg[:, :, t], y[:, c % 2, :, :], zg[:, :, t], ALU.mult).then_inc(gate_done, 1)

            def sum_squares(b, c):
                t = slice(c * CH, (c + 1) * CH)
                ch = Chain(pool, sum_chain, 3 * NC, b)
                ch.k = 3 * c
                pool.wait_ge(sq_done, b * NC + c + 1)
                ch.step(g_.tensor_tensor(sq[:, 0:4, :], sq[:, 0:4, :], sq[:, 4:8, :], ALU.add))
                ch.step(g_.tensor_tensor(sq[:, 0:2, :], sq[:, 0:2, :], sq[:, 2:4, :], ALU.add))
                ch.step(g_.tensor_tensor(ssum[:, t], sq[:, 0, :], sq[:, 1, :], ALU.add))

            def root(st, tt):
                if tt == TT - 1:
                    pool.wait_ge(q3_free, st.scan + 1)
                else:
                    bk, _, count = st.bank(f"q{tt}")
                    pool.wait_ge(in_free[bk], count)
                g_.tensor_tensor(rinv[:, tt:tt + 1], msv[:, tt:tt + 1], half[:, :], ALU.pow).then_inc(rinv_done, 1)

            def ln_root(b, tt):
                pool.wait_ge(ln_chain, b * 12 + 3 * tt + 3)
                g_.tensor_tensor(rstd[:, tt % 2:tt % 2 + 1], mv[:, tt % 2, 1:2], half[:, :], ALU.pow).then_inc(rstd_done, 1)

            def body(st):
                b = st.scan
                skip_term(b, 0)
                for n in range(SLOTS):
                    c, g = n // NG, n % NG
                    if g == 0:
                        to_end(b, n)
                    if g < NG - 1:
                        to_end(b, n + 1)
                    if g == 1 and c > 0:
                        gate(st, c - 1)
                    if g == 1 and 1 <= c < NC - 1:
                        decay_state(b, c)
                    if g == 2 and c + 1 < NC:
                        skip_term(b, c + 1)
                    if g == 3 and c > 0:
                        sum_squares(b, c - 1)
                    for tt in range(TT):
                        if n > 0 and f"q{tt}" in st.at(n - 1):
                            root(st, tt)
                        if n > 0 and f"o{tt}" in st.at(n - 1):
                            ln_root(b, tt)
                gate(st, NC - 1)
                sum_squares(b, NC - 1)
                root(st, TT - 1)
                ln_root(b, TT - 1)
                if st.proj is not None:
                    reduce_u(b + 2)

            g_.memset(xpad[:, :, :, :], 0.0).then_inc(pro_pool, 1)
            reduce_u(0)
            pool.wait_ge(pro_dve, MAXES_READY)
            g_.partition_all_reduce(maxes_all[:, :], maxes[:, :], P, RMAX).then_inc(pro_pool, 1)
            reduce_u(1)
            body(Stage("body", 0))
            with pool.Fori(1, nb - 1) as i:
                body(Stage("body", i))
            body(Stage("last", nb - 1))

            def hidden(f, first):
                for m in range(FT + 2):
                    at = f * FT + m
                    if m < FT:
                        for i, (to, part) in enumerate(((gate_sum, gate_part), (up_sum, up_part))):
                            pool.wait_ge(act_read, at * 4 + 2 * i + 2)
                            g_.tensor_tensor(to[:, m % 2, :], to[:, m % 2, :], part[:, m % 2, :], ALU.add)\
                                .then_inc(part_done, 1)
                    if m == 0 and not first:
                        root_of_var(f - 1, TT - 1)
                    if m >= 2:
                        pool.wait_ge(hh_done, at - 1)
                        if m == 2:
                            need(pool, dn_full, f * TT)
                        g_.tensor_tensor(h_lo[:, m - 2, :], hf[:, (m - 2) % 2, :], h_hi[:, m - 2, :], ALU.subtract)\
                            .then_inc(hl_done, 1)

            def root_of_y(f, tt):
                i = tt % 2
                pool.wait_ge(ms_done, f * TT + tt + 1)
                g_.tensor_tensor(ri2[:, i:i + 1], ms2[:, i:i + 1], half[:, :], ALU.pow).then_inc(ri_done, 1)

            def root_of_var(f, tt):
                i = tt % 2
                pool.wait_ge(o_chain, f * 20 + 5 * tt + 5)
                g_.tensor_tensor(rs2[:, i:i + 1], mv2[:, i, 1:2], half[:, :], ALU.pow).then_inc(rs_done, 1)

            def ffn(f, first):
                hidden(f, first)
                for tt in range(TT):
                    root_of_y(f, tt)
                    if tt < TT - 1:
                        root_of_var(f, tt)

            ffn(0, True)
            with pool.Fori(1, nb - 1) as f:
                ffn(f, False)
            ffn(nb - 1, False)
            root_of_var(nb - 1, TT - 1)


def kernel(L0_attn_u, L0_attn_in_proj_w, L0_attn_conv_w, L0_attn_conv_b, L0_attn_dt_bias, L0_attn_A_log,
           L0_attn_D, L0_attn_norm_weight, L0_attn_out_proj_w, L0_ffn_gate_up_packed, L0_ffn_gate_up_scales,
           L0_ffn_down_packed, L0_ffn_down_scales):
    import concourse.bacc as bacc
    from concourse.bass_utils import run_bass_kernel_spmd

    arrays = lay_out(*(np.asarray(a) for a in (
        L0_attn_u, L0_attn_in_proj_w, L0_attn_conv_w, L0_attn_conv_b, L0_attn_dt_bias, L0_attn_A_log, L0_attn_D,
        L0_attn_norm_weight, L0_attn_out_proj_w, L0_ffn_gate_up_packed, L0_ffn_gate_up_scales, L0_ffn_down_packed,
        L0_ffn_down_scales)))
    nc = bacc.Bacc("TRN2", target_bir_lowering=False, num_devices=1, dynamic_dma_scratch_size=1024)
    args = [nc.dram_tensor(n, a.shape, mybir.dt.from_np(a.dtype), kind="ExternalInput").ap() for n, a in arrays.items()]
    args.append(nc.dram_tensor("out", [NB * L, DM], F32, kind="ExternalOutput").ap())
    build(nc, *args)
    result = run_bass_kernel_spmd(nc, [arrays], core_ids=[0])
    return result.results[0]["out"].reshape(NB, L, DM)


def lay_out(u, w_in, conv_w, conv_b, dt_bias, a_log, d, norm_w, w_out, gu, gu_s, dn, dn_s):
    c = np.ascontiguousarray

    def bf16_bits(a):
        return (c(a, np.float32).view(np.uint32) >> 16).astype(np.uint16)

    h2, tile, g = np.meshgrid(range(2), range(CT), range(NG), indexing="ij")
    heads = (8 * tile + 2 * g + h2).ravel()
    zs, xb, ds = w_in[:DI], w_in[DI:2 * DI + 2 * NS], w_in[2 * DI + 2 * NS:]
    w_rows = np.concatenate([ds[heads], xb[DI:], xb[:DI], zs])
    order = np.concatenate([np.arange(DI, DI + 2 * NS), np.arange(DI)])
    tokens = u.reshape(NB * L, DM)
    sel = np.zeros((2, NH, CT, P), np.float32)
    for q, h in enumerate(heads):
        sel[:, q, h // 8, (h % 8) * HD:(h % 8 + 1) * HD] = 1
    rhs = np.zeros((24 + CH, NP, CH), np.float32)
    for r in range(3):
        for k in range(CT):
            rhs[8 * r + k, NG * k:NG * k + NG] = 1
    rhs[24:] = np.where(np.arange(CH)[None, None, :] < np.arange(CH)[:, None, None], NEG, 0)
    lhs = np.zeros((94, NG, 2, CH), np.float32)
    dec = np.zeros((6, 2, P), np.float32)
    for r in range(3):
        for h in range(2):
            lhs[2 * r + h, :, h] = 1
            dec[2 * r + h, h] = 1
    lhs[30:] = np.eye(CH)[:, None, None, :]
    mask = np.broadcast_to(np.arange(LH) % CH != 0, (P, LH))
    p = np.arange(P)
    return {
        "u_t": c(np.concatenate([tokens.T, np.zeros((DM, L), u.dtype)], 1)),
        "u_tok": c(tokens),
        "w_in_t": c(w_rows.T),
        "conv_w": c(conv_w[order].reshape(2 + CT, P, TAPS).transpose(1, 0, 2)),
        "conv_b": c(conv_b[order].reshape(2 + CT, P).T),
        "dt_bias": c(dt_bias[heads][:, None]),
        "a_log": c(np.tile(a_log[heads], 2)[:, None]),
        "d_skip": c(np.repeat(d, HD).reshape(CT, P).T),
        "norm_w": c(norm_w.reshape(CT, P).T),
        "w_out_t": c(w_out.T),
        "gu_words": c(np.repeat(gu.T, 8, axis=0)),
        "gu_scales": c(gu_s.reshape(KT, 2 * FT, P).transpose(2, 0, 1)),
        "dn_words": c(np.repeat(dn.T, 8, axis=0).reshape(FT, P, DM).transpose(1, 0, 2)),
        "dn_scales": c(np.broadcast_to(dn_s, (P, FT, DM))),
        "all_scales": c(np.concatenate([gu_s.reshape(P, -1), dn_s.reshape(P, -1)], 1)),
        "c_sel": bf16_bits(sel.reshape(P, CT, P)),
        "c_rhs": bf16_bits(rhs),
        "c_lhs": bf16_bits(lhs.reshape(94, NG, P)),
        "c_dec": bf16_bits(dec),
        "c_ident": np.eye(P, dtype=np.float32),
        "c_mask": bf16_bits(mask),
        "c_shift": c(4 * (p % 8)[:, None]).astype(np.int32),
    }
```
